# Optimizing a Trainium2 kernel written in Bass

```python
import numpy as np
import jax
import jax.numpy as jnp

def _softmax(x, axis=-1):
    return jax.nn.softmax(x, axis=axis)

def _gelu(x):
    return jax.nn.gelu(x, approximate=True)

def _silu(x):
    return jax.nn.silu(x)

def _sigmoid(x):
    return jax.nn.sigmoid(x)

def _layernorm(x, axis=-1, eps=1e-05):
    m = jnp.mean(x, axis=axis, keepdims=True)
    v = jnp.var(x, axis=axis, keepdims=True)
    return (x - m) / jnp.sqrt(v + eps)

def _scatter_add(tgt, idx, src, axis=0):
    return tgt.at[idx].add(src)

def _segment_sum(src, seg, n):
    return jax.ops.segment_sum(src, seg, n)
kernel_name = 'mk_adaln_attn_ffn_d4_seqx_r8_03987c'

def setup_inputs(seed: int=0):
    np.random.seed(seed)
    _w = jnp.asarray

    def _rec_inputs():
        import jax
        import jax.numpy as jnp
        _rk = jax.random.key(seed)
        x = -0.0003929 + 0.9999 * jax.random.normal(jax.random.fold_in(_rk, 1), (32, 128, 128), jnp.float32)
        _lenS = 128 - jax.random.randint(jax.random.fold_in(_rk, 7), (32,), 0, max(1, 128 // 4) + 1, jnp.int32)
        _lenS2 = 128 - jax.random.randint(jax.random.fold_in(_rk, 8), (32,), 0, max(1, 128 // 4) + 1, jnp.int32)
        fside_Bx1x1024x16_0 = 0.00222621 + 0.99962 * jax.random.normal(jax.random.fold_in(_rk, 11), (32, 1, 128, 16), jnp.float32)
        cond_1024 = -0.00745576 + 0.997402 * jax.random.normal(jax.random.fold_in(_rk, 12), (32, 128), jnp.float32)
        return (x, fside_Bx1x1024x16_0, cond_1024)
    x, fside_Bx1x1024x16_0, cond_1024 = _rec_inputs()

    def _L0_cond_setup():
        import jax, jax.numpy as jnp
        import numpy as np
        B, F_, IN, OUT, R = (32, 64, 128, 128, 16)
        key = jax.random.key(seed)
        ks = jax.random.split(key, 6)
        x = jax.random.normal(ks[0], (B, F_, IN), dtype=jnp.float32)
        u = jax.random.normal(ks[1], (B, 1, OUT, R), dtype=jnp.float32)
        v = jax.random.normal(ks[2], (B, 1, IN, R), dtype=jnp.float32)
        b = jax.random.normal(ks[3], (B, 1, OUT), dtype=jnp.float32)
        lim = 1.0 / np.sqrt(IN)
        W = jax.random.uniform(ks[4], (OUT, IN), minval=-lim, maxval=lim, dtype=jnp.float32)
        fc_bias = jax.random.uniform(ks[5], (OUT,), minval=-lim, maxval=lim, dtype=jnp.float32)
        return {'x': x, 'u': u, 'v': v, 'b': b, 'W': W, 'fc_bias': fc_bias}
    _L0_cond_all = _L0_cond_setup()
    _L0_cond_in = {k: v for k, v in _L0_cond_all.items() if k in ('W', 'fc_bias')}
    del _L0_cond_all

    def _L0_attn_setup():
        import jax, jax.numpy as jnp
        import numpy as np
        D_MODEL = 128
        N_HEADS = 16
        SEQ = 64
        key = jax.random.key(seed)
        ks = jax.random.split(key, 12)
        B = 16
        x = jax.random.normal(ks[0], (B, SEQ, D_MODEL), dtype=jnp.float32)
        c = jax.random.normal(ks[1], (B, SEQ, 8), dtype=jnp.float32)
        s = 1.0 / np.sqrt(D_MODEL)
        Wq = jax.random.normal(ks[2], (D_MODEL, D_MODEL), dtype=jnp.float32) * s
        bq = jnp.zeros((D_MODEL,), dtype=jnp.float32)
        Wk = jax.random.normal(ks[3], (D_MODEL, D_MODEL), dtype=jnp.float32) * s
        bk = jnp.zeros((D_MODEL,), dtype=jnp.float32)
        Wv = jax.random.normal(ks[4], (D_MODEL, D_MODEL), dtype=jnp.float32) * s
        bv = jnp.zeros((D_MODEL,), dtype=jnp.float32)
        Wo = jax.random.normal(ks[5], (D_MODEL, D_MODEL), dtype=jnp.float32) * s
        bo = jnp.zeros((D_MODEL,), dtype=jnp.float32)
        rel_table = jax.random.normal(ks[6], (2 * SEQ - 1, N_HEADS), dtype=jnp.float32) * 0.02
        return {'x': x, 'c': c, 'Wq': Wq, 'bq': bq, 'Wk': Wk, 'bk': bk, 'Wv': Wv, 'bv': bv, 'Wo': Wo, 'bo': bo, 'rel_table': rel_table}
    _L0_attn_all = _L0_attn_setup()
    _L0_attn_in = {k: v for k, v in _L0_attn_all.items() if k in ('c', 'Wq', 'bq', 'Wk', 'bk', 'Wv', 'bv', 'Wo', 'bo', 'rel_table')}
    del _L0_attn_all

    def _L0_cond2_setup():
        import jax, jax.numpy as jnp
        import numpy as np
        LATENT = 128
        key = jax.random.key(seed)
        k1, k2, k3, k4 = jax.random.split(key, 4)
        B, T, D = (64, 64, LATENT)
        h_t = jax.random.normal(k1, (B, D), dtype=jnp.float32)
        z = jax.random.normal(k2, (B, T, D), dtype=jnp.float32)
        bound = 1.0 / np.sqrt(2 * D)
        W = jax.random.uniform(k3, (D, 2 * D), minval=-bound, maxval=bound, dtype=jnp.float32)
        b = jax.random.uniform(k4, (D,), minval=-bound, maxval=bound, dtype=jnp.float32)
        alpha = jnp.full((D,), 0.1, dtype=jnp.float32)
        return {'h_t': h_t, 'z': z, 'W': W, 'b': b, 'alpha': alpha}
    _L0_cond2_all = _L0_cond2_setup()
    _L0_cond2_in = {k: v for k, v in _L0_cond2_all.items() if k in ('W', 'b', 'alpha')}
    del _L0_cond2_all

    def _L0_ffn_setup():
        import jax, jax.numpy as jnp
        import numpy as np
        B, T, D, E, H = (8, 256, 128, 8, 32)
        LN_EPS = 1e-05
        key = jax.random.key(seed)
        ks = jax.random.split(key, 4)
        return {'x': jax.random.normal(ks[0], (B, T, D), dtype=jnp.float32), 'Wg': jax.random.normal(ks[1], (E, D), dtype=jnp.float32) * 0.02, 'ln_scale': jnp.ones((E, D), dtype=jnp.float32), 'ln_bias': jnp.zeros((E, D), dtype=jnp.float32), 'W1': jax.random.normal(ks[2], (E, D, H), dtype=jnp.float32) * 0.02, 'b1': jnp.zeros((E, H), dtype=jnp.float32), 'W2': jax.random.normal(ks[3], (E, H, D), dtype=jnp.float32) * 0.02, 'b2': jnp.zeros((E, D), dtype=jnp.float32)}
    _L0_ffn_all = _L0_ffn_setup()
    _L0_ffn_in = {k: v for k, v in _L0_ffn_all.items() if k in ('Wg', 'ln_scale', 'ln_bias', 'W1', 'b1', 'W2', 'b2')}
    del _L0_ffn_all

    def _L1_cond_setup():
        import jax, jax.numpy as jnp
        import numpy as np
        D = 128
        H = 128
        key = jax.random.key(seed)
        k1, k2, k3, k4 = jax.random.split(key, 4)
        x = jax.random.normal(k1, (32, 64, D), dtype=jnp.float32)
        h0 = jax.random.normal(k2, (32, H), dtype=jnp.float32)
        Wx = jax.random.normal(k3, (D, 4 * H), dtype=jnp.float32) / jnp.sqrt(float(D))
        Wh = jax.random.normal(k4, (H, 4 * H), dtype=jnp.float32) / jnp.sqrt(float(H))
        b = jnp.zeros((4 * H,), dtype=jnp.float32)
        return {'x': x, 'h0': h0, 'Wx': Wx, 'Wh': Wh, 'b': b}
    _L1_cond_all = _L1_cond_setup()
    _L1_cond_in = {k: v for k, v in _L1_cond_all.items() if k in ('Wx', 'Wh', 'b')}
    del _L1_cond_all

    def _L1_attn_setup():
        import jax, jax.numpy as jnp
        import numpy as np
        import math
        DIM = 128
        H = 16
        D = 64
        M = 64
        B = 1
        N = 256

        def _orf_omega(key):
            blocks = []
            n_blocks = (M + D - 1) // D
            for i in range(n_blocks):
                G = jax.random.normal(jax.random.fold_in(key, i), (D, D), dtype=jnp.float32)
                Q, _ = jnp.linalg.qr(G)
                blocks.append(Q.T)
            return jnp.concatenate(blocks, axis=0)[:M]

        def _phi(x, omega):
            proj = jnp.einsum('bhnd,md->bhnm', x, omega)
            norm = 0.5 * jnp.sum(x * x, axis=-1, keepdims=True)
            return jnp.exp(proj - norm) / math.sqrt(M)

        def _heads(t):
            b, n, _ = t.shape
            return t.reshape(b, n, H, D).transpose(0, 2, 1, 3)
        key = jax.random.key(seed)
        ks = jax.random.split(key, 7)
        inner = H * D
        x = jax.random.normal(ks[0], (B, N, DIM), dtype=jnp.float32)
        omega = _orf_omega(ks[1])
        wq = jax.random.normal(ks[2], (inner, DIM), dtype=jnp.float32) * 0.02
        wk = jax.random.normal(ks[3], (inner, DIM), dtype=jnp.float32) * 0.02
        wv = jax.random.normal(ks[4], (inner, DIM), dtype=jnp.float32) * 0.02
        wo = jax.random.normal(ks[5], (DIM, inner), dtype=jnp.float32) * 0.02
        bo = jnp.zeros((DIM,), dtype=jnp.float32)
        return {'x': x, 'omega': omega, 'wq': wq, 'wk': wk, 'wv': wv, 'wo': wo, 'bo': bo}
    _L1_attn_all = _L1_attn_setup()
    _L1_attn_in = {k: v for k, v in _L1_attn_all.items() if k in ('omega', 'wq', 'wk', 'wv', 'wo', 'bo')}
    del _L1_attn_all

    def _L1_cond2_setup():
        import jax, jax.numpy as jnp
        import numpy as np
        import math
        D = 128
        H = 128
        key = jax.random.key(seed)
        k1, k2, k3, k4 = jax.random.split(key, 4)
        x = jax.random.normal(k1, (64, 64, D), dtype=jnp.float32)
        h0 = jax.random.normal(k2, (64, H), dtype=jnp.float32)
        Wx = jax.random.normal(k3, (D, 4 * H), dtype=jnp.float32) / math.sqrt(D)
        Wh = jax.random.normal(k4, (H, 4 * H), dtype=jnp.float32) / math.sqrt(H)
        b = jnp.zeros((4 * H,), dtype=jnp.float32)
        return {'x': x, 'h0': h0, 'Wx': Wx, 'Wh': Wh, 'b': b}
    _L1_cond2_all = _L1_cond2_setup()
    _L1_cond2_in = {k: v for k, v in _L1_cond2_all.items() if k in ('Wx', 'Wh', 'b')}
    del _L1_cond2_all

    def _L1_ffn_setup():
        import jax, jax.numpy as jnp
        import numpy as np
        IN_DIM = 128
        HIDDEN = 128
        OUT_DIM = 128
        NUM_EXPERTS = 16
        TOP_K = 2
        ROUTER_TEMP = 1.0
        LN_EPS = 1e-05

        def _layernorm(h, g, b):
            mu = jnp.mean(h, axis=-1, keepdims=True)
            var = jnp.mean(jnp.square(h - mu), axis=-1, keepdims=True)
            return (h - mu) * jax.lax.rsqrt(var + LN_EPS) * g + b
        key = jax.random.key(seed)
        ks = jax.random.split(key, 8)
        s_in = 1.0 / np.sqrt(IN_DIM)
        s_h = 1.0 / np.sqrt(HIDDEN)
        x = jax.random.normal(ks[0], (4, 256, IN_DIM), dtype=jnp.float32)
        Wr = jax.random.uniform(ks[1], (IN_DIM, NUM_EXPERTS), jnp.float32, -s_in, s_in)
        br = jax.random.uniform(ks[2], (NUM_EXPERTS,), jnp.float32, -s_in, s_in)
        W1 = jax.random.uniform(ks[3], (NUM_EXPERTS, IN_DIM, HIDDEN), jnp.float32, -s_in, s_in)
        b1 = jax.random.uniform(ks[4], (NUM_EXPERTS, HIDDEN), jnp.float32, -s_in, s_in)
        g1 = jnp.ones((NUM_EXPERTS, HIDDEN), jnp.float32)
        be1 = jnp.zeros((NUM_EXPERTS, HIDDEN), jnp.float32)
        W2 = jax.random.uniform(ks[5], (NUM_EXPERTS, HIDDEN, OUT_DIM), jnp.float32, -s_h, s_h)
        b2 = jax.random.uniform(ks[6], (NUM_EXPERTS, OUT_DIM), jnp.float32, -s_h, s_h)
        return {'x': x, 'Wr': Wr, 'br': br, 'W1': W1, 'b1': b1, 'g1': g1, 'be1': be1, 'W2': W2, 'b2': b2}
    _L1_ffn_all = _L1_ffn_setup()
    _L1_ffn_in = {k: v for k, v in _L1_ffn_all.items() if k in ('Wr', 'br', 'W1', 'b1', 'g1', 'be1', 'W2', 'b2')}
    del _L1_ffn_all

    def _L2_cond_setup():
        import jax, jax.numpy as jnp
        import numpy as np
        import math
        D = 128
        H = 128
        key = jax.random.key(seed)
        k1, k2, k3, k4 = jax.random.split(key, 4)
        x = jax.random.normal(k1, (64, 64, D), dtype=jnp.float32)
        h0 = jax.random.normal(k2, (64, H), dtype=jnp.float32)
        Wx = jax.random.normal(k3, (D, 4 * H), dtype=jnp.float32) / math.sqrt(D)
        Wh = jax.random.normal(k4, (H, 4 * H), dtype=jnp.float32) / math.sqrt(H)
        b = jnp.zeros((4 * H,), dtype=jnp.float32)
        return {'x': x, 'h0': h0, 'Wx': Wx, 'Wh': Wh, 'b': b}
    _L2_cond_all = _L2_cond_setup()
    _L2_cond_in = {k: v for k, v in _L2_cond_all.items() if k in ('Wx', 'Wh', 'b')}
    del _L2_cond_all

    def _L2_attn_setup():
        import jax, jax.numpy as jnp
        import numpy as np
        D_MODEL = 128
        N_HEADS = 16
        HEAD_DIM = D_MODEL // N_HEADS
        KV_LATENT = 32
        LN_EPS = 1e-05

        def apply_rope(x):
            b, h, t, d = x.shape
            half = d // 2
            pos = jnp.arange(t, dtype=x.dtype)[:, None]
            inv_freq = 1.0 / 10000.0 ** (jnp.arange(half, dtype=x.dtype) / half)
            angles = pos * inv_freq[None, :]
            sin = jnp.sin(angles)[None, None]
            cos = jnp.cos(angles)[None, None]
            x1, x2 = (x[..., :half], x[..., half:])
            return jnp.concatenate([x1 * cos - x2 * sin, x1 * sin + x2 * cos], axis=-1)
        key = jax.random.key(seed)
        ks = jax.random.split(key, 6)
        d, L = (D_MODEL, KV_LATENT)
        s = 1.0 / np.sqrt(d)
        sl = 1.0 / np.sqrt(L)
        return {'x': jax.random.normal(ks[0], (2, 256, d), dtype=jnp.float32), 'W_q': jax.random.uniform(ks[1], (d, d), jnp.float32, -s, s), 'W_dkv': jax.random.uniform(ks[2], (d, L), jnp.float32, -s, s), 'W_uk': jax.random.uniform(ks[3], (L, d), jnp.float32, -sl, sl), 'W_uv': jax.random.uniform(ks[4], (L, d), jnp.float32, -sl, sl), 'W_o': jax.random.uniform(ks[5], (d, d), jnp.float32, -s, s), 'ln_gamma': jnp.ones((L,), jnp.float32), 'ln_beta': jnp.zeros((L,), jnp.float32)}
    _L2_attn_all = _L2_attn_setup()
    _L2_attn_in = {k: v for k, v in _L2_attn_all.items() if k in ('W_q', 'W_dkv', 'W_uk', 'W_uv', 'W_o', 'ln_gamma', 'ln_beta')}
    del _L2_attn_all

    def _L2_cond2_setup():
        import jax, jax.numpy as jnp
        import numpy as np
        B, T, D_IN, V_IN, E = (64, 128, 128, 128, 128)
        key = jax.random.key(seed)
        ks = jax.random.split(key, 16)
        s = 0.01
        return {'video': jax.random.normal(ks[0], (B, V_IN), jnp.float32), 'seq': jax.random.normal(ks[1], (B, T, D_IN), jnp.float32), 'W_z': jax.random.normal(ks[2], (D_IN, E), jnp.float32) * s, 'U_z': jax.random.normal(ks[3], (E, E), jnp.float32) * s, 'C_z': jax.random.normal(ks[4], (V_IN, E), jnp.float32) * s, 'b_z': jnp.zeros((E,), jnp.float32), 'W_r': jax.random.normal(ks[5], (D_IN, E), jnp.float32) * s, 'U_r': jax.random.normal(ks[6], (E, E), jnp.float32) * s, 'C_r': jax.random.normal(ks[7], (V_IN, E), jnp.float32) * s, 'b_r': jnp.zeros((E,), jnp.float32), 'W': jax.random.normal(ks[8], (D_IN, E), jnp.float32) * s, 'U': jax.random.normal(ks[9], (E, E), jnp.float32) * s, 'C': jax.random.normal(ks[10], (V_IN, E), jnp.float32) * s, 'b': jnp.zeros((E,), jnp.float32)}
    _L2_cond2_all = _L2_cond2_setup()
    _L2_cond2_in = {k: v for k, v in _L2_cond2_all.items() if k in ('W_z', 'U_z', 'C_z', 'b_z', 'W_r', 'U_r', 'C_r', 'b_r', 'W', 'U', 'C', 'b')}
    del _L2_cond2_all

    def _L2_ffn_setup():
        import jax, jax.numpy as jnp
        import numpy as np
        NUM_NOD = 6
        MAX_PREV = 5
        NUM_EDGE = 20
        D = 128
        H = 8
        LN_EPS = 1e-06

        def _layernorm(x, g, b):
            mu = jnp.mean(x, axis=-1, keepdims=True)
            var = jnp.mean(jnp.square(x - mu), axis=-1, keepdims=True)
            return (x - mu) * jax.lax.rsqrt(var + LN_EPS) * g + b

        def _mha(q, k, v, wq, wk, wv, wo):
            B, S, d = q.shape
            dh = d // H
            qh = (q @ wq).reshape(B, S, H, dh)
            kh = (k @ wk).reshape(B, S, H, dh)
            vh = (v @ wv).reshape(B, S, H, dh)
            scores = jnp.einsum('bqhd,bkhd->bhqk', qh, kh) / jnp.sqrt(jnp.asarray(dh, q.dtype))
            attn = jax.nn.softmax(scores, axis=-1)
            ctx = jnp.einsum('bhqk,bkhd->bqhd', attn, vh).reshape(B, S, d)
            return ctx @ wo
        key = jax.random.key(seed)
        ks = jax.random.split(key, 12)
        B, S = (8, 128)
        scale = 1.0 / np.sqrt(D)
        return {'inputs': jax.random.normal(ks[0], (B, S, D), jnp.float32), 'ew': jax.random.uniform(ks[1], (NUM_NOD, 3), jnp.float32), 'act_w': jax.random.uniform(ks[2], (NUM_NOD,), jnp.float32), 'We': jax.random.normal(ks[3], (NUM_EDGE, D, D), jnp.float32) * scale, 'be': jnp.zeros((NUM_EDGE, D), jnp.float32), 'Wq': jax.random.normal(ks[4], (NUM_NOD, D, D), jnp.float32) * scale, 'Wk': jax.random.normal(ks[5], (NUM_NOD, D, D), jnp.float32) * scale, 'Wv': jax.random.normal(ks[6], (NUM_NOD, D, D), jnp.float32) * scale, 'Wo': jax.random.normal(ks[7], (NUM_NOD, D, D), jnp.float32) * scale, 'ln_g': jnp.ones((D,), jnp.float32), 'ln_b': jnp.zeros((D,), jnp.float32)}
    _L2_ffn_all = _L2_ffn_setup()
    _L2_ffn_in = {k: v for k, v in _L2_ffn_all.items() if k in ('ew', 'act_w', 'We', 'be', 'Wq', 'Wk', 'Wv', 'Wo', 'ln_g', 'ln_b')}
    del _L2_ffn_all

    def _L3_cond_setup():
        import jax, jax.numpy as jnp
        import numpy as np
        IN_FEATURES = 128
        OUT_FEATURES = 128
        BATCH = 32
        SEQ = 128
        EPS = 1e-08
        key = jax.random.key(seed)
        k1, k2, k3 = jax.random.split(key, 3)
        Efou = jax.random.normal(k1, (BATCH, SEQ, IN_FEATURES), dtype=jnp.float32)
        y = jax.random.normal(k2, (BATCH, IN_FEATURES), dtype=jnp.float32)
        weight = jax.random.normal(k3, (IN_FEATURES, OUT_FEATURES), dtype=jnp.float32)
        return {'Efou': Efou, 'y': y, 'weight': weight}
    _L3_cond_all = _L3_cond_setup()
    _L3_cond_in = {k: v for k, v in _L3_cond_all.items() if k in ('weight',)}
    del _L3_cond_all

    def _L3_attn_setup():
        import jax, jax.numpy as jnp
        import numpy as np
        D_MODEL = 128
        NUM_HEADS = 16
        HEAD_DIM = D_MODEL // NUM_HEADS
        WINDOW = 128
        SCALE = HEAD_DIM ** (-0.5)
        key = jax.random.key(seed)
        ks = jax.random.split(key, 5)
        B, S = (2, 256)
        x = jax.random.normal(ks[0], (B, S, D_MODEL), dtype=jnp.float32)
        init = lambda k: jax.random.normal(k, (D_MODEL, D_MODEL), dtype=jnp.float32) * D_MODEL ** (-0.5)
        return {'x': x, 'Wq': init(ks[1]), 'Wk': init(ks[2]), 'Wv': init(ks[3]), 'Wo': init(ks[4])}
    _L3_attn_all = _L3_attn_setup()
    _L3_attn_in = {k: v for k, v in _L3_attn_all.items() if k in ('Wq', 'Wk', 'Wv', 'Wo')}
    del _L3_attn_all

    def _L3_cond2_setup():
        import jax, jax.numpy as jnp
        import numpy as np
        D, HS, HE, E, K = (128, 256, 128, 8, 2)
        B, T = (4, 128)
        N_SHARED = 1
        key = jax.random.key(seed)
        ks = jax.random.split(key, 9)
        g = lambda k, shape, s: jax.random.normal(k, shape, jnp.float32) * s
        return {'x': g(ks[0], (B, T, D), 1.0), 't_emb': g(ks[1], (B, D), 1.0), 'router_W': g(ks[2], (2 * D, E), 0.01), 'router_bias': jnp.zeros((E,), jnp.float32), 'w1': g(ks[3], (D, HS), 0.02), 'w3': g(ks[4], (D, HS), 0.02), 'w2': g(ks[5], (HS, D), 0.02), 'W1e': g(ks[6], (E, D, HE), 0.02), 'W2e': g(ks[7], (E, HE, D), 0.02)}
    _L3_cond2_all = _L3_cond2_setup()
    _L3_cond2_in = {k: v for k, v in _L3_cond2_all.items() if k in ('router_W', 'router_bias', 'w1', 'w3', 'w2', 'W1e', 'W2e')}
    del _L3_cond2_all

    def _L3_ffn_setup():
        import jax, jax.numpy as jnp
        import numpy as np
        EPS = 1e-12

        def _l2norm(v):
            n = jnp.sqrt(jnp.sum(v * v, axis=-1, keepdims=True))
            return v / jnp.maximum(n, EPS)
        key = jax.random.key(seed)
        ks = jax.random.split(key, 6)
        B, S, D, F, E = (2, 256, 128, 512, 8)
        std = 0.02
        return {'x': jax.random.normal(ks[0], (B, S, D), jnp.float32), 'Wp': jax.random.normal(ks[1], (D, D), jnp.float32) * (1.0 / np.sqrt(D)), 'sim_matrix': jax.random.normal(ks[2], (E, D), jnp.float32) * std, 'temperature': jnp.asarray(1.0, jnp.float32), 'W1': jax.random.normal(ks[3], (E, D, F), jnp.float32) * (1.0 / np.sqrt(D)), 'b1': jnp.zeros((E, F), jnp.float32), 'W2': jax.random.normal(ks[4], (E, F, D), jnp.float32) * (1.0 / np.sqrt(F)), 'b2': jnp.zeros((E, D), jnp.float32)}
    _L3_ffn_all = _L3_ffn_setup()
    _L3_ffn_in = {k: v for k, v in _L3_ffn_all.items() if k in ('Wp', 'sim_matrix', 'temperature', 'W1', 'b1', 'W2', 'b2')}
    del _L3_ffn_all
    return {'x': x, 'fside_Bx1x1024x16_0': fside_Bx1x1024x16_0, 'cond_1024': cond_1024, 'L0_cond_W': _L0_cond_in['W'], 'L0_cond_fc_bias': _L0_cond_in['fc_bias'], 'L0_attn_c': _L0_attn_in['c'], 'L0_attn_Wq': _L0_attn_in['Wq'], 'L0_attn_bq': _L0_attn_in['bq'], 'L0_attn_Wk': _L0_attn_in['Wk'], 'L0_attn_bk': _L0_attn_in['bk'], 'L0_attn_Wv': _L0_attn_in['Wv'], 'L0_attn_bv': _L0_attn_in['bv'], 'L0_attn_Wo': _L0_attn_in['Wo'], 'L0_attn_bo': _L0_attn_in['bo'], 'L0_attn_rel_table': _L0_attn_in['rel_table'], 'L0_cond2_W': _L0_cond2_in['W'], 'L0_cond2_b': _L0_cond2_in['b'], 'L0_cond2_alpha': _L0_cond2_in['alpha'], 'L0_ffn_Wg': _L0_ffn_in['Wg'], 'L0_ffn_ln_scale': _L0_ffn_in['ln_scale'], 'L0_ffn_ln_bias': _L0_ffn_in['ln_bias'], 'L0_ffn_W1': _L0_ffn_in['W1'], 'L0_ffn_b1': _L0_ffn_in['b1'], 'L0_ffn_W2': _L0_ffn_in['W2'], 'L0_ffn_b2': _L0_ffn_in['b2'], 'L1_cond_Wx': _L1_cond_in['Wx'], 'L1_cond_Wh': _L1_cond_in['Wh'], 'L1_cond_b': _L1_cond_in['b'], 'L1_attn_omega': _L1_attn_in['omega'], 'L1_attn_wq': _L1_attn_in['wq'], 'L1_attn_wk': _L1_attn_in['wk'], 'L1_attn_wv': _L1_attn_in['wv'], 'L1_attn_wo': _L1_attn_in['wo'], 'L1_attn_bo': _L1_attn_in['bo'], 'L1_cond2_Wx': _L1_cond2_in['Wx'], 'L1_cond2_Wh': _L1_cond2_in['Wh'], 'L1_cond2_b': _L1_cond2_in['b'], 'L1_ffn_Wr': _L1_ffn_in['Wr'], 'L1_ffn_br': _L1_ffn_in['br'], 'L1_ffn_W1': _L1_ffn_in['W1'], 'L1_ffn_b1': _L1_ffn_in['b1'], 'L1_ffn_g1': _L1_ffn_in['g1'], 'L1_ffn_be1': _L1_ffn_in['be1'], 'L1_ffn_W2': _L1_ffn_in['W2'], 'L1_ffn_b2': _L1_ffn_in['b2'], 'L2_cond_Wx': _L2_cond_in['Wx'], 'L2_cond_Wh': _L2_cond_in['Wh'], 'L2_cond_b': _L2_cond_in['b'], 'L2_attn_W_q': _L2_attn_in['W_q'], 'L2_attn_W_dkv': _L2_attn_in['W_dkv'], 'L2_attn_W_uk': _L2_attn_in['W_uk'], 'L2_attn_W_uv': _L2_attn_in['W_uv'], 'L2_attn_W_o': _L2_attn_in['W_o'], 'L2_attn_ln_gamma': _L2_attn_in['ln_gamma'], 'L2_attn_ln_beta': _L2_attn_in['ln_beta'], 'L2_cond2_W_z': _L2_cond2_in['W_z'], 'L2_cond2_U_z': _L2_cond2_in['U_z'], 'L2_cond2_C_z': _L2_cond2_in['C_z'], 'L2_cond2_b_z': _L2_cond2_in['b_z'], 'L2_cond2_W_r': _L2_cond2_in['W_r'], 'L2_cond2_U_r': _L2_cond2_in['U_r'], 'L2_cond2_C_r': _L2_cond2_in['C_r'], 'L2_cond2_b_r': _L2_cond2_in['b_r'], 'L2_cond2_W': _L2_cond2_in['W'], 'L2_cond2_U': _L2_cond2_in['U'], 'L2_cond2_C': _L2_cond2_in['C'], 'L2_cond2_b': _L2_cond2_in['b'], 'L2_ffn_ew': _L2_ffn_in['ew'], 'L2_ffn_act_w': _L2_ffn_in['act_w'], 'L2_ffn_We': _L2_ffn_in['We'], 'L2_ffn_be': _L2_ffn_in['be'], 'L2_ffn_Wq': _L2_ffn_in['Wq'], 'L2_ffn_Wk': _L2_ffn_in['Wk'], 'L2_ffn_Wv': _L2_ffn_in['Wv'], 'L2_ffn_Wo': _L2_ffn_in['Wo'], 'L2_ffn_ln_g': _L2_ffn_in['ln_g'], 'L2_ffn_ln_b': _L2_ffn_in['ln_b'], 'L3_cond_weight': _L3_cond_in['weight'], 'L3_attn_Wq': _L3_attn_in['Wq'], 'L3_attn_Wk': _L3_attn_in['Wk'], 'L3_attn_Wv': _L3_attn_in['Wv'], 'L3_attn_Wo': _L3_attn_in['Wo'], 'L3_cond2_router_W': _L3_cond2_in['router_W'], 'L3_cond2_router_bias': _L3_cond2_in['router_bias'], 'L3_cond2_w1': _L3_cond2_in['w1'], 'L3_cond2_w3': _L3_cond2_in['w3'], 'L3_cond2_w2': _L3_cond2_in['w2'], 'L3_cond2_W1e': _L3_cond2_in['W1e'], 'L3_cond2_W2e': _L3_cond2_in['W2e'], 'L3_ffn_Wp': _L3_ffn_in['Wp'], 'L3_ffn_sim_matrix': _L3_ffn_in['sim_matrix'], 'L3_ffn_temperature': _L3_ffn_in['temperature'], 'L3_ffn_W1': _L3_ffn_in['W1'], 'L3_ffn_b1': _L3_ffn_in['b1'], 'L3_ffn_W2': _L3_ffn_in['W2'], 'L3_ffn_b2': _L3_ffn_in['b2']}

def reference(x, fside_Bx1x1024x16_0, cond_1024, L0_cond_W, L0_cond_fc_bias, L0_attn_c, L0_attn_Wq, L0_attn_bq, L0_attn_Wk, L0_attn_bk, L0_attn_Wv, L0_attn_bv, L0_attn_Wo, L0_attn_bo, L0_attn_rel_table, L0_cond2_W, L0_cond2_b, L0_cond2_alpha, L0_ffn_Wg, L0_ffn_ln_scale, L0_ffn_ln_bias, L0_ffn_W1, L0_ffn_b1, L0_ffn_W2, L0_ffn_b2, L1_cond_Wx, L1_cond_Wh, L1_cond_b, L1_attn_omega, L1_attn_wq, L1_attn_wk, L1_attn_wv, L1_attn_wo, L1_attn_bo, L1_cond2_Wx, L1_cond2_Wh, L1_cond2_b, L1_ffn_Wr, L1_ffn_br, L1_ffn_W1, L1_ffn_b1, L1_ffn_g1, L1_ffn_be1, L1_ffn_W2, L1_ffn_b2, L2_cond_Wx, L2_cond_Wh, L2_cond_b, L2_attn_W_q, L2_attn_W_dkv, L2_attn_W_uk, L2_attn_W_uv, L2_attn_W_o, L2_attn_ln_gamma, L2_attn_ln_beta, L2_cond2_W_z, L2_cond2_U_z, L2_cond2_C_z, L2_cond2_b_z, L2_cond2_W_r, L2_cond2_U_r, L2_cond2_C_r, L2_cond2_b_r, L2_cond2_W, L2_cond2_U, L2_cond2_C, L2_cond2_b, L2_ffn_ew, L2_ffn_act_w, L2_ffn_We, L2_ffn_be, L2_ffn_Wq, L2_ffn_Wk, L2_ffn_Wv, L2_ffn_Wo, L2_ffn_ln_g, L2_ffn_ln_b, L3_cond_weight, L3_attn_Wq, L3_attn_Wk, L3_attn_Wv, L3_attn_Wo, L3_cond2_router_W, L3_cond2_router_bias, L3_cond2_w1, L3_cond2_w3, L3_cond2_w2, L3_cond2_W1e, L3_cond2_W2e, L3_ffn_Wp, L3_ffn_sim_matrix, L3_ffn_temperature, L3_ffn_W1, L3_ffn_b1, L3_ffn_W2, L3_ffn_b2):
    import jax
    import jax.numpy as jnp

    def _L0_cond_ref(x, u, v, b, W, fc_bias):
        import jax, jax.numpy as jnp
        import numpy as np
        B, F_, IN, OUT, R = (32, 64, 128, 128, 16)
        inch = x.shape[-1]
        r = v.shape[-1]
        z1 = jnp.einsum('bfi,bir->bfr', x, v[:, 0]) / inch
        z = jnp.einsum('bfr,bor->bfo', z1, u[:, 0]) / r
        y = jnp.einsum('bfi,oi->bfo', x, W) + fc_bias + z + b
        return jax.nn.gelu(y, approximate=False)

    def _L0_attn_ref(x, c, Wq, bq, Wk, bk, Wv, bv, Wo, bo, rel_table):
        import jax, jax.numpy as jnp
        import numpy as np
        D_MODEL = 128
        N_HEADS = 16
        SEQ = 64
        B, S, D = x.shape
        H = N_HEADS
        dk = D // H
        scale = 1.0 / np.sqrt(dk)
        q = (x @ Wq + bq).reshape(B, S, H, dk)
        k = (x @ Wk + bk).reshape(B, S, H, dk)
        v = (x @ Wv + bv).reshape(B, S, H, dk)
        scores = jnp.einsum('bihd,bjhd->bhij', q, k) * scale
        rel_index = jnp.arange(S)[:, None] + jnp.arange(S - 1, -1, -1)[None, :]
        bias = rel_table[rel_index]
        scores = scores + jnp.transpose(bias, (2, 0, 1))[None]
        probs = jax.nn.softmax(scores, axis=-1)
        out = jnp.einsum('bhij,bjhd->bihd', probs, v).reshape(B, S, D)
        return out @ Wo + bo

    def _L0_cond2_ref(h_t, z, W, b, alpha):
        import jax, jax.numpy as jnp
        import numpy as np
        LATENT = 128
        D = h_t.shape[-1]
        Wh = W[:, :D]
        Wz = W[:, D:]
        leak = 1.0 - alpha

        def step(h, z_t):
            gate = jax.nn.sigmoid(h @ Wh.T + z_t @ Wz.T + b)
            h_new = jnp.tanh(h * leak + gate * z_t)
            return (h_new, h_new)
        _, hs = jax.lax.scan(step, h_t, jnp.swapaxes(z, 0, 1))
        return jnp.swapaxes(hs, 0, 1)

    def _L0_ffn_ref(x, Wg, ln_scale, ln_bias, W1, b1, W2, b2):
        import jax, jax.numpy as jnp
        import numpy as np
        B, T, D, E, H = (8, 256, 128, 8, 32)
        LN_EPS = 1e-05
        Bs, Ts, Ds = x.shape
        xt = x.reshape(Bs * Ts, Ds)
        logits = xt @ Wg.T
        top1 = jnp.argmax(logits, axis=-1)
        mu = jnp.mean(xt, axis=-1, keepdims=True)
        var = jnp.mean(jnp.square(xt - mu), axis=-1, keepdims=True)
        xhat = (xt - mu) * jax.lax.rsqrt(var + LN_EPS)
        n_experts = Wg.shape[0]

        def body(y, p):
            s_e, b_e, w1, bb1, w2, bb2, eid = p
            h = jax.nn.gelu((xhat * s_e + b_e) @ w1 + bb1, approximate=False)
            out = h @ w2 + bb2
            mask = (top1 == eid)[:, None].astype(out.dtype)
            return (y + mask * out, None)
        y0 = jnp.zeros_like(xt)
        y, _ = jax.lax.scan(body, y0, (ln_scale, ln_bias, W1, b1, W2, b2, jnp.arange(n_experts)))
        return y.reshape(Bs, Ts, Ds)

    def _L1_cond_ref(x, h0, Wx, Wh, b):
        import jax, jax.numpy as jnp
        import numpy as np
        D = 128
        H = 128
        Hdim = h0.shape[1]
        x_proj = jnp.einsum('ntd,df->ntf', x, Wx) + b

        def step(carry, xp_t):
            prev_h, prev_c = carry
            h_bar = xp_t + prev_h @ Wh
            i = jax.nn.sigmoid(h_bar[:, 0:Hdim])
            f = jax.nn.sigmoid(h_bar[:, Hdim:2 * Hdim])
            o = jax.nn.sigmoid(h_bar[:, 2 * Hdim:3 * Hdim])
            g = jnp.tanh(h_bar[:, 3 * Hdim:4 * Hdim])
            next_c = f * prev_c + i * g
            next_h = o * jnp.tanh(next_c)
            return ((next_h, next_c), next_h)
        c0 = jnp.zeros_like(h0)
        xs = jnp.swapaxes(x_proj, 0, 1)
        _, hs = jax.lax.scan(step, (h0, c0), xs)
        return jnp.swapaxes(hs, 0, 1)

    def _L1_attn_ref(x, omega, wq, wk, wv, wo, bo):
        import jax, jax.numpy as jnp
        import numpy as np
        import math
        DIM = 128
        H = 16
        D = 64
        M = 64
        B = 1
        N = 256

        def _orf_omega(key):
            blocks = []
            n_blocks = (M + D - 1) // D
            for i in range(n_blocks):
                G = jax.random.normal(jax.random.fold_in(key, i), (D, D), dtype=jnp.float32)
                Q, _ = jnp.linalg.qr(G)
                blocks.append(Q.T)
            return jnp.concatenate(blocks, axis=0)[:M]

        def _phi(x, omega):
            proj = jnp.einsum('bhnd,md->bhnm', x, omega)
            norm = 0.5 * jnp.sum(x * x, axis=-1, keepdims=True)
            return jnp.exp(proj - norm) / math.sqrt(M)

        def _heads(t):
            b, n, _ = t.shape
            return t.reshape(b, n, H, D).transpose(0, 2, 1, 3)
        b, n, _ = x.shape
        q = _heads(x @ wq.T)
        k = _heads(x @ wk.T)
        v = _heads(x @ wv.T)
        phi_q = _phi(q, omega)
        phi_k = _phi(k, omega)
        kv = jnp.einsum('bhnm,bhnd->bhnmd', phi_k, v)
        kv_cumsum = jnp.cumsum(kv, axis=2)
        k_cumsum = jnp.cumsum(phi_k, axis=2)
        out = jnp.einsum('bhnm,bhnmd->bhnd', phi_q, kv_cumsum)
        z = 1.0 / (jnp.einsum('bhnm,bhnm->bhn', phi_q, k_cumsum) + 1e-06)
        out = out * z[..., None]
        out = out.transpose(0, 2, 1, 3).reshape(b, n, H * D)
        return out @ wo.T + bo

    def _L1_cond2_ref(x, h0, Wx, Wh, b):
        import jax, jax.numpy as jnp
        import numpy as np
        import math
        D = 128
        H = 128
        xz = jnp.einsum('ntd,dk->ntk', x, Wx) + b
        c0 = jnp.zeros_like(h0)

        def step(carry, xz_t):
            prev_h, prev_c = carry
            z = xz_t + prev_h @ Wh
            ai, af, ao, ag = jnp.split(z, 4, axis=1)
            i = jax.nn.sigmoid(ai)
            f = jax.nn.sigmoid(af)
            o = jax.nn.sigmoid(ao)
            g = jnp.tanh(ag)
            next_c = f * prev_c + i * g
            next_h = o * jnp.tanh(next_c)
            return ((next_h, next_c), next_h)
        _, hs = jax.lax.scan(step, (h0, c0), jnp.swapaxes(xz, 0, 1))
        return jnp.swapaxes(hs, 0, 1)

    def _L1_ffn_ref(x, Wr, br, W1, b1, g1, be1, W2, b2):
        import jax, jax.numpy as jnp
        import numpy as np
        IN_DIM = 128
        HIDDEN = 128
        OUT_DIM = 128
        NUM_EXPERTS = 16
        TOP_K = 2
        ROUTER_TEMP = 1.0
        LN_EPS = 1e-05

        def _layernorm(h, g, b):
            mu = jnp.mean(h, axis=-1, keepdims=True)
            var = jnp.mean(jnp.square(h - mu), axis=-1, keepdims=True)
            return (h - mu) * jax.lax.rsqrt(var + LN_EPS) * g + b
        orig_shape = x.shape[:-1]
        x_flat = x.reshape(-1, x.shape[-1])
        logits = (x_flat @ Wr + br) / max(ROUTER_TEMP, 1e-06)
        probs = jax.nn.softmax(logits, axis=-1)
        topk_w, topk_idx = jax.lax.top_k(probs, TOP_K)
        topk_w = topk_w / jnp.clip(jnp.sum(topk_w, axis=-1, keepdims=True), 1e-09)
        h = jnp.einsum('nc,ech->neh', x_flat, W1) + b1
        h = _layernorm(h, g1, be1)
        h = jax.nn.gelu(h, approximate=False)
        expert_out = jnp.einsum('neh,eho->neo', h, W2) + b2
        sel = jnp.take_along_axis(expert_out, topk_idx[:, :, None], axis=1)
        y_flat = jnp.sum(sel * topk_w[:, :, None], axis=1)
        return y_flat.reshape(*orig_shape, y_flat.shape[-1])

    def _L2_cond_ref(x, h0, Wx, Wh, b):
        import jax, jax.numpy as jnp
        import numpy as np
        import math
        D = 128
        H = 128
        Hdim = h0.shape[1]
        xW = jnp.einsum('ntd,dk->ntk', x, Wx) + b
        c0 = jnp.zeros_like(h0)

        def step(carry, xw_t):
            prev_h, prev_c = carry
            a = xw_t + prev_h @ Wh
            i = jax.nn.sigmoid(a[:, :Hdim])
            f = jax.nn.sigmoid(a[:, Hdim:2 * Hdim])
            o = jax.nn.sigmoid(a[:, 2 * Hdim:3 * Hdim])
            g = jnp.tanh(a[:, 3 * Hdim:])
            next_c = f * prev_c + i * g
            next_h = o * jnp.tanh(next_c)
            return ((next_h, next_c), next_h)
        xW_t = jnp.swapaxes(xW, 0, 1)
        _, hs = jax.lax.scan(step, (h0, c0), xW_t)
        hn = jnp.swapaxes(hs, 0, 1)
        return hn

    def _L2_attn_ref(x, W_q, W_dkv, W_uk, W_uv, W_o, ln_gamma, ln_beta):
        import jax, jax.numpy as jnp
        import numpy as np
        D_MODEL = 128
        N_HEADS = 16
        HEAD_DIM = D_MODEL // N_HEADS
        KV_LATENT = 32
        LN_EPS = 1e-05

        def apply_rope(x):
            b, h, t, d = x.shape
            half = d // 2
            pos = jnp.arange(t, dtype=x.dtype)[:, None]
            inv_freq = 1.0 / 10000.0 ** (jnp.arange(half, dtype=x.dtype) / half)
            angles = pos * inv_freq[None, :]
            sin = jnp.sin(angles)[None, None]
            cos = jnp.cos(angles)[None, None]
            x1, x2 = (x[..., :half], x[..., half:])
            return jnp.concatenate([x1 * cos - x2 * sin, x1 * sin + x2 * cos], axis=-1)
        b, t, _ = x.shape
        q = (x @ W_q).reshape(b, t, N_HEADS, HEAD_DIM).transpose(0, 2, 1, 3)
        lat = x @ W_dkv
        mu = jnp.mean(lat, axis=-1, keepdims=True)
        var = jnp.mean(jnp.square(lat - mu), axis=-1, keepdims=True)
        lat = (lat - mu) * jax.lax.rsqrt(var + LN_EPS) * ln_gamma + ln_beta
        k = (lat @ W_uk).reshape(b, t, N_HEADS, HEAD_DIM).transpose(0, 2, 1, 3)
        v = (lat @ W_uv).reshape(b, t, N_HEADS, HEAD_DIM).transpose(0, 2, 1, 3)
        q = apply_rope(q)
        k = apply_rope(k)
        scores = jnp.einsum('bhqd,bhkd->bhqk', q, k) / jnp.sqrt(jnp.float32(HEAD_DIM))
        causal = jnp.tril(jnp.ones((t, t), dtype=bool))
        scores = jnp.where(causal[None, None], scores, -jnp.inf)
        attn = jax.nn.softmax(scores, axis=-1)
        out = jnp.einsum('bhqk,bhkd->bhqd', attn, v)
        out = out.transpose(0, 2, 1, 3).reshape(b, t, D_MODEL)
        return out @ W_o

    def _L2_cond2_ref(video, seq, W_z, U_z, C_z, b_z, W_r, U_r, C_r, b_r, W, U, C, b):
        import jax, jax.numpy as jnp
        import numpy as np
        B, T, D_IN, V_IN, E = (64, 128, 128, 128, 128)
        vz = video @ C_z + b_z
        vr = video @ C_r + b_r
        vh = video @ C + b
        xz = jnp.einsum('btd,de->bte', seq, W_z)
        xr = jnp.einsum('btd,de->bte', seq, W_r)
        xh = jnp.einsum('btd,de->bte', seq, W)

        def step(h, xs):
            xzt, xrt, xht = xs
            z = jax.nn.sigmoid(xzt + h @ U_z + vz)
            r = jax.nn.sigmoid(xrt + h @ U_r + vr)
            hh = jnp.tanh(xht + r * h @ U + vh)
            h_new = (1.0 - z) * h + z * hh
            return (h_new, h_new)
        h0 = jnp.zeros((seq.shape[0], U.shape[0]), seq.dtype)
        xs = (jnp.swapaxes(xz, 0, 1), jnp.swapaxes(xr, 0, 1), jnp.swapaxes(xh, 0, 1))
        _, out_t = jax.lax.scan(step, h0, xs)
        return jnp.swapaxes(out_t, 0, 1)

    def _L2_ffn_ref(inputs, ew, act_w, We, be, Wq, Wk, Wv, Wo, ln_g, ln_b):
        import jax, jax.numpy as jnp
        import numpy as np
        NUM_NOD = 6
        MAX_PREV = 5
        NUM_EDGE = 20
        D = 128
        H = 8
        LN_EPS = 1e-06

        def _layernorm(x, g, b):
            mu = jnp.mean(x, axis=-1, keepdims=True)
            var = jnp.mean(jnp.square(x - mu), axis=-1, keepdims=True)
            return (x - mu) * jax.lax.rsqrt(var + LN_EPS) * g + b

        def _mha(q, k, v, wq, wk, wv, wo):
            B, S, d = q.shape
            dh = d // H
            qh = (q @ wq).reshape(B, S, H, dh)
            kh = (k @ wk).reshape(B, S, H, dh)
            vh = (v @ wv).reshape(B, S, H, dh)
            scores = jnp.einsum('bqhd,bkhd->bhqk', qh, kh) / jnp.sqrt(jnp.asarray(dh, q.dtype))
            attn = jax.nn.softmax(scores, axis=-1)
            ctx = jnp.einsum('bhqk,bkhd->bqhd', attn, vh).reshape(B, S, d)
            return ctx @ wo
        nodes = {-1: inputs}
        lind = 0
        for c in range(NUM_NOD):
            nsrc = min(c + 1, MAX_PREV)
            snode = c - nsrc
            eq, ek, ev = (lind + nsrc - 1, lind, lind + nsrc // 2)
            in_q, in_k, in_v = (c - 1, snode, snode + nsrc // 2)
            q = ew[c, 0] * (nodes[in_q] @ We[eq] + be[eq])
            k = ew[c, 1] * (nodes[in_k] @ We[ek] + be[ek])
            v = ew[c, 2] * (nodes[in_v] @ We[ev] + be[ev])
            o = _mha(q, k, v, Wq[c], Wk[c], Wv[c], Wo[c])
            nodes[c] = act_w[c] * o + q
            lind += nsrc
        out = nodes[NUM_NOD - 1]
        return _layernorm(out, ln_g, ln_b)

    def _L3_cond_ref(Efou, y, weight):
        import jax, jax.numpy as jnp
        import numpy as np
        IN_FEATURES = 128
        OUT_FEATURES = 128
        BATCH = 32
        SEQ = 128
        EPS = 1e-08
        scale = 1.0 / np.sqrt(np.float32(weight.shape[0]))
        ys = y * scale
        d = jax.lax.rsqrt(jnp.einsum('bi,io->bo', ys * ys, weight * weight) + EPS)
        out = jnp.einsum('bsi,io->bso', Efou * ys[:, None, :], weight) * d[:, None, :]
        return out

    def _L3_attn_ref(x, Wq, Wk, Wv, Wo):
        import jax, jax.numpy as jnp
        import numpy as np
        D_MODEL = 128
        NUM_HEADS = 16
        HEAD_DIM = D_MODEL // NUM_HEADS
        WINDOW = 128
        SCALE = HEAD_DIM ** (-0.5)
        B, S, _ = x.shape

        def heads(W):
            return (x @ W.T).reshape(B, S, NUM_HEADS, HEAD_DIM).transpose(0, 2, 1, 3)
        q, k, v = (heads(Wq), heads(Wk), heads(Wv))
        attn = jnp.einsum('bhqd,bhkd->bhqk', q, k) * SCALE
        idx = jnp.arange(S)
        band = jnp.abs(idx[:, None] - idx[None, :]) <= WINDOW
        attn = jnp.where(band[None, None], attn, -jnp.inf)
        attn = jax.nn.softmax(attn, axis=-1)
        out = jnp.einsum('bhqk,bhkd->bhqd', attn, v)
        out = out.transpose(0, 2, 1, 3).reshape(B, S, D_MODEL)
        return out @ Wo.T

    def _L3_cond2_ref(x, t_emb, router_W, router_bias, w1, w3, w2, W1e, W2e):
        import jax, jax.numpy as jnp
        import numpy as np
        D, HS, HE, E, K = (128, 256, 128, 8, 2)
        B, T = (4, 128)
        N_SHARED = 1
        Bb, Tt, C = x.shape
        xf = x.reshape(-1, C)
        tf = jnp.broadcast_to(t_emb[:, None, :], (Bb, Tt, C)).reshape(-1, C)
        N = xf.shape[0]
        shared = jax.nn.silu(xf @ w1) * (xf @ w3) @ w2
        s = jax.nn.sigmoid((jnp.concatenate([xf, tf], axis=-1) @ router_W).astype(jnp.float32))
        sel_scores = s + router_bias
        _, topk_idx = jax.lax.top_k(sel_scores, K)
        s_sel = jnp.take_along_axis(s, topk_idx, axis=1)
        denom = s_sel.sum(axis=1, keepdims=True)
        gates = jnp.where(denom > 1e-09, s_sel / (denom + 1e-09), 1.0 / K).astype(x.dtype)
        combine = jnp.zeros((N, E), x.dtype).at[jnp.arange(N)[:, None], topk_idx].add(gates)
        h = jax.nn.gelu(jnp.einsum('nc,ech->enh', xf, W1e), approximate=False)
        y = jnp.einsum('enh,ehc->enc', h, W2e)
        routed = jnp.einsum('ne,enc->nc', combine, y)
        return ((shared + routed) / (N_SHARED + K)).reshape(Bb, Tt, C)

    def _L3_ffn_ref(x, Wp, sim_matrix, temperature, W1, b1, W2, b2):
        import jax, jax.numpy as jnp
        import numpy as np
        EPS = 1e-12

        def _l2norm(v):
            n = jnp.sqrt(jnp.sum(v * v, axis=-1, keepdims=True))
            return v / jnp.maximum(n, EPS)
        E = sim_matrix.shape[0]
        top_k = 2
        proj = jnp.einsum('bsd,ed->bse', x, Wp)
        pn = _l2norm(proj)
        sn = _l2norm(sim_matrix)
        gate_scores = jnp.einsum('bsd,ed->bse', pn, sn) / temperature
        top_v, top_i = jax.lax.top_k(gate_scores, top_k)
        gate_probs = jax.nn.softmax(top_v, axis=-1)
        comb = jnp.sum(jax.nn.one_hot(top_i, E, dtype=x.dtype) * gate_probs[..., None], axis=-2)
        h = jax.nn.gelu(jnp.einsum('bsd,edf->ebsf', x, W1) + b1[:, None, None, :], approximate=False)
        eo = jnp.einsum('ebsf,efd->ebsd', h, W2) + b2[:, None, None, :]
        out = jnp.einsum('ebsd,bse->bsd', eo, comb)
        return out
    x = x + _L0_attn_ref(_L0_cond_ref(x, fside_Bx1x1024x16_0, fside_Bx1x1024x16_0, cond_1024[:, None, :], L0_cond_W, L0_cond_fc_bias), L0_attn_c, L0_attn_Wq, L0_attn_bq, L0_attn_Wk, L0_attn_bk, L0_attn_Wv, L0_attn_bv, L0_attn_Wo, L0_attn_bo, L0_attn_rel_table)
    x = x + _L0_ffn_ref(_L0_cond2_ref(cond_1024, x, L0_cond2_W, L0_cond2_b, L0_cond2_alpha), L0_ffn_Wg, L0_ffn_ln_scale, L0_ffn_ln_bias, L0_ffn_W1, L0_ffn_b1, L0_ffn_W2, L0_ffn_b2)
    x = x + _L1_attn_ref(_L1_cond_ref(x, cond_1024, L1_cond_Wx, L1_cond_Wh, L1_cond_b), L1_attn_omega, L1_attn_wq, L1_attn_wk, L1_attn_wv, L1_attn_wo, L1_attn_bo)
    x = x + _L1_ffn_ref(_L1_cond2_ref(x, cond_1024, L1_cond2_Wx, L1_cond2_Wh, L1_cond2_b), L1_ffn_Wr, L1_ffn_br, L1_ffn_W1, L1_ffn_b1, L1_ffn_g1, L1_ffn_be1, L1_ffn_W2, L1_ffn_b2)
    x = x + _L2_attn_ref(_L2_cond_ref(x, cond_1024, L2_cond_Wx, L2_cond_Wh, L2_cond_b), L2_attn_W_q, L2_attn_W_dkv, L2_attn_W_uk, L2_attn_W_uv, L2_attn_W_o, L2_attn_ln_gamma, L2_attn_ln_beta)
    x = x + _L2_ffn_ref(_L2_cond2_ref(cond_1024, x, L2_cond2_W_z, L2_cond2_U_z, L2_cond2_C_z, L2_cond2_b_z, L2_cond2_W_r, L2_cond2_U_r, L2_cond2_C_r, L2_cond2_b_r, L2_cond2_W, L2_cond2_U, L2_cond2_C, L2_cond2_b), L2_ffn_ew, L2_ffn_act_w, L2_ffn_We, L2_ffn_be, L2_ffn_Wq, L2_ffn_Wk, L2_ffn_Wv, L2_ffn_Wo, L2_ffn_ln_g, L2_ffn_ln_b)
    x = x + _L3_attn_ref(_L3_cond_ref(x, cond_1024, L3_cond_weight), L3_attn_Wq, L3_attn_Wk, L3_attn_Wv, L3_attn_Wo)
    x = x + _L3_ffn_ref(_L3_cond2_ref(x, cond_1024, L3_cond2_router_W, L3_cond2_router_bias, L3_cond2_w1, L3_cond2_w3, L3_cond2_w2, L3_cond2_W1e, L3_cond2_W2e), L3_ffn_Wp, L3_ffn_sim_matrix, L3_ffn_temperature, L3_ffn_W1, L3_ffn_b1, L3_ffn_W2, L3_ffn_b2)
    return x

_drawn_inputs = setup_inputs


def setup_inputs(seed=0):
    import zlib

    import numpy as np

    out = dict(_drawn_inputs(seed))
    spreads = {'L0_attn_bq': (0.0, 0.537),
     'L0_attn_bk': (0.0, 2.0),
     'L0_attn_bv': (0.0, 0.1),
     'L0_attn_bo': (0.0, 0.1),
     'L0_cond2_alpha': (0.10000000149011612, 0.6),
     'L0_ffn_ln_scale': (1.0, 0.6),
     'L0_ffn_ln_bias': (0.0, 0.8),
     'L0_ffn_b1': (0.0, 0.403),
     'L0_ffn_b2': (0.0, 0.1),
     'L1_cond_b': (0.0, 0.452),
     'L1_attn_bo': (0.0, 0.1),
     'L1_cond2_b': (0.0, 0.1),
     'L1_ffn_g1': (1.0, 0.2),
     'L1_ffn_be1': (0.0, 0.415),
     'L2_cond_b': (0.0, 0.289),
     'L2_attn_ln_gamma': (1.0, 0.2),
     'L2_attn_ln_beta': (0.0, 0.288),
     'L2_cond2_b_z': (0.0, 2.0),
     'L2_cond2_b_r': (0.0, 0.8),
     'L2_cond2_b': (0.0, 0.1),
     'L2_ffn_be': (0.0, 0.1),
     'L2_ffn_ln_g': (1.0, 0.2),
     'L2_ffn_ln_b': (0.0, 0.1),
     'L3_cond2_router_bias': (0.0, 0.1),
     'L3_ffn_b1': (0.0, 0.471),
     'L3_ffn_b2': (0.0, 0.1)}
    factors = {'fside_Bx1x1024x16_0': 4.44,
     'L0_attn_rel_table': 8.0,
     'L0_cond2_b': 7.136,
     'L1_attn_omega': 8.0,
     'L1_attn_wq': 8.0,
     'L1_attn_wk': 8.0,
     'L2_attn_W_q': 8.0,
     'L2_attn_W_uk': 8.0,
     'L2_cond2_W_z': 22.857,
     'L2_cond2_U_z': 52.603,
     'L2_cond2_C_z': 28.691,
     'L2_cond2_W_r': 8.0,
     'L2_cond2_U_r': 34.483,
     'L2_cond2_C_r': 8.0,
     'L2_cond2_U': 8.0,
     'L2_ffn_Wq': 64.0,
     'L2_ffn_Wk': 64.0,
     'L3_ffn_W1': 8.0,
     'L3_ffn_W2': 3.258}
    for name, (base, spread) in spreads.items():
        noise = np.random.default_rng([zlib.crc32(name.encode()), seed]).standard_normal(out[name].shape)
        drawn = base * np.exp(spread * noise) if base else spread * noise
        out[name] = jnp.asarray(drawn.astype(out[name].dtype))
    for name, factor in factors.items():
        out[name] = (out[name] * factor).astype(out[name].dtype)
    return out
```

```python
import math
from contextlib import ExitStack, contextmanager

import numpy as np
import concourse.bass as bass
from concourse import mybir

F32 = mybir.dt.float32
ALU = mybir.AluOpType
ACT = mybir.ActivationFunctionType
AX_X = mybir.AxisListType.X

P = 128
NB = 32
NTOK = NB * P
BANK = 512
CHUNK = 512
NCHUNK = NTOK // CHUNK
MASKED = -1.0e30

PACKS = {
    "const": dict(ident=P, center=P, mean=P, head8=4, head16=2, causal_add=P, causal_mul=P, gate_pick=P,
                  cos=P, sin=P, center32=32, mean32=P, half_block=P, cond=NB, eps5=1, eps6=1, eps8=1,
                  ln_m=1, tie8=8, tie16=16),
    "p0": dict(W=P, fc_bias=1, Wq=P, Wk=P, Wv=P, Wo=P, bq=1, bk=1, bv=1, bo=1, rel=16 * P),
    "p1": dict(WhT=P, WzT=P, b=1, alpha=1, WgT=8, ln_scale=8, ln_bias=8, W1=256, b1=2, W2=2 * P, b2=P),
    "p2": dict(Wx=512, Wh=512, b=P, omegaT=P, wqT=1024, wkT=1024, wvT=1024, woT=1024, bo=1),
    "p3": dict(Wx=512, Wh=512, b=P, Wr=16, br=16, W1T=2048, b1=16, g1=16, be1=16, W2=2048, b2=P),
    "p4": dict(Wx=512, Wh=512, b=P, Wq=P, Wqs=P, WdT=P, Wuk=P, Wuks=P, Wuv=P, Wo=P, gamma=1, beta=1),
    "p5": dict(Wz=P, Uz=P, Cz=P, bz=1, Wr=P, Ur=P, Cr=P, br=1, W=P, U=P, C=P, b=1, ew=18, act=6,
               We=6 * P, WeT=18 * P, be=18, Wq=6 * P, Wk=6 * P, Wv=6 * P, Wo=6 * P, ln_g=1, ln_b=1),
    "p6": dict(weight=P, Wq=P, Wk=P, Wv=P, Wo=P),
    "p7": dict(rW=8, rT=8, rbias=8, w1=256, w3=256, w2=2 * P, W1e=8 * P, W2e=8 * P, Wp=P, WpT=P, sim=P,
               temp=1, W1=32 * P, b1=32, W2=32 * P, b2=P),
}
WIDTH = {k: sum(v.values()) for k, v in PACKS.items()}
REGION = [max(WIDTH[f"p{k}"] for k in range(r, 8, 2)) for r in range(2)]
LOADS = ["const"] + [f"p{k}" for k in range(8)]


class Step:

    def __init__(self, i, k, unroll):
        self.i, self.k, self.unroll = i, k, unroll
        self.n, self.m, self.u = i * unroll + k, k % unroll, i + k // unroll

    def back(self):
        return Step(self.i, self.k - 1, self.unroll)


class View:

    def __init__(self, tile, pack):
        self.tile, self.at, here = tile, {}, 0
        for name, n in PACKS[pack].items():
            self.at[name] = (here, n)
            here += n

    def __call__(self, name, lo=0, n=None, rows=P, first=0):
        here, width = self.at[name]
        n = width - lo if n is None else n
        return self.tile[first:first + rows, here + lo:here + lo + n]


class Core:

    def __init__(self, nc, ctx):
        self.nc = nc
        self.x = ctx.enter_context(nc.sbuf_tensor("x_res", [P, NTOK], F32))
        self.a = ctx.enter_context(nc.sbuf_tensor("act_a", [P, NTOK], F32))
        self.b = ctx.enter_context(nc.sbuf_tensor("act_b", [P, NTOK], F32))
        self.region = [ctx.enter_context(nc.sbuf_tensor(f"weights{r}", [P, REGION[r]], F32)) for r in range(2)]
        self.gates = ctx.enter_context(nc.sbuf_tensor("gates", [P, NB * 16], F32))
        self.ctile = ctx.enter_context(nc.sbuf_tensor("constants", [P, WIDTH["const"]], F32))
        self.ps = ctx.enter_context(nc.psum_tensor("banks", [P, 8, BANK], F32))
        self.loaded = {k: ctx.enter_context(nc.semaphore(f"loaded_{k}")) for k in LOADS + ["x", "f"]}
        self.const = View(self.ctile, "const")

    def gate(self, ne):
        return self.gates[:, 0:NB * ne].rearrange("p (t e) -> p t e", e=ne)

    def pack(self, k):
        return View(self.region[k % 2], f"p{k}")


@contextmanager
def stage_scope(nc):
    before = nc.snapshot_sems()
    with ExitStack() as ctx:
        yield ctx
    nc.clear_and_free_semaphores(nc.allocated_since(before))
    nc.all_engine_barrier()


def load_pack(sp, core, dram, k):
    w = WIDTH[f"p{k}"]
    half = w // 2
    sp.dma_start(core.region[k % 2][:, 0:half], dram[f"p{k}"][:, 0:half]).then_inc(core.loaded[f"p{k}"], 16)
    sp.dma_start(core.region[k % 2][:, half:w], dram[f"p{k}"][:, half:w]).then_inc(core.loaded[f"p{k}"], 16)


def wait_pack(eng, core, k):
    eng.wait_ge(core.loaded[f"p{k}"], 32)


def past(eng, sem, value):
    if not isinstance(value, int) or value > 0:
        eng.wait_ge(sem, value)


def tok(t, n):
    return bass.ds(t, n)


def low_rank_stage(core, dram):
    nc, w, ps = core.nc, core.pack(0), core.ps
    with stage_scope(nc) as ctx:
        sb = lambda name, shape: ctx.enter_context(nc.sbuf_tensor("lr_" + name, shape, F32))
        sem = lambda name: nc.alloc_semaphore("lr_" + name)
        factor = sb("factor", [16, 2, P])
        weight = sb("weight", [P, 2, P])
        shift = sb("shift", [P, NB])
        shift_ready, factor_ready, gram_done, weight_ready, y_done, gelu_done = map(
            sem, ["shift_ready", "factor_ready", "gram_done", "weight_ready", "y_done", "gelu_done"])
        block = ctx.enter_context(nc.Block())

        @block.sync
        def _(sp):
            sp.dma_start(core.b[0:16, :], dram["factors"]).then_inc(core.loaded["f"], 16)
            load_pack(sp, core, dram, 0)
            sp.dma_start(core.ctile[:, :], dram["const"]).then_inc(core.loaded["const"], 16)
            sp.dma_start(core.x[:, :], dram["x"]).then_inc(core.loaded["x"], 16)
            load_pack(sp, core, dram, 1)

        @block.gpsimd
        def _(pool):
            pool.wait_ge(core.loaded["f"], 16)

            def copy(b, p, first):
                if not first:
                    pool.wait_ge(gram_done, b - 1)
                pool.tensor_copy(factor[:, p, :], core.b[0:16, tok(b * P, P)]).then_inc(factor_ready, 1)

            copy(0, 0, True)
            copy(1, 1, True)
            with pool.Fori(1, NB // 2) as i:
                copy(i * 2, 0, False)
                copy(i * 2 + 1, 1, False)

        @block.tensor
        def _(pe):
            pe.wait_ge(core.loaded["x"], 16)

            def pair(i, first):
                for p in range(2):
                    pe.wait_ge(factor_ready, i * 2 + p + 1)
                    if not first:
                        pe.wait_ge(weight_ready, i * 2 + p - 1)
                    pe.matmul(ps[:, p, 0:P], factor[:, p, :], factor[:, p, :], start=True, stop=True).then_inc(
                        gram_done, 1)
                for p in range(2):
                    pe.wait_ge(weight_ready, i * 2 + p + 1)
                    if not first:
                        pe.wait_ge(gelu_done, i * 2 + p - 1)
                    pe.matmul(ps[:, 2 + p, 0:P], weight[:, p, :], core.x[:, tok((i * 2 + p) * P, P)],
                              start=True, stop=True).then_inc(y_done, 1)

            pair(0, True)
            with pe.Fori(1, NB // 2) as i:
                pair(i, False)

        @block.vector
        def _(dve):
            dve.wait_ge(core.loaded["const"], 16)
            wait_pack(dve, core, 0)
            dve.tensor_scalar(shift[:, :], core.const("cond"), w("fc_bias"), None, ALU.add).then_inc(shift_ready, 1)

            def one(b, p, first):
                dve.wait_ge(gram_done, b + 1)
                if not first:
                    dve.wait_ge(y_done, b - 1)
                dve.scalar_tensor_tensor(out=weight[:, p, :], in0=ps[:, p, 0:P], scalar=1.0 / (P * 16),
                                         in1=w("W"), op0=ALU.mult, op1=ALU.add).then_inc(weight_ready, 1)

            one(0, 0, True)
            one(1, 1, True)
            with dve.Fori(1, NB // 2) as i:
                one(i * 2, 0, False)
                one(i * 2 + 1, 1, False)

        @block.scalar
        def _(act):
            act.wait_ge(shift_ready, 1)
            with act.Fori(0, NB // 2) as i:
                for p in range(2):
                    b = i * 2 + p
                    act.wait_ge(y_done, b + 1)
                    act.activation(core.a[:, tok(b * P, P)], ps[:, 2 + p, 0:P], ACT.Gelu,
                                   bias=shift[:, tok(b, 1)]).then_inc(gelu_done, 1)


def attention_stage(core, name, steps, unroll, heads, cfg, next_load=None):
    nc, ps, const = core.nc, core.ps, core.const
    dh = P // heads
    per = 32 // dh
    batches = 4 // per
    nt = batches * P
    nh = batches * heads
    head_mask = const("head8" if dh == 8 else "head16")
    QKV, CTX = 6, 7
    with stage_scope(nc) as ctx:
        sb = lambda n, shape: ctx.enter_context(nc.sbuf_tensor(f"{name}_{n}", shape, F32))
        sem = lambda n: nc.alloc_semaphore(f"{name}_{n}")
        qm = sb("q_masked", [P, 2, per, nt])
        kt = sb("key", [P, 2, nt])
        span = heads * (dh + 1)
        vt = sb("value", [P, 2, batches, heads * (span + dh + 1)])
        e = sb("probs", [P, 2, 4, BANK])
        et = sb("probs_turned", [P, 4, BANK])
        mx = sb("row_max", [P, 2, 4])
        rs = sb("row_scale", [P, nh])
        o = sb("context", [P, nt])
        ot = sb("context_turned", [P, nt])
        s = {n: sem(n) for n in ["zero_ready", "ones_ready", "qk_done", "q_ready", "k_ready", "v_done", "v_ready",
                                 "scores_done", "max_ready", "scores_read", "exp_done", "turn_done", "turned_ready",
                                 "pv_done", "scale_ready", "context_ready", "ct_done", "ct_ready", "out_done",
                                 "out_read", "source_ready", "own"]}
        bufs = cfg(nc, ctx, s, name, qm, kt, ot)

        def own_columns(lo, hi):
            return vt[:, :, :, :].rearrange("q p b (h c) -> q p b h c", h=heads)[:, :, :, :, lo:hi]

        block = ctx.enter_context(nc.Block())
        loops = steps // unroll - 1
        assert (loops + 1) * unroll == steps and unroll >= 4

        def tiles(g):
            for t in range(4):
                bb, r = t // per, t % per
                yield t, bb, r, g * per + r

        def run(eng, body):
            for k in range(unroll):
                body(*(Step(0, k - d, unroll) if k >= d else None for d in range(4)))
            with eng.Fori(0, loops) as i:
                for k in range(unroll, 2 * unroll):
                    body(*(Step(i, k - d, unroll) for d in range(4)))
            for k in range(steps, steps + 3):
                body(*(Step(0, k - d, unroll) if k - d < steps else None for d in range(4)))

        @block.sync
        def _(sp):
            if next_load is not None:
                next_load(sp)

        @block.gpsimd
        def _(pool):
            pool.memset(vt[:, :, :, :], 0.0).then_inc(s["zero_ready"], 1)
            pool.wait_ge(s["zero_ready"], 1)
            for p in range(2):
                for bb in range(batches):
                    last = pool.memset(own_columns(dh, dh + 1)[:, p, bb], 1.0)
            last.then_inc(s["ones_ready"], 1)

            def body(a, m, c, t):
                if a is not None:
                    bufs["pool"](pool, a)

            run(pool, body)

        @block.tensor
        def _(pe):
            bufs["start"](pe)

            def project(st):
                past(pe, s["out_read"], st.n - 2)
                past(pe, s["v_ready"], st.n)
                bufs["pe_qk"](pe, st, QKV).then_inc(s["qk_done"], 1)

            def value(st):
                pe.wait_ge(s["q_ready"], st.n + 1)
                pe.wait_ge(s["k_ready"], st.n + 1)
                bufs["pe_v"](pe, st, QKV).then_inc(s["v_done"], 1)

            def scores(st, g):
                n, p = st.n, st.m % 2
                past(pe, s["scores_read"], n * 4 + (g - 3))
                bias = bufs.get("bias")
                if bias is not None:
                    bias(pe, ps[:, g, :].rearrange("p (t j) -> p t j", t=4), g)
                for t, bb, r, h in tiles(g):
                    last = pe.matmul(ps[:, g, t * P:(t + 1) * P], qm[32 * g:32 * g + 32, p, r, bb * P:(bb + 1) * P],
                                     kt[32 * g:32 * g + 32, p, bb * P:(bb + 1) * P],
                                     start=bias is None, stop=True, skip_group_check=bias is not None)
                last.then_inc(s["scores_done"], 1)

            def turn(st, g):
                n, p = st.n, st.m % 2
                pe.wait_ge(s["exp_done"], n * 4 + (g + 1))
                past(pe, s["turned_ready"], n * 4 + (g - 1))
                for t in range(4):
                    last = pe.transpose(ps[:, 4 + g % 2, t * P:(t + 1) * P], e[:, p, g, t * P:(t + 1) * P],
                                        const("ident"))
                last.then_inc(s["turn_done"], 1)

            def context(st, g):
                n, p = st.n, st.m % 2
                pe.wait_ge(s["turned_ready"], n * 4 + (g + 1))
                if g == 0:
                    pe.wait_ge(s["v_ready"], n + 1)
                    past(pe, s["context_ready"], n)
                for t, bb, r, h in tiles(g):
                    last = pe.matmul(ps[:, CTX, bb * span:(bb + 1) * span], et[:, g, t * P:(t + 1) * P],
                                     vt[:, p, bb, h * span:(h + 1) * span], start=(g == 0 and t == 0),
                                     stop=(g == 3), skip_group_check=True)
                last.then_inc(s["pv_done"], 1)

            def turn_context(st, newest):
                pe.wait_ge(s["context_ready"], st.n + 1)
                if newest is not None:
                    pe.wait_ge(s["v_ready"], newest.n + 1)
                for bb in range(batches):
                    last = pe.transpose(ps[:, QKV, bb * P:(bb + 1) * P], o[:, bb * P:(bb + 1) * P], const("ident"))
                last.then_inc(s["ct_done"], 1)

            def output(st):
                pe.wait_ge(s["ct_ready"], st.n + 1)
                bufs["pe_out"](pe, st, QKV).then_inc(s["out_done"], 1)

            def body(a, m, c, t):
                for g in range(4):
                    if c is not None:
                        turn(c, g)
                    if g == 3 and a is not None:
                        project(a)
                    if m is not None:
                        scores(m, g)
                    if g == 1 and t is not None:
                        turn_context(t, m)
                    if g >= 1 and c is not None:
                        context(c, g - 1)
                    if g == 2 and t is not None:
                        output(t)
                if c is not None:
                    context(c, 3)
                if a is not None:
                    value(a)

            run(pe, body)

        @block.scalar
        def _(act):
            bufs["start"](act)
            act.wait_ge(s["ones_ready"], 1)

            def value(st):
                act.wait_ge(s["v_done"], st.n + 1)
                past(act, s["pv_done"], st.n * 4 - 4)
                act.activation(own_columns(0, dh)[:, st.m % 2], ps[:, QKV, 0:nt].rearrange(
                    "p (b h d) -> p b h d", b=batches, d=dh), ACT.Copy).then_inc(s["v_ready"], 1)

            def exps(st, g):
                act.wait_ge(s["scores_read"], st.n * 4 + (g + 1))
                act.activation(e[:, st.m % 2, g, :], e[:, st.m % 2, g, :], ACT.Exp).then_inc(s["exp_done"], 1)

            def turned(st, g):
                act.wait_ge(s["turn_done"], st.n * 4 + (g + 1))
                past(act, s["pv_done"], st.n * 4 + (g - 3))
                act.activation(et[:, g, :], ps[:, 4 + g % 2, :], ACT.Copy).then_inc(s["turned_ready"], 1)

            def context(st):
                act.wait_ge(s["ct_done"], st.n + 1)
                past(act, s["out_done"], st.n)
                act.activation(ot[:, :], ps[:, QKV, 0:nt], ACT.Identity, bias=bufs["bv"](st.m)).then_inc(
                    s["ct_ready"], 1)

            def body(a, m, c, t):
                for g in range(4):
                    if c is not None:
                        turned(c, g)
                    if g == 0 and m is not None:
                        value(m)
                    if g == 1 and t is not None:
                        context(t)
                    if g == 3 and a is not None and "act_k" in bufs:
                        bufs["act_k"](act, a, QKV)
                    if g >= 1 and m is not None:
                        exps(m, g - 1)
                if m is not None:
                    exps(m, 3)

            run(act, body)

        @block.vector
        def _(dve):
            bufs["start"](dve)

            def softmax_in(st, g):
                n = st.n
                dve.wait_ge(s["scores_done"], n * 4 + (g + 1))
                bank = ps[:, g, :].rearrange("p (t j) -> p t j", t=4)
                past(dve, s["scores_read"], n * 4 + (g - 1))
                dve.tensor_reduce(mx[:, g % 2, :], bank, AX_X, ALU.max).then_inc(s["max_ready"], 1)
                dve.wait_ge(s["max_ready"], n * 4 + (g + 1))
                past(dve, s["turn_done"], n * 4 + (g - 7))
                dve.tensor_tensor(e[:, st.m % 2, g, :].rearrange("p (t j) -> p t j", t=4), bank,
                                  mx[:, g % 2, :].unsqueeze(2).broadcast_to([P, 4, P]), ALU.subtract).then_inc(
                    s["scores_read"], 1)

            def normalise(st):
                n = st.n
                dve.wait_ge(s["pv_done"], n * 4 + 4)
                ctx_ps = ps[:, CTX, 0:nh * (dh + 1)].rearrange("p (h d) -> p h d", d=dh + 1)
                past(dve, s["context_ready"], n)
                dve.reciprocal(rs[:, :], ctx_ps[:, :, dh]).then_inc(s["scale_ready"], 1)
                dve.wait_ge(s["scale_ready"], n + 1)
                past(dve, s["ct_done"], n)
                dve.tensor_tensor(o[:, :].rearrange("p (h d) -> p h d", d=dh), ctx_ps[:, :, 0:dh],
                                  rs[:, :].unsqueeze(2).broadcast_to([P, nh, dh]), ALU.mult).then_inc(
                    s["context_ready"], 1)

            def body(a, m, c, t):
                for g in range(4):
                    if g == 3 and t is not None:
                        dve.wait_ge(s["out_done"], t.n + 1)
                        bufs["dve_out"](dve, t, QKV).then_inc(s["out_read"], 1)
                    if g == 3 and a is not None:
                        bufs["dve_q"](dve, a, QKV, head_mask)
                    if m is not None:
                        softmax_in(m, g)
                if c is not None:
                    normalise(c)

            run(dve, body)


def plain_attention(core, k, with_bias):
    w, const, ps = core.pack(k), core.const, core.ps

    def cfg(nc, ctx, s, name, qm, kt, ot):
        src = ctx.enter_context(nc.sbuf_tensor(f"{name}_src", [P, 2, P], F32))
        zero = None if with_bias else ctx.enter_context(nc.sbuf_tensor(f"{name}_zero", [P, 1], F32))

        def start(eng):
            wait_pack(eng, core, k)
            if zero is not None:
                if eng is nc.vector:
                    eng.memset(zero[:, :], 0.0).then_inc(s["own"], 1)
                eng.wait_ge(s["own"], 1)

        def pool(pool, st):
            n, m = st.n, st.m
            past(pool, s["v_done"], n - 1)
            pool.tensor_copy(src[:, m % 2, :], core.a[:, tok(n * P, P)]).then_inc(s["source_ready"], 1)

        def pe_qk(pe, st, bank):
            n, m = st.n, st.m
            pe.wait_ge(s["source_ready"], n + 1)
            pe.matmul(ps[:, bank, 0:P], w("Wq"), src[:, m % 2, :], start=True, stop=True)
            return pe.matmul(ps[:, bank, P:2 * P], w("Wk"), src[:, m % 2, :], start=True, stop=True)

        def pe_v(pe, st, bank):
            n, m = st.n, st.m
            return pe.matmul(ps[:, bank, 0:P], src[:, m % 2, :], w("Wv"), start=True, stop=True)

        def pe_out(pe, st, bank):
            n, m = st.n, st.m
            return pe.matmul(ps[:, bank, P:2 * P], w("Wo"), ot[:, :], start=True, stop=True)

        bq, bk, bv, bo = [w(x) if with_bias else zero[:, :] for x in ("bq", "bk", "bv", "bo")]

        def act_k(act, st, bank):
            n, m = st.n, st.m
            act.wait_ge(s["q_ready"], n + 1)
            act.activation(kt[:, m % 2, :], ps[:, bank, P:2 * P], ACT.Identity, bias=bk).then_inc(s["k_ready"], 1)

        def dve_q(dve, st, bank, head_mask):
            n, m = st.n, st.m
            dve.wait_ge(s["qk_done"], n + 1)
            dve.scalar_tensor_tensor(out=qm[:, m % 2, :, :], in0=ps[:, bank, 0:P].unsqueeze(1).broadcast_to([P, 4, P]),
                                     scalar=bq, in1=head_mask.unsqueeze(2).broadcast_to([P, 4, P]),
                                     op0=ALU.add, op1=ALU.mult).then_inc(s["q_ready"], 1)

        def dve_out(dve, st, bank):
            n, m = st.n, st.m
            xb = core.x[:, tok(n * P, P)]
            return dve.scalar_tensor_tensor(out=xb, in0=ps[:, bank, P:2 * P], scalar=bo, in1=xb,
                                            op0=ALU.add, op1=ALU.add)

        cfg_out = dict(start=start, pool=pool, pe_qk=pe_qk, pe_v=pe_v, pe_out=pe_out, act_k=act_k, dve_q=dve_q,
                       dve_out=dve_out, bv=lambda m: bv)
        if with_bias:
            def bias(pe, out, g):
                pe.matmul(out, const("ident"), w("rel", g * BANK, BANK).rearrange("p (t j) -> p t j", t=4), start=True,
                          stop=False, skip_group_check=True)

            cfg_out["bias"] = bias
        return cfg_out

    return cfg


def at_position(tile, t):
    return tile[:, :].rearrange("p (b t) -> p t b", t=P)[:, bass.ds(t, 1), :]


def time_loop(eng, step, last):
    with eng.Fori(0, P // 4 - 1) as i:
        for p in range(4):
            step(i * 4 + p, p % 2)
    step(P - 4, 0)
    step(P - 3, 1)
    last(P - 2, 0)
    last(P - 1, 1)


def keep_states(pool, core, h, h_ready, kept):
    def step(t, p):
        pool.wait_ge(h_ready, t + 2)
        pool.tensor_copy(at_position(core.a, t), h[:, p, :].unsqueeze(1)).then_inc(kept, 1)

    time_loop(pool, step, step)


def lstm_stage(core, name, k, next_load=None):
    nc, w, ps, const = core.nc, core.pack(k), core.ps, core.const
    with stage_scope(nc) as ctx:
        sb = lambda n, shape: ctx.enter_context(nc.sbuf_tensor(f"{name}_{n}", shape, F32))
        sem = lambda n: nc.alloc_semaphore(f"{name}_{n}")
        h = sb("h", [P, 2, NB])
        sig = sb("sig", [P, 2, 3, NB])
        cand = sb("cand", [P, 2, NB])
        c = sb("c", [P, NB])
        ic = sb("ic", [P, NB])
        fc = sb("fc", [P, NB])
        tc = sb("tc", [P, 2, NB])
        z_done, sig_ready, cand_ready, c_ready, tc_ready, h_ready, kept, parts, c_set = map(
            sem, ["z_done", "sig_ready", "cand_ready", "c_ready", "tc_ready", "h_ready", "kept", "parts", "c_set"])
        block = ctx.enter_context(nc.Block())

        @block.sync
        def _(sp):
            if next_load is not None:
                next_load(sp)

        @block.gpsimd
        def _(pool):
            keep_states(pool, core, h, h_ready, kept)

        @block.tensor
        def _(pe):
            wait_pack(pe, core, k)

            def pre(t, p):
                past(pe, cand_ready, t - 1)
                pe.matmul(ps[:, p, 0:P], w("b", rows=4), const("gate_pick", rows=4), start=True, stop=False,
                          skip_group_check=True)
                for g in range(4):
                    pe.matmul(ps[:, p, g * NB:(g + 1) * NB], w("Wx", g * P, P), at_position(core.x, t),
                              start=False, stop=False, skip_group_check=True)

            def rec(t, p):
                pe.wait_ge(h_ready, t + 1)
                for g in range(4):
                    last = pe.matmul(ps[:, p, g * NB:(g + 1) * NB], w("Wh", g * P, P), h[:, 1 - p, :],
                                     start=False, stop=True, skip_group_check=True)
                last.then_inc(z_done, 1)

            pre(0, 0)
            pre(1, 1)
            rec(0, 0)

            def step(t, p):
                pre(t, p)
                rec(t - 1, 1 - p)

            with pe.Fori(0, P // 4 - 1) as i:
                for p in range(4):
                    step(i * 4 + (p + 2), p % 2)
            step(P - 2, 0)
            step(P - 1, 1)
            rec(P - 1, 1)

        @block.scalar
        def _(act):
            def step(t, p):
                act.wait_ge(z_done, t + 1)
                act.activation(sig[:, p, :, :], ps[:, p, 0:3 * NB].rearrange("p (g b) -> p g b", g=3),
                               ACT.Sigmoid).then_inc(sig_ready, 1)
                act.activation(cand[:, p, :], ps[:, p, 3 * NB:4 * NB], ACT.Tanh).then_inc(cand_ready, 1)
                act.wait_ge(c_ready, t + 1)
                act.activation(tc[:, p, :], c[:, :], ACT.Tanh).then_inc(tc_ready, 1)

            time_loop(act, step, step)

        @block.vector
        def _(dve):
            dve.tensor_copy(h[:, 1, :], const("cond")).then_inc(h_ready, 1)
            dve.memset(c[:, :], 0.0).then_inc(c_set, 1)
            dve.wait_ge(c_set, 1)

            def step(t, p):
                dve.wait_ge(sig_ready, t + 1)
                past(dve, c_ready, t)
                dve.tensor_tensor(fc[:, :], c[:, :], sig[:, p, 1, :], ALU.mult).then_inc(parts, 1)
                dve.wait_ge(cand_ready, t + 1)
                dve.tensor_tensor(ic[:, :], cand[:, p, :], sig[:, p, 0, :], ALU.mult).then_inc(parts, 1)
                dve.wait_ge(parts, t * 2 + 2)
                past(dve, tc_ready, t)
                dve.tensor_tensor(c[:, :], fc[:, :], ic[:, :], ALU.add).then_inc(c_ready, 1)
                dve.wait_ge(tc_ready, t + 1)
                past(dve, kept, t - 1)
                dve.tensor_tensor(h[:, p, :], tc[:, p, :], sig[:, p, 2, :], ALU.mult).then_inc(h_ready, 1)

            step(0, 0)
            step(1, 1)
            with dve.Fori(0, P // 4 - 1) as i:
                for p in range(4):
                    step(i * 4 + (p + 2), p % 2)
            step(P - 2, 0)
            step(P - 1, 1)


def leaky_stage(core, next_load=None):
    nc, w, ps, const = core.nc, core.pack(1), core.ps, core.const
    with stage_scope(nc) as ctx:
        sb = lambda n, shape: ctx.enter_context(nc.sbuf_tensor(f"leaky_{n}", shape, F32))
        sem = lambda n: nc.alloc_semaphore(f"leaky_{n}")
        h = sb("h", [P, 2, NB])
        gate = sb("gate", [P, 2, NB])
        gz = sb("gz", [P, NB])
        pre_act = sb("pre_act", [P, 2, NB])
        leak = sb("leak", [P, 1])
        z_done, gate_ready, gz_ready, mixed, h_ready, kept, leak_ready = map(
            sem, ["z_done", "gate_ready", "gz_ready", "mixed", "h_ready", "kept", "leak_ready"])
        block = ctx.enter_context(nc.Block())

        @block.sync
        def _(sp):
            if next_load is not None:
                next_load(sp)

        @block.gpsimd
        def _(pool):
            keep_states(pool, core, h, h_ready, kept)

        @block.tensor
        def _(pe):
            wait_pack(pe, core, 1)

            def pre(t, p):
                past(pe, gate_ready, t - 1)
                pe.matmul(ps[:, p, 0:NB], w("WzT"), at_position(core.x, t), start=True, stop=False)

            def rec(t, p):
                pe.wait_ge(h_ready, t + 1)
                pe.matmul(ps[:, p, 0:NB], w("WhT"), h[:, 1 - p, :], start=False, stop=True).then_inc(z_done, 1)

            pre(0, 0)
            pre(1, 1)
            rec(0, 0)
            with pe.Fori(0, P // 4 - 1) as i:
                for p in range(4):
                    pre(i * 4 + (p + 2), p % 2)
                    rec(i * 4 + (p + 1), 1 - p % 2)
            pre(P - 2, 0)
            rec(P - 3, 1)
            pre(P - 1, 1)
            rec(P - 2, 0)
            rec(P - 1, 1)

        @block.scalar
        def _(act):
            wait_pack(act, core, 1)
            act.activation(h[:, 1, :], const("cond"), ACT.Copy).then_inc(h_ready, 1)

            def step(t, p):
                act.wait_ge(z_done, t + 1)
                act.activation(gate[:, p, :], ps[:, p, 0:NB], ACT.Sigmoid, bias=w("b")).then_inc(gate_ready, 1)
                act.wait_ge(mixed, t + 1)
                past(act, kept, t - 1)
                act.activation(h[:, p, :], pre_act[:, p, :], ACT.Tanh).then_inc(h_ready, 1)

            step(0, 0)
            step(1, 1)
            with act.Fori(0, P // 4 - 1) as i:
                for p in range(4):
                    step(i * 4 + (p + 2), p % 2)
            step(P - 2, 0)
            step(P - 1, 1)

        @block.vector
        def _(dve):
            wait_pack(dve, core, 1)
            dve.tensor_scalar(leak[:, :], w("alpha"), -1.0, 1.0, ALU.mult, ALU.add).then_inc(leak_ready, 1)
            dve.wait_ge(leak_ready, 1)

            def step(t, p):
                dve.wait_ge(gate_ready, t + 1)
                past(dve, mixed, t)
                dve.tensor_tensor(gz[:, :].unsqueeze(1), gate[:, p, :].unsqueeze(1), at_position(core.x, t),
                                  ALU.mult).then_inc(gz_ready, 1)
                dve.wait_ge(gz_ready, t + 1)
                dve.wait_ge(h_ready, t + 1)
                dve.scalar_tensor_tensor(out=pre_act[:, p, :], in0=h[:, 1 - p, :], scalar=leak[:, :], in1=gz[:, :],
                                         op0=ALU.mult, op1=ALU.add).then_inc(mixed, 1)

            step(0, 0)
            step(1, 1)
            with dve.Fori(0, P // 4 - 1) as i:
                for p in range(4):
                    step(i * 4 + (p + 2), p % 2)
            step(P - 2, 0)
            step(P - 1, 1)


def gru_stage(core, next_load=None):
    nc, w, ps, const = core.nc, core.pack(5), core.ps, core.const
    with stage_scope(nc) as ctx:
        sb = lambda n, shape: ctx.enter_context(nc.sbuf_tensor(f"gru_{n}", shape, F32))
        sem = lambda n: nc.alloc_semaphore(f"gru_{n}")
        h = sb("h", [P, 2, NB])
        r = sb("r", [P, NB])
        z = sb("z", [P, NB])
        rh = sb("rh", [P, NB])
        cand = sb("cand", [P, NB])
        diff = sb("diff", [P, NB])
        (r_done, z_done, cand_done, r_ready, z_ready, rh_ready, cand_ready, diff_ready, h_ready, kept) = map(
            sem, ["r_done", "z_done", "cand_done", "r_ready", "z_ready", "rh_ready", "cand_ready", "diff_ready",
                  "h_ready", "kept"])
        block = ctx.enter_context(nc.Block())

        @block.sync
        def _(sp):
            if next_load is not None:
                next_load(sp)

        @block.gpsimd
        def _(pool):
            keep_states(pool, core, h, h_ready, kept)

        @block.tensor
        def _(pe):
            wait_pack(pe, core, 5)

            def pre(t, p):
                past(pe, cand_ready, t - 1)
                for bank, x_w, c_w in ((p, "Wr", "Cr"), (2 + p, "Wz", "Cz"), (4 + p, "W", "C")):
                    pe.matmul(ps[:, bank, 0:NB], w(c_w), const("cond"), start=True, stop=False)
                    pe.matmul(ps[:, bank, 0:NB], w(x_w), at_position(core.x, t), start=False, stop=False)

            def gates(t, p):
                pe.wait_ge(h_ready, t + 1)
                pe.matmul(ps[:, p, 0:NB], w("Ur"), h[:, 1 - p, :], start=False, stop=True).then_inc(r_done, 1)
                pe.matmul(ps[:, 2 + p, 0:NB], w("Uz"), h[:, 1 - p, :], start=False, stop=True).then_inc(z_done, 1)

            def candidate(t, p):
                pe.wait_ge(rh_ready, t + 1)
                pe.matmul(ps[:, 4 + p, 0:NB], w("U"), rh[:, :], start=False, stop=True).then_inc(cand_done, 1)

            def step(t, p):
                pre(t, p)
                gates(t - 1, 1 - p)
                candidate(t - 1, 1 - p)

            pre(0, 0)
            step(1, 1)
            with pe.Fori(0, P // 4 - 1) as i:
                for p in range(4):
                    step(i * 4 + (p + 2), p % 2)
            step(P - 2, 0)
            step(P - 1, 1)
            gates(P - 1, 1)
            candidate(P - 1, 1)

        @block.scalar
        def _(act):
            wait_pack(act, core, 5)

            def step(t, p):
                act.wait_ge(r_done, t + 1)
                act.activation(r[:, :], ps[:, p, 0:NB], ACT.Sigmoid, bias=w("br")).then_inc(r_ready, 1)
                act.wait_ge(z_done, t + 1)
                act.activation(z[:, :], ps[:, 2 + p, 0:NB], ACT.Sigmoid, bias=w("bz")).then_inc(z_ready, 1)
                act.wait_ge(cand_done, t + 1)
                act.activation(cand[:, :], ps[:, 4 + p, 0:NB], ACT.Tanh, bias=w("b")).then_inc(cand_ready, 1)

            step(0, 0)
            step(1, 1)
            with act.Fori(0, P // 4 - 1) as i:
                for p in range(4):
                    step(i * 4 + (p + 2), p % 2)
            step(P - 2, 0)
            step(P - 1, 1)

        @block.vector
        def _(dve):
            dve.memset(h[:, 1, :], 0.0).then_inc(h_ready, 1)

            def step(t, p):
                dve.wait_ge(r_ready, t + 1)
                dve.wait_ge(h_ready, t + 1)
                dve.tensor_tensor(rh[:, :], r[:, :], h[:, 1 - p, :], ALU.mult).then_inc(rh_ready, 1)
                dve.wait_ge(cand_ready, t + 1)
                dve.tensor_tensor(diff[:, :], cand[:, :], h[:, 1 - p, :], ALU.subtract).then_inc(diff_ready, 1)
                dve.wait_ge(diff_ready, t * 2 + 1)
                dve.tensor_tensor(diff[:, :], diff[:, :], z[:, :], ALU.mult).then_inc(diff_ready, 1)
                dve.wait_ge(diff_ready, t * 2 + 2)
                past(dve, kept, t - 1)
                dve.tensor_tensor(h[:, p, :], diff[:, :], h[:, 1 - p, :], ALU.add).then_inc(h_ready, 1)

            step(0, 0)
            step(1, 1)
            with dve.Fori(0, P // 4 - 1) as i:
                for p in range(4):
                    step(i * 4 + (p + 2), p % 2)
            step(P - 2, 0)
            step(P - 1, 1)


def norm_stage(core, name, k, src, dst, m, lhs, mean, eps, gamma=None, beta=None, add_to=None, prepare=None):
    nc, ps, const = core.nc, core.ps, core.const
    with stage_scope(nc) as ctx:
        sb = lambda n, shape: ctx.enter_context(nc.sbuf_tensor(f"{name}_{n}", shape, F32))
        sem = lambda n: nc.alloc_semaphore(f"{name}_{n}")
        xc = sb("centred", [m, 2, CHUNK])
        sq = sb("square", [m, 2, CHUNK])
        sd = sb("deviation", [m, 2, CHUNK])
        inv = sb("inverse", [m, 2, CHUNK])
        s = {n: sem(n) for n in ["centred_done", "centred_ready", "square_ready", "var_done", "sd_ready", "inv_ready",
                                 "norm_ready", "scaled", "written", "prepared"]}
        block = ctx.enter_context(nc.Block())

        def pairs(eng, one):
            one(0, 0)
            one(1, 1)
            with eng.Fori(1, NCHUNK // 2) as i:
                one(i * 2, 0)
                one(i * 2 + 1, 1)

        @block.tensor
        def _(pe):
            wait_pack(pe, core, k)
            if prepare is not None:
                prepare["pe"](pe, s)

            def centre(c, p):
                past(pe, s["centred_ready"], c - 1)
                pe.matmul(ps[0:m, p, :], lhs, src[:, tok(c * CHUNK, CHUNK)], start=True, stop=True).then_inc(
                    s["centred_done"], 1)

            def variance(c, p):
                pe.wait_ge(s["square_ready"], c + 1)
                past(pe, s["sd_ready"], c - 1)
                pe.matmul(ps[:, 2 + p, :], mean, sq[:, p, :], start=True, stop=True).then_inc(s["var_done"], 1)

            def two(c):
                centre(c, 0)
                centre(c + 1, 1)
                variance(c, 0)
                variance(c + 1, 1)

            two(0)
            with pe.Fori(1, NCHUNK // 2) as i:
                two(i * 2)

        @block.scalar
        def _(act):
            if prepare is not None:
                prepare["act"](act, s)

            def two(c):
                for p in range(2):
                    act.wait_ge(s["centred_done"], c + p + 1)
                    past(act, s["norm_ready"], c + p - 1)
                    act.activation(xc[:, p, :], ps[0:m, p, :], ACT.Copy).then_inc(s["centred_ready"], 1)
                for p in range(2):
                    act.wait_ge(s["var_done"], c + p + 1)
                    past(act, s["inv_ready"], c + p - 1)
                    act.activation(sd[:, p, :], ps[0:m, 2 + p, :], ACT.Sqrt, bias=eps[0:m, :]).then_inc(
                        s["sd_ready"], 1)

            two(0)
            with act.Fori(1, NCHUNK // 2) as i:
                two(i * 2)

        @block.gpsimd
        def _(pool):
            def one(c, p):
                pool.wait_ge(s["centred_ready"], c + 1)
                past(pool, s["var_done"], c - 1)
                pool.tensor_tensor(sq[:, p, :], xc[:, p, :], xc[:, p, :], ALU.mult).then_inc(s["square_ready"], 1)

            pairs(pool, one)

        @block.vector
        def _(dve):
            def one(c, p):
                dve.wait_ge(s["sd_ready"], c + 1)
                past(dve, s["norm_ready"], c - 1)
                dve.reciprocal(inv[:, p, :], sd[:, p, :]).then_inc(s["inv_ready"], 1)
                dve.wait_ge(s["inv_ready"], c + 1)
                if gamma is None:
                    dve.tensor_tensor(dst[0:m, tok(c * CHUNK, CHUNK)], xc[:, p, :], inv[:, p, :],
                                      ALU.mult).then_inc(s["norm_ready"], 1)
                    return
                dve.scalar_tensor_tensor(out=xc[:, p, :], in0=xc[:, p, :], scalar=gamma, in1=inv[:, p, :],
                                         op0=ALU.mult, op1=ALU.mult).then_inc(s["scaled"], 1)
                dve.wait_ge(s["scaled"], c + 1)
                out = dst[0:m, tok(c * CHUNK, CHUNK)]
                if add_to is None:
                    dve.tensor_scalar(out, xc[:, p, :], beta, None, ALU.add).then_inc(s["norm_ready"], 1)
                else:
                    dve.scalar_tensor_tensor(out=out, in0=xc[:, p, :], scalar=beta,
                                             in1=add_to[0:m, tok(c * CHUNK, CHUNK)], op0=ALU.add,
                                             op1=ALU.add).then_inc(s["norm_ready"], 1)

            pairs(dve, one)


class Chain:

    def __init__(self, dve, sem):
        self.dve, self.sem, self.n = dve, sem, 0

    def __call__(self, ins):
        self.n += 1
        ins.then_inc(self.sem, 1)
        self.dve.wait_ge(self.sem, self.n)


def pick_first_best(dve, link, values, tie, ne, best, hot, n=NB):
    link(dve.tensor_reduce(best, values, AX_X, ALU.max))
    link(dve.tensor_tensor(hot, values, best.unsqueeze(2).broadcast_to([P, n, ne]), ALU.is_equal))
    link(dve.tensor_tensor(hot, hot, tie.unsqueeze(1).broadcast_to([P, n, ne]), ALU.mult))
    link(dve.tensor_reduce(best, hot, AX_X, ALU.max))
    link(dve.tensor_tensor(hot, hot, best.unsqueeze(2).broadcast_to([P, n, ne]), ALU.is_equal))


def router_stage(core, name, k, src, ne, router, gate_fn, gates, extra=None, act_fn=None, pe_first=None, next_load=None):
    nc, ps = core.nc, core.ps
    with stage_scope(nc) as ctx:
        sb = lambda n, shape: ctx.enter_context(nc.sbuf_tensor(f"{name}_{n}", shape, F32))
        sem = lambda n: nc.alloc_semaphore(f"{name}_{n}")
        logits_done, own, act_done, dve_ready = map(sem, ["logits_done", "own", "act_done", "dve_ready"])
        bufs = extra(sb, sem) if extra is not None else {}
        block = ctx.enter_context(nc.Block())

        @block.sync
        def _(sp):
            if next_load is not None:
                next_load(sp)

        @block.gpsimd
        def _(pool):
            if "pool" in bufs:
                bufs["pool"](pool)

        @block.tensor
        def _(pe):
            wait_pack(pe, core, k)
            rhs = router(bufs)
            if pe_first is not None:
                pe_first(pe, bufs)
            for t in range(NB):
                out = ps[:, 0, t * ne:(t + 1) * ne]
                more = "second" in bufs
                last = pe.matmul(out, src[:, t * P:(t + 1) * P], rhs, start=True, stop=not more)
                if more:
                    last = pe.matmul(out, core.b[:, t * P:(t + 1) * P], bufs["second"], start=False, stop=True)
            last.then_inc(logits_done, 1)

        @block.scalar
        def _(act):
            if act_fn is not None:
                act_fn(act, ps, logits_done, act_done, dve_ready, bufs)

        @block.vector
        def _(dve):
            wait_pack(dve, core, k)
            link = Chain(dve, own)
            logits = ps[:, 0, 0:NB * ne].rearrange("p (t e) -> p t e", e=ne)
            gate_fn(dve, link, logits, gates, logits_done, act_done, dve_ready, bufs, sb)


def expert_stage(core, name, k, ne, gates, hidden, out_rhs, depth, rows_of, b2=None, shared=None, finish=None,
                 next_load=None, setup=None, n_hidden=None):
    nc, ps, const = core.nc, core.ps, core.const
    nj = n_hidden
    slots = 2 * max(depth, 1) if depth > 1 else 3
    with stage_scope(nc) as ctx:
        sb = lambda n, shape: ctx.enter_context(nc.sbuf_tensor(f"{name}_{n}", shape, F32))
        sem = lambda n: nc.alloc_semaphore(f"{name}_{n}")
        hs = sb("hidden", [P, slots, CHUNK])
        acc = sb("acc", [P, 4, P])
        g = sb("gate", [P, 4, ne])
        gt = sb("gate_turned", [ne, 4, P])
        s = {n: sem(n) for n in ["g_ready", "gt_done", "gt_ready", "init_done", "h_done", "h_ready", "y_done",
                                 "y_added", "sum_turned", "stored", "used"]}
        bufs = setup(sb, sem, s) if setup is not None else {}
        block = ctx.enter_context(nc.Block())

        def chunks(eng, one):
            one(0)
            with eng.Fori(1, NCHUNK) as c:
                one(c)

        first_tile = lambda e: rows_of(e)[0]

        @block.sync
        def _(sp):
            if next_load is not None:
                next_load(sp)

        @block.gpsimd
        def _(pool):
            def one(c):
                past(pool, s["y_added"], c * ne)
                pool.tensor_copy(g[:, :, :], gates[:, bass.ds(c * 4, 4), :]).then_inc(s["g_ready"], 1)
                if "pool" in hidden:
                    hidden["pool"](pool, c, bufs)

            chunks(pool, one)

        @block.tensor
        def _(pe):
            wait_pack(pe, core, k)

            def hidden_tile(c, j):
                if "pe" not in hidden:
                    return
                past(pe, s["h_ready"], c * nj + (j - 1))
                hidden["pe"](pe, c, j, j % 2, bufs).then_inc(s["h_done"], 1)

            def one(c):
                if "pe_first" in hidden:
                    hidden["pe_first"](pe, c, bufs)
                if b2 is not None:
                    pe.wait_ge(s["g_ready"], c + 1)
                    past(pe, s["stored"], c)
                    for t in range(4):
                        last = pe.transpose(ps[0:ne, 4, t * P:(t + 1) * P], g[:, t, :], const("ident"))
                    last.then_inc(s["gt_done"], 1)
                    pe.wait_ge(s["gt_ready"], c + 1)
                    past(pe, s["used"], c)
                    for t in range(4):
                        last = pe.matmul(ps[:, 5, t * P:(t + 1) * P], gt[:, t, :], b2, start=True, stop=True)
                    last.then_inc(s["init_done"], 1)
                else:
                    past(pe, s["used"], c)
                    shared["pe"](pe, c, bufs).then_inc(s["init_done"], 1)
                sent = 0
                for e in range(ne):
                    tile, lo, n = rows_of(e)
                    ahead = min(nj, tile + 2 * depth) if depth > 1 else min(nj, tile + 2)
                    while sent < ahead:
                        hidden_tile(c, sent)
                        sent += 1
                    past(pe, s["y_added"], c * ne + (e - 1))
                    pe.wait_ge(s["h_ready"], c * nj + (tile + depth))
                    for t in range(4):
                        for f in range(depth):
                            last = pe.matmul(ps[:, 2 + e % 2, t * P:(t + 1) * P],
                                             hs[lo:lo + n, (tile + f) % slots, t * P:(t + 1) * P],
                                             out_rhs(e, f, lo, n), start=(f == 0), stop=(f == depth - 1))
                    last.then_inc(s["y_done"], 1)
                pe.wait_ge(s["y_added"], c * ne + ne)
                past(pe, s["stored"], c)
                for t in range(4):
                    last = pe.transpose(ps[:, 4, t * P:(t + 1) * P], acc[:, t, :], const("ident"))
                last.then_inc(s["sum_turned"], 1)

            chunks(pe, one)

        @block.scalar
        def _(act):
            wait_pack(act, core, k)
            users = [max([e for e in range(ne) if first_tile(e) <= j < first_tile(e) + depth]) for j in range(nj)]

            def one(c):
                if "act_first" in hidden:
                    hidden["act_first"](act, c, bufs)
                if b2 is not None:
                    act.wait_ge(s["gt_done"], c + 1)
                    past(act, s["init_done"], c)
                    act.activation(gt[:, :, :], ps[0:ne, 4, :].rearrange("p (t j) -> p t j", t=4),
                                   ACT.Copy).then_inc(s["gt_ready"], 1)
                for j in range(nj):
                    if "pe" in hidden:
                        act.wait_ge(s["h_done"], c * nj + (j + 1))
                    if j >= slots:
                        act.wait_ge(s["y_done"], c * ne + (users[j - slots] + 1))
                    else:
                        past(act, s["y_done"], c * ne)
                    hidden["act"](act, c, j, j % 2, hs[:, j % slots, :], bufs).then_inc(s["h_ready"], 1)

            chunks(act, one)

        @block.vector
        def _(dve):
            wait_pack(dve, core, k)

            def one(c):
                if "dve_first" in hidden:
                    hidden["dve_first"](dve, c, bufs)
                dve.wait_ge(s["init_done"], c + 1)
                past(dve, s["sum_turned"], c)
                dve.tensor_copy(acc[:, :, :], ps[:, 5, :].rearrange("p (t j) -> p t j", t=4)).then_inc(s["used"], 1)
                dve.wait_ge(s["g_ready"], c + 1)
                for e in range(ne):
                    dve.wait_ge(s["y_done"], c * ne + (e + 1))
                    dve.wait_ge(s["used"], c + 1)
                    past(dve, s["y_added"], c * ne + e)
                    for t in range(4):
                        last = dve.scalar_tensor_tensor(out=acc[:, t, :], in0=ps[:, 2 + e % 2, t * P:(t + 1) * P],
                                                        scalar=g[:, t, e:e + 1], in1=acc[:, t, :], op0=ALU.mult,
                                                        op1=ALU.add)
                    last.then_inc(s["y_added"], 1)
                dve.wait_ge(s["sum_turned"], c + 1)
                finish(dve, c, ps[:, 4, :]).then_inc(s["stored"], 1)

            chunks(dve, one)


def layer0_gates(core):
    def extra(sb, sem):
        return dict(lg=sb("scores", [P, NB, 8]), best=sb("best", [P, NB]))

    def gate_fn(dve, link, logits, gates, logits_done, act_done, dve_ready, bufs, sb):
        dve.wait_ge(logits_done, 1)
        link(dve.tensor_copy(bufs["lg"][:, :, :], logits))
        pick_first_best(dve, link, bufs["lg"][:, :, :], core.const("tie8"), 8, bufs["best"][:, :], gates)

    return extra, gate_fn


def layer0_experts(core):
    w, ps = core.pack(1), core.ps

    def setup(sb, sem, s):
        return dict(w1=sb("w1_scaled", [P, 256]), b1=sb("b1_full", [P, 2]), folded=sem("folded"), shifted=sem("shifted"))

    def pe_first(pe, c, bufs):
        if isinstance(c, int):
            for e in range(8):
                lo = 32 * (e % 4)
                last = pe.matmul(ps[lo:lo + 32, 7, e // 4:e // 4 + 1], w("W1", e * 32, 32),
                                 w("ln_bias", e, 1), start=True, stop=True)
            last.then_inc(bufs["shifted"], 1)
            pe.wait_ge(bufs["folded"], 9)

    def dve_first(dve, c, bufs):
        if isinstance(c, int):
            for e in range(8):
                dve.tensor_scalar(bufs["w1"][:, e * 32:(e + 1) * 32], w("W1", e * 32, 32), w("ln_scale", e, 1), None,
                                  ALU.mult).then_inc(bufs["folded"], 1)
            dve.wait_ge(bufs["shifted"], 1)
            dve.tensor_tensor(bufs["b1"][:, :], ps[:, 7, 0:2], w("b1"), ALU.add).then_inc(bufs["folded"], 1)

    def pe(pe, c, j, bank, bufs):
        return pe.matmul(ps[:, bank, :], bufs["w1"][:, j * P:(j + 1) * P], core.b[:, tok(c * CHUNK, CHUNK)],
                         start=True, stop=True)

    def act_first(act, c, bufs):
        if isinstance(c, int):
            act.wait_ge(bufs["folded"], 9)

    def act(act, c, j, bank, out, bufs):
        return act.activation(out, ps[:, bank, :], ACT.Gelu, bias=bufs["b1"][:, j:j + 1])

    hidden = dict(pe=pe, act=act, pe_first=pe_first, dve_first=dve_first, act_first=act_first)
    return setup, hidden


def add_to_x(core):
    def finish(dve, c, bank):
        xs = core.x[:, tok(c * CHUNK, CHUNK)]
        return dve.tensor_tensor(xs, bank, xs, ALU.add)

    return finish


def two_best(dve, link, core, values, work, tie, ne, best, hot, hot2):
    pick_first_best(dve, link, values, tie, ne, best, hot)
    link(dve.scalar_tensor_tensor(out=work, in0=hot, scalar=-1.0e30, in1=values, op0=ALU.mult, op1=ALU.add))
    pick_first_best(dve, link, work, tie, ne, best, hot2)
    link(dve.tensor_tensor(hot, hot, hot2, ALU.add))


def layer1_gates(core):
    w = core.pack(3)

    def extra(sb, sem):
        return dict(lg=sb("scores", [P, NB, 16]), best=sb("best", [P, NB]), work=sb("work", [P, NB, 16]),
                    hot=sb("hot", [P, NB, 16]), hot2=sb("hot2", [P, NB, 16]))

    def act_fn(act, ps, logits_done, act_done, dve_ready, bufs):
        act.wait_ge(dve_ready, 1)
        act.activation(bufs["lg"][:, :, :], bufs["lg"][:, :, :], ACT.Exp).then_inc(act_done, 1)

    def gate_fn(dve, link, logits, gates, logits_done, act_done, dve_ready, bufs, sb):
        lg, best, work, hot, hot2 = (bufs[n] for n in ("lg", "best", "work", "hot", "hot2"))
        wide = lambda: best[:, :].unsqueeze(2).broadcast_to([P, NB, 16])
        dve.wait_ge(logits_done, 1)
        link(dve.tensor_tensor(lg[:, :, :], logits, w("br").unsqueeze(1).broadcast_to([P, NB, 16]), ALU.add))
        link(dve.tensor_reduce(best[:, :], lg[:, :, :], AX_X, ALU.max))
        dve.tensor_tensor(lg[:, :, :], lg[:, :, :], wide(), ALU.subtract).then_inc(dve_ready, 1)
        dve.wait_ge(act_done, 1)
        link(dve.tensor_reduce(best[:, :], lg[:, :, :], AX_X, ALU.add))
        link(dve.reciprocal(best[:, :], best[:, :]))
        link(dve.tensor_tensor(lg[:, :, :], lg[:, :, :], wide(), ALU.mult))
        two_best(dve, link, core, lg[:, :, :], work[:, :, :], core.const("tie16"), 16, best[:, :], hot[:, :, :],
                 hot2[:, :, :])
        link(dve.tensor_tensor(gates, lg[:, :, :], hot[:, :, :], ALU.mult))
        link(dve.tensor_reduce(best[:, :], gates, AX_X, ALU.add))
        link(dve.tensor_scalar(best[:, :], best[:, :], 1.0e-9, None, ALU.max))
        link(dve.reciprocal(best[:, :], best[:, :]))
        link(dve.tensor_tensor(gates, gates, wide(), ALU.mult))

    return extra, gate_fn, act_fn


def layer1_experts(core):
    w, ps, const = core.pack(3), core.ps, core.const
    NE = 16

    def setup(sb, sem, s):
        b = dict(w1=sb("w1_centred", [P, NE * P]), b1=sb("b1_centred", [P, NE]), u=sb("units", [P, NE, CHUNK]),
                 sq=sb("square", [P, 2, CHUNK]), sd=sb("deviation", [P, 2, CHUNK]), inv=sb("inverse", [P, 2, CHUNK]))
        for n in ["fold_done", "folded", "centred_done", "centred_ready", "square_ready", "var_done", "sd_ready",
                  "inv_ready", "unit_ready"]:
            b[n] = sem(n)
        b["s"] = s
        return b

    def pe_first(pe, c, b):
        if isinstance(c, int):
            for e in range(NE):
                past(pe, b["folded"], e - 1)
                pe.matmul(ps[:, 6 + e % 2, 0:P], w("W1T", e * P, P), const("center"), start=True,
                          stop=True).then_inc(b["fold_done"], 1)
            pe.wait_ge(b["folded"], NE - 1)
            pe.matmul(ps[:, 6, 0:NE], const("center"), w("b1"), start=True, stop=True).then_inc(b["fold_done"], 1)
            pe.wait_ge(b["folded"], NE + 1)

        def centre(e):
            past(pe, b["centred_ready"], c * NE + (e - 1))
            pe.matmul(ps[:, 6 + e % 2, :], b["w1"][:, e * P:(e + 1) * P], core.a[:, tok(c * CHUNK, CHUNK)],
                      start=True, stop=True).then_inc(b["centred_done"], 1)

        def variance(e):
            pe.wait_ge(b["square_ready"], c * NE + (e + 1))
            past(pe, b["sd_ready"], c * NE + (e - 1))
            pe.matmul(ps[:, e % 2, :], const("mean"), b["sq"][:, e % 2, :], start=True, stop=True).then_inc(
                b["var_done"], 1)

        centre(0)
        centre(1)
        for e in range(NE):
            if e + 2 < NE:
                centre(e + 2)
            variance(e)

    def act_first(act, c, b):
        def centred(e):
            act.wait_ge(b["centred_done"], c * NE + (e + 1))
            past(act, b["s"]["h_ready"], c * NE - (NE - 1 - e))
            act.activation(b["u"][:, e, :], ps[:, 6 + e % 2, :], ACT.Identity, bias=b["b1"][:, e:e + 1]).then_inc(
                b["centred_ready"], 1)

        def deviation(e):
            act.wait_ge(b["var_done"], c * NE + (e + 1))
            past(act, b["inv_ready"], c * NE + (e - 1))
            act.activation(b["sd"][:, e % 2, :], ps[:, e % 2, :], ACT.Sqrt, bias=const("eps5")).then_inc(
                b["sd_ready"], 1)

        if isinstance(c, int):
            act.wait_ge(b["folded"], NE + 1)
        centred(0)
        centred(1)
        for e in range(NE):
            if e + 2 < NE:
                centred(e + 2)
            deviation(e)

    def pool(pool, c, b):
        for e in range(NE):
            pool.wait_ge(b["centred_ready"], c * NE + (e + 1))
            past(pool, b["var_done"], c * NE + (e - 1))
            pool.tensor_tensor(b["sq"][:, e % 2, :], b["u"][:, e, :], b["u"][:, e, :], ALU.mult).then_inc(
                b["square_ready"], 1)

    def dve_first(dve, c, b):
        if isinstance(c, int):
            for e in range(NE):
                dve.wait_ge(b["fold_done"], e + 1)
                dve.tensor_copy(b["w1"][:, e * P:(e + 1) * P], ps[:, 6 + e % 2, 0:P]).then_inc(b["folded"], 1)
            dve.wait_ge(b["fold_done"], NE + 1)
            dve.tensor_copy(b["b1"][:, :], ps[:, 6, 0:NE]).then_inc(b["folded"], 1)
        for e in range(NE):
            dve.wait_ge(b["sd_ready"], c * NE + (e + 1))
            past(dve, b["unit_ready"], c * NE + (e - 1))
            dve.reciprocal(b["inv"][:, e % 2, :], b["sd"][:, e % 2, :]).then_inc(b["inv_ready"], 1)
            dve.wait_ge(b["inv_ready"], c * NE + (e + 1))
            dve.tensor_tensor(b["u"][:, e, :], b["u"][:, e, :], b["inv"][:, e % 2, :], ALU.mult).then_inc(
                b["unit_ready"], 1)

    def act(act, c, j, bank, out, b):
        act.wait_ge(b["unit_ready"], c * NE + (j + 1))
        return act.activation(out, b["u"][:, j, :], ACT.Gelu, bias=w("be1", j, 1), scale=w("g1", j, 1))

    return setup, dict(pe_first=pe_first, act_first=act_first, dve_first=dve_first, pool=pool, act=act)


def layer3_gates(core):
    w = core.pack(7)

    def extra(sb, sem):
        b = dict(lg=sb("scores", [P, NB, 8]), best=sb("best", [P, NB]), work=sb("work", [P, NB, 8]),
                 hot=sb("hot", [P, NB, 8]), hot2=sb("hot2", [P, NB, 8]), low=sb("low", [P, NB]),
                 cond_ready=sem("cond_ready"), second=w("rT"))

        def pool(pool):
            pool.tensor_copy(core.b[:, :].rearrange("p (b t) -> p b t", t=P),
                             core.const("cond").unsqueeze(2).broadcast_to([P, NB, P])).then_inc(b["cond_ready"], 1)

        b["pool"] = pool
        return b

    def pe_first(pe, b):
        pe.wait_ge(b["cond_ready"], 1)

    def act_fn(act, ps, logits_done, act_done, dve_ready, b):
        act.wait_ge(logits_done, 1)
        act.activation(b["lg"][:, :, :], ps[:, 0, 0:NB * 8].rearrange("p (t e) -> p t e", e=8),
                       ACT.Sigmoid).then_inc(act_done, 1)

    def gate_fn(dve, link, logits, gates, logits_done, act_done, dve_ready, b, sb):
        lg, best, work, hot, hot2, low = (b[n] for n in ("lg", "best", "work", "hot", "hot2", "low"))
        bc = lambda t: t[:, :].unsqueeze(2).broadcast_to([P, NB, 8])
        dve.wait_ge(act_done, 1)
        link(dve.tensor_tensor(work[:, :, :], lg[:, :, :], w("rbias").unsqueeze(1).broadcast_to([P, NB, 8]), ALU.add))
        two_best(dve, link, core, work[:, :, :], work[:, :, :], core.const("tie8"), 8, best[:, :], hot[:, :, :],
                 hot2[:, :, :])
        link(dve.tensor_tensor(gates, lg[:, :, :], hot[:, :, :], ALU.mult))
        link(dve.tensor_reduce(best[:, :], gates, AX_X, ALU.add))
        link(dve.tensor_scalar(low[:, :], best[:, :], 1.0e-9, 0.5, ALU.is_le, ALU.mult))
        link(dve.tensor_tensor(hot[:, :, :], hot[:, :, :], bc(low), ALU.mult))
        link(dve.tensor_scalar(low[:, :], best[:, :], 1.0e-9, None, ALU.is_gt))
        link(dve.tensor_scalar(best[:, :], best[:, :], 1.0e-9, None, ALU.add))
        link(dve.reciprocal(best[:, :], best[:, :]))
        link(dve.tensor_tensor(best[:, :], best[:, :], low[:, :], ALU.mult))
        link(dve.tensor_tensor(gates, gates, bc(best), ALU.mult))
        link(dve.tensor_tensor(gates, gates, hot[:, :, :], ALU.add))

    return extra, gate_fn, act_fn, pe_first


def layer3_experts(core):
    w, ps = core.pack(7), core.ps

    def setup(sb, sem, s):
        b = dict(gate=sb("shared_gate", [P, 2, CHUNK]), up=sb("shared", [P, 2, CHUNK]))
        for n in ["gate_done", "up_done", "gate_ready", "up_ready"]:
            b[n] = sem(n)
        b["s"] = s
        return b

    def chunk(c):
        return core.x[:, tok(c * CHUNK, CHUNK)]

    def pe_first(pe, c, b):
        for f in range(2):
            past(pe, b["gate_ready"], c * 2 + f)
            pe.matmul(ps[:, 6, :], w("w1", f * P, P), chunk(c), start=True, stop=True).then_inc(b["gate_done"], 1)
            past(pe, b["up_ready"], c * 2 + f)
            pe.matmul(ps[:, 7, :], w("w3", f * P, P), chunk(c), start=True, stop=True).then_inc(b["up_done"], 1)

    def act_first(act, c, b):
        for f in range(2):
            act.wait_ge(b["gate_done"], c * 2 + (f + 1))
            past(act, b["up_ready"], c * 2 + (f - 1))
            act.activation(b["gate"][:, f, :], ps[:, 6, :], ACT.Silu).then_inc(b["gate_ready"], 1)

    def dve_first(dve, c, b):
        for f in range(2):
            dve.wait_ge(b["up_done"], c * 2 + (f + 1))
            dve.wait_ge(b["gate_ready"], c * 2 + (f + 1))
            past(dve, b["s"]["init_done"], c)
            dve.tensor_tensor(b["up"][:, f, :], ps[:, 7, :], b["gate"][:, f, :], ALU.mult).then_inc(b["up_ready"], 1)

    def shared_pe(pe, c, b):
        pe.wait_ge(b["up_ready"], c * 2 + 2)
        for t in range(4):
            for f in range(2):
                last = pe.matmul(ps[:, 5, t * P:(t + 1) * P], b["up"][:, f, t * P:(t + 1) * P], w("w2", f * P, P),
                                 start=(f == 0), stop=(f == 1))
        return last

    def pe(pe, c, j, bank, b):
        return pe.matmul(ps[:, bank, :], w("W1e", j * P, P), chunk(c), start=True, stop=True)

    def act(act, c, j, bank, out, b):
        return act.activation(out, ps[:, bank, :], ACT.Gelu)

    def finish(dve, c, bank):
        return dve.tensor_scalar(core.a[:, tok(c * CHUNK, CHUNK)], bank, 1.0 / 3.0, None, ALU.mult)

    hidden = dict(pe=pe, act=act, pe_first=pe_first, act_first=act_first, dve_first=dve_first)
    return setup, hidden, dict(pe=shared_pe), finish


def cosine_gates(core):
    w, ps, const = core.pack(7), core.ps, core.const

    def extra(sb, sem):
        b = dict(lg=sb("scores", [P, NB, 8]), best=sb("best", [P, NB]), work=sb("work", [P, NB, 8]),
                 hot=sb("hot", [P, NB, 8]), hot2=sb("hot2", [P, NB, 8]), norm=sb("norm", [P, NB]),
                 sq=sb("square", [P, 2, CHUNK]), sn=sb("sim_unit", [8, P]), snt=sb("sim_turned", [P, 8]),
                 ss=sb("sim_sum", [8, 1]), ssq=sb("sim_square", [8, P]), comp=sb("composite", [P, 8]),
                 itemp=sb("inverse_temp", [P, 1]))
        for n in ["sim_sq", "sim_scaled", "sim_turned", "comp_done", "snt_ready", "comp_ready", "proj_done",
                  "proj_read", "sq_summed", "norm_ready"]:
            b[n] = sem(n)
        return b

    def pe_first(pe, b):
        pe.wait_ge(b["sim_scaled"], 1)
        pe.transpose(ps[:, 6, 0:8], b["sn"][:, :], const("ident", 0, 8, rows=8)).then_inc(b["sim_turned"], 1)
        pe.wait_ge(b["snt_ready"], 1)
        pe.matmul(ps[:, 7, 0:8], w("Wp"), b["snt"][:, :], start=True, stop=True).then_inc(b["comp_done"], 1)
        pe.wait_ge(b["comp_ready"], 1)
        for q in range(NB // 4):
            past(pe, b["proj_read"], q - 1)
            for t in range(4):
                tile = core.a[:, (q * 4 + t) * P:(q * 4 + t + 1) * P]
                last = pe.matmul(ps[:, 1 + q % 2, t * P:(t + 1) * P], tile, w("WpT"), start=True, stop=True)
            last.then_inc(b["proj_done"], 1)

    def act_fn(act, ps_, logits_done, act_done, dve_ready, b):
        act.wait_ge(core.loaded["p7"], 32)
        act.activation(b["ssq"][:, :], w("sim", rows=8), ACT.Square).then_inc(b["sim_sq"], 1)
        act.wait_ge(dve_ready, 1)
        act.activation(b["ss"][:, :], b["ss"][:, :], ACT.Sqrt).then_inc(act_done, 1)
        for q in range(NB // 4):
            act.wait_ge(b["proj_done"], q + 1)
            past(act, b["sq_summed"], q - 1)
            act.activation(b["sq"][:, q % 2, :], ps[:, 1 + q % 2, :], ACT.Square).then_inc(b["proj_read"], 1)
        act.wait_ge(b["sq_summed"], NB // 4)
        act.activation(b["norm"][:, :], b["norm"][:, :], ACT.Sqrt).then_inc(b["norm_ready"], 1)
        act.wait_ge(dve_ready, 2)
        act.activation(b["work"][:, :, :], b["work"][:, :, :], ACT.Exp).then_inc(act_done, 1)

    def gate_fn(dve, link, logits, gates, logits_done, act_done, dve_ready, b, sb):
        lg, best, work, hot, hot2 = (b[n] for n in ("lg", "best", "work", "hot", "hot2"))
        bc = lambda t: t[:, :].unsqueeze(2).broadcast_to([P, NB, 8])
        dve.wait_ge(b["sim_sq"], 1)
        dve.tensor_reduce(b["ss"][:, :], b["ssq"][:, :], AX_X, ALU.add).then_inc(dve_ready, 1)
        link(dve.reciprocal(b["itemp"][:, :], w("temp")))
        dve.wait_ge(act_done, 1)
        link(dve.tensor_scalar(b["ss"][:, :], b["ss"][:, :], 1.0e-12, None, ALU.max))
        link(dve.reciprocal(b["ss"][:, :], b["ss"][:, :]))
        dve.tensor_scalar(b["sn"][:, :], w("sim", rows=8), b["ss"][:, :], None, ALU.mult).then_inc(b["sim_scaled"], 1)
        dve.wait_ge(b["sim_turned"], 1)
        dve.tensor_copy(b["snt"][:, :], ps[:, 6, 0:8]).then_inc(b["snt_ready"], 1)
        dve.wait_ge(b["comp_done"], 1)
        dve.tensor_copy(b["comp"][:, :], ps[:, 7, 0:8]).then_inc(b["comp_ready"], 1)
        for q in range(NB // 4):
            dve.wait_ge(b["proj_read"], q + 1)
            dve.tensor_reduce(b["norm"][:, q * 4:(q + 1) * 4], b["sq"][:, q % 2, :].rearrange("p (t j) -> p t j", t=4),
                              AX_X, ALU.add).then_inc(b["sq_summed"], 1)
        dve.wait_ge(b["norm_ready"], 1)
        link(dve.tensor_scalar(b["norm"][:, :], b["norm"][:, :], 1.0e-12, None, ALU.max))
        link(dve.reciprocal(b["norm"][:, :], b["norm"][:, :]))
        dve.wait_ge(logits_done, 1)
        link(dve.tensor_tensor(lg[:, :, :], logits, bc(b["norm"]), ALU.mult))
        link(dve.tensor_scalar(lg[:, :, :], lg[:, :, :], b["itemp"][:, :], None, ALU.mult))
        two_best(dve, link, core, lg[:, :, :], work[:, :, :], core.const("tie8"), 8, best[:, :], hot[:, :, :],
                 hot2[:, :, :])
        link(dve.tensor_reduce(best[:, :], lg[:, :, :], AX_X, ALU.max))
        dve.tensor_tensor(work[:, :, :], lg[:, :, :], bc(best), ALU.subtract).then_inc(dve_ready, 1)
        dve.wait_ge(act_done, 2)
        link(dve.tensor_tensor(gates, work[:, :, :], hot[:, :, :], ALU.mult))
        link(dve.tensor_reduce(best[:, :], gates, AX_X, ALU.add))
        link(dve.reciprocal(best[:, :], best[:, :]))
        link(dve.tensor_tensor(gates, gates, bc(best), ALU.mult))

    return extra, gate_fn, act_fn, pe_first


def wide_experts(core):
    w, ps = core.pack(7), core.ps

    def pe(pe, c, j, bank, b):
        return pe.matmul(ps[:, bank, :], w("W1", j * P, P), core.a[:, tok(c * CHUNK, CHUNK)], start=True, stop=True)

    def act(act, c, j, bank, out, b):
        return act.activation(out, ps[:, bank, :], ACT.Gelu, bias=w("b1", j, 1))

    return dict(pe=pe, act=act)


def linear_attention_stage(core, next_load=None):
    nc, w, ps, const = core.nc, core.pack(2), core.ps, core.const
    NJ, DH = 8, 64
    PHI, VAL, SCORE, SUMS, OUT = 2, 3, 4, 6, 7
    last_step = NB * NJ - 1
    with stage_scope(nc) as ctx:
        sb = lambda n, shape: ctx.enter_context(nc.sbuf_tensor(f"lin_{n}", shape, F32))
        sem = lambda n: nc.alloc_semaphore(f"lin_{n}")
        src = sb("src", [P, P])
        qk = sb("qk", [P, 2, 2 * P])
        sq = sb("square", [P, 2, 2 * P])
        phi = sb("features", [P, 2, 2, P])
        vt = sb("value", [P, 2, 2, DH + 1])
        sm = sb("masked", [P, 2, 2, P])
        den = sb("denominator", [P, 2])
        inv = sb("inverse", [P, 2])
        o = sb("context", [P, 2, P])
        ot = sb("context_turned", [P, NJ, P])
        s = {n: sem(n) for n in ["source_ready", "ones_ready", "qk_done", "qk_ready", "sq_ready", "phi_done", "phi_ready",
                                 "v_done", "v_ready", "s_done", "s_masked", "sum_done", "den_ready", "inv_ready",
                                 "context_ready", "ct_done", "ct_ready", "out_done", "out_read"]}
        block = ctx.enter_context(nc.Block())

        def run(eng, front, mid, tail):
            for k in range(NJ):
                front(Step(0, k, NJ))
                if k >= 1:
                    mid(Step(0, k - 1, NJ))
                if k >= 2:
                    tail(Step(0, k - 2, NJ))
            with eng.Fori(0, NB - 1) as i:
                for k in range(NJ, 2 * NJ):
                    front(Step(i, k, NJ))
                    mid(Step(i, k - 1, NJ))
                    tail(Step(i, k - 2, NJ))
            mid(Step(0, last_step, NJ))
            tail(Step(0, last_step - 1, NJ))
            tail(Step(0, last_step, NJ))

        def nothing(st):
            pass

        @block.sync
        def _(sp):
            if next_load is not None:
                next_load(sp)

        @block.gpsimd
        def _(pool):
            def front(st):
                if st.m == 0:
                    past(pool, s["v_done"], st.n)
                    pool.tensor_copy(src[:, :], core.a[:, tok(st.u * P, P)]).then_inc(s["source_ready"], 1)

            run(pool, front, nothing, nothing)

        @block.tensor
        def _(pe):
            wait_pack(pe, core, 2)

            def front(st):
                n, p = st.n, st.m % 2
                if st.m == 0:
                    pe.wait_ge(s["source_ready"], st.u + 1)
                past(pe, s["sq_ready"], n - 1)
                pe.matmul(ps[:, p, 0:P], w("wqT", st.m * P, P), src[:, :], start=True, stop=True)
                pe.matmul(ps[:, p, P:2 * P], w("wkT", st.m * P, P), src[:, :], start=True, stop=True).then_inc(
                    s["qk_done"], 1)
                past(pe, s["v_ready"], n)
                pe.matmul(ps[:, VAL, 0:P], src[:, :], w("wvT", st.m * P, P), start=True, stop=True).then_inc(
                    s["v_done"], 1)

            def features(st):
                n, p = st.n, st.m % 2
                pe.wait_ge(s["qk_ready"], n + 1)
                past(pe, s["phi_ready"], n)
                pe.matmul(ps[:, PHI, 0:2 * P], w("omegaT"), qk[:, p, :], start=True, stop=False)
                pe.wait_ge(s["sq_ready"], n + 1)
                pe.matmul(ps[:, PHI, 0:2 * P], const("half_block"), sq[:, p, :], start=False, stop=True).then_inc(
                    s["phi_done"], 1)

            def scores(st):
                n, p = st.n, st.m % 2
                pe.wait_ge(s["phi_ready"], n + 1)
                past(pe, s["s_masked"], n)
                for hh in range(2):
                    last = pe.matmul(ps[:, SCORE + hh, 0:P], phi[DH * hh:DH * (hh + 1), p, 1, :],
                                     phi[DH * hh:DH * (hh + 1), p, 0, :], start=True, stop=True)
                last.then_inc(s["s_done"], 1)

            def sums(st):
                n, p = st.n, st.m % 2
                pe.wait_ge(s["s_masked"], n + 1)
                pe.wait_ge(s["v_ready"], n + 1)
                past(pe, s["context_ready"], n)
                for hh in range(2):
                    last = pe.matmul(ps[:, SUMS, hh * (DH + 1):(hh + 1) * (DH + 1)], sm[:, p, hh, :],
                                     vt[:, p, hh, :], start=True, stop=True)
                last.then_inc(s["sum_done"], 1)

            def tail(st):
                n, p = st.n, st.m % 2
                pe.wait_ge(s["context_ready"], n + 1)
                past(pe, s["ct_ready"], n)
                if st.m == 0:
                    past(pe, s["out_read"], st.u)
                pe.transpose(ps[:, OUT, 0:P], o[:, p, :], const("ident")).then_inc(s["ct_done"], 1)
                if st.m == NJ - 1:
                    pe.wait_ge(s["ct_ready"], n + 1)
                    for j in range(NJ):
                        last = pe.matmul(ps[:, OUT, P:2 * P], w("woT", j * P, P), ot[:, j, :], start=(j == 0),
                                         stop=(j == NJ - 1))
                    last.then_inc(s["out_done"], 1)

            def step(st, first=0):
                front(st)
                if first < 2:
                    scores(st.back())
                if first < 1:
                    tail(st.back().back())
                features(st)
                if first < 2:
                    sums(st.back())

            step(Step(0, 0, NJ), 2)
            step(Step(0, 1, NJ), 1)
            for k in range(2, NJ):
                step(Step(0, k, NJ))
            with pe.Fori(0, NB - 1) as i:
                for k in range(NJ, 2 * NJ):
                    step(Step(i, k, NJ))
            scores(Step(0, last_step, NJ))
            tail(Step(0, last_step - 1, NJ))
            sums(Step(0, last_step, NJ))
            tail(Step(0, last_step, NJ))

        @block.scalar
        def _(act):
            def front(st):
                n, p = st.n, st.m % 2
                act.wait_ge(s["qk_ready"], n + 1)
                past(act, s["phi_done"], n - 1)
                act.activation(sq[:, p, :], ps[:, p, 0:2 * P], ACT.Square).then_inc(s["sq_ready"], 1)
                act.wait_ge(s["phi_done"], n + 1)
                past(act, s["s_done"], n - 1)
                act.activation(phi[:, p, :, :], ps[:, PHI, 0:2 * P].rearrange("p (t j) -> p t j", t=2), ACT.Exp,
                               bias=const("ln_m")).then_inc(s["phi_ready"], 1)

            def tail(st):
                n = st.n
                act.wait_ge(s["ct_done"], n + 1)
                if st.m == 0:
                    past(act, s["out_done"], st.u)
                act.activation(ot[:, st.m, :], ps[:, OUT, 0:P], ACT.Copy).then_inc(s["ct_ready"], 1)

            def step(st, has_tail=True):
                if has_tail:
                    tail(st.back().back())
                front(st)

            step(Step(0, 0, NJ), False)
            step(Step(0, 1, NJ), False)
            for k in range(2, NJ):
                step(Step(0, k, NJ))
            with act.Fori(0, NB - 1) as i:
                for k in range(NJ, 2 * NJ):
                    step(Step(i, k, NJ))
            tail(Step(0, last_step - 1, NJ))
            tail(Step(0, last_step, NJ))

        @block.vector
        def _(dve):
            wait_pack(dve, core, 2)
            dve.memset(vt[:, :, :, DH:DH + 1], 1.0).then_inc(s["ones_ready"], 1)
            dve.wait_ge(s["ones_ready"], 1)

            def front(st):
                n, p = st.n, st.m % 2
                dve.wait_ge(s["qk_done"], n + 1)
                past(dve, s["phi_done"], n - 1)
                dve.tensor_copy(qk[:, p, :], ps[:, p, 0:2 * P]).then_inc(s["qk_ready"], 1)
                dve.wait_ge(s["v_done"], n + 1)
                past(dve, s["sum_done"], n - 1)
                dve.tensor_copy(vt[:, p, :, 0:DH], ps[:, VAL, 0:P].rearrange("p (h d) -> p h d", h=2)).then_inc(
                    s["v_ready"], 1)

            def mask(st):
                n, p = st.n, st.m % 2
                dve.wait_ge(s["s_done"], n + 1)
                past(dve, s["sum_done"], n - 1)
                dve.tensor_tensor(sm[:, p, :, :], ps[:, SCORE:SCORE + 2, 0:P],
                                  const("causal_mul").unsqueeze(1).broadcast_to([P, 2, P]), ALU.mult).then_inc(
                    s["s_masked"], 1)

            def normalise(st):
                n, p = st.n, st.m % 2
                dve.wait_ge(s["sum_done"], n + 1)
                sums = ps[:, SUMS, 0:2 * (DH + 1)].rearrange("p (h d) -> p h d", h=2)
                past(dve, s["inv_ready"], n)
                dve.tensor_scalar(den[:, :], sums[:, :, DH], 1.0e-6, None, ALU.add).then_inc(s["den_ready"], 1)
                dve.wait_ge(s["den_ready"], n + 1)
                past(dve, s["context_ready"], n)
                dve.reciprocal(inv[:, :], den[:, :]).then_inc(s["inv_ready"], 1)
                dve.wait_ge(s["inv_ready"], n + 1)
                past(dve, s["ct_done"], n - 1)
                dve.tensor_tensor(o[:, p, :].rearrange("p (h d) -> p h d", h=2), sums[:, :, 0:DH],
                                  inv[:, :].unsqueeze(2).broadcast_to([P, 2, DH]), ALU.mult).then_inc(
                    s["context_ready"], 1)

            def output(st):
                if st.m == NJ - 1:
                    dve.wait_ge(s["out_done"], st.u + 1)
                    xb = core.x[:, tok(st.u * P, P)]
                    dve.scalar_tensor_tensor(out=xb, in0=ps[:, OUT, P:2 * P], scalar=w("bo"), in1=xb, op0=ALU.add,
                                             op1=ALU.add).then_inc(s["out_read"], 1)

            def step(st, first=0):
                front(st)
                if first < 2:
                    mask(st.back())
                if first < 1:
                    output(st.back().back())
                if first < 2:
                    normalise(st.back())

            step(Step(0, 0, NJ), 2)
            step(Step(0, 1, NJ), 1)
            for k in range(2, NJ):
                step(Step(0, k, NJ))
            with dve.Fori(0, NB - 1) as i:
                for k in range(NJ, 2 * NJ):
                    step(Step(i, k, NJ))
            mask(Step(0, last_step, NJ))
            output(Step(0, last_step - 1, NJ))
            normalise(Step(0, last_step, NJ))
            output(Step(0, last_step, NJ))


def latent_stage(core):
    nc, w, ps, const = core.nc, core.pack(4), core.ps, core.const
    with ExitStack() as ctx:
        wd = ctx.enter_context(nc.sbuf_tensor("latent_weight", [P, 32], F32))

        def pe_prepare(pe, s):
            pe.matmul(ps[:, 6, 0:32], w("WdT", rows=32), const("center32", rows=32), start=True, stop=True).then_inc(
                s["prepared"], 1)
            pe.wait_ge(s["prepared"], 2)

        def act_prepare(act, s):
            act.wait_ge(s["prepared"], 1)
            act.activation(wd[:, :], ps[:, 6, 0:32], ACT.Copy).then_inc(s["prepared"], 1)

        norm_stage(core, "latent", 4, core.a, core.b, 32, wd[:, :], const("mean32", rows=32), const("eps5"),
                   gamma=w("gamma", rows=32), beta=w("beta", rows=32), prepare=dict(pe=pe_prepare, act=act_prepare))


def latent_attention(core):
    w, const, ps = core.pack(4), core.const, core.ps

    def cfg(nc, ctx, s, name, qm, kt, ot):
        sb = lambda n, shape: ctx.enter_context(nc.sbuf_tensor(f"{name}_{n}", shape, F32))
        src, lat = sb("src", [P, 2, P]), sb("latent", [32, 2, P])
        even, odd, q = sb("times_cos", [P, 2, P]), sb("times_sin", [P, 2, P]), sb("query", [P, P])
        zero = sb("zero", [P, 1])
        ident16, mask16 = [ctx.enter_context(nc.sbuf_tensor(f"{name}_{n}", [P, P], mybir.dt.bfloat16))
                           for n in ("ident16", "mask16")]
        rotated = nc.alloc_semaphore(f"{name}_rotated")

        def start(eng):
            wait_pack(eng, core, 4)
            if eng is nc.vector:
                eng.memset(zero[:, :], 0.0).then_inc(s["own"], 1)
                eng.tensor_copy(ident16[:, :], const("ident")).then_inc(s["own"], 1)
                eng.tensor_copy(mask16[:, :], const("causal_add")).then_inc(s["own"], 1)
            eng.wait_ge(s["own"], 3)

        def bias(pe, out, g):
            pe.matmul(out, ident16[:, :], mask16[:, :].unsqueeze(1).broadcast_to([P, 4, P]), start=True, stop=False,
                      skip_group_check=True)

        def pool(pool, st):
            n, m = st.n, st.m
            past(pool, s["v_done"], n - 1)
            pool.tensor_copy(src[:, m % 2, :], core.a[:, tok(n * P, P)]).then_inc(s["source_ready"], 1)
            pool.tensor_copy(lat[:, m % 2, :], core.b[0:32, tok(n * P, P)]).then_inc(s["source_ready"], 1)

        def pe_qk(pe, st, bank):
            n, p = st.n, st.m % 2
            pe.wait_ge(s["source_ready"], n * 2 + 2)
            pe.matmul(ps[:, bank, 0:P], w("Wq"), src[:, p, :], start=True, stop=True)
            pe.matmul(ps[:, bank, 2 * P:3 * P], w("Wqs"), src[:, p, :], start=True, stop=True)
            pe.matmul(ps[:, bank, P:2 * P], w("Wuk", rows=32), lat[:, p, :], start=True, stop=True)
            return pe.matmul(ps[:, bank, 3 * P:4 * P], w("Wuks", rows=32), lat[:, p, :], start=True, stop=True)

        def pe_v(pe, st, bank):
            return pe.matmul(ps[:, bank, 0:P], lat[:, st.m % 2, :], w("Wuv", rows=32), start=True, stop=True)

        def pe_out(pe, st, bank):
            return pe.matmul(ps[:, bank, P:2 * P], w("Wo"), ot[:, :], start=True, stop=True)

        def dve_q(dve, st, bank, head_mask):
            n, p = st.n, st.m % 2
            both = lambda lo: ps[:, bank, lo:lo + 2 * P].rearrange("p (t j) -> p t j", t=2)
            over = lambda c: const(c).unsqueeze(1).broadcast_to([P, 2, P])
            dve.wait_ge(s["qk_done"], n + 1)
            past(dve, s["q_ready"], n)
            past(dve, s["k_ready"], n)
            dve.tensor_tensor(even[:, :, :], both(0), over("cos"), ALU.mult).then_inc(rotated, 1)
            dve.tensor_tensor(odd[:, :, :], both(2 * P), over("sin"), ALU.mult).then_inc(rotated, 1)
            dve.wait_ge(rotated, n * 3 + 2)
            dve.tensor_tensor(q[:, :], even[:, 0, :], odd[:, 0, :], ALU.add).then_inc(rotated, 1)
            dve.tensor_tensor(kt[:, p, :], even[:, 1, :], odd[:, 1, :], ALU.add).then_inc(s["k_ready"], 1)
            dve.wait_ge(rotated, n * 3 + 3)
            dve.tensor_tensor(qm[:, p, :, :], q[:, :].unsqueeze(1).broadcast_to([P, 4, P]),
                              head_mask.unsqueeze(2).broadcast_to([P, 4, P]), ALU.mult).then_inc(s["q_ready"], 1)

        def dve_out(dve, st, bank):
            xb = core.x[:, tok(st.n * P, P)]
            return dve.tensor_tensor(xb, ps[:, bank, P:2 * P], xb, ALU.add)

        return dict(start=start, pool=pool, pe_qk=pe_qk, pe_v=pe_v, pe_out=pe_out, dve_q=dve_q, dve_out=dve_out,
                    bv=lambda m: zero[:, :], bias=bias)

    return cfg


CELLS, MAX_PREV, PAIRS = 6, 5, 4


def cell_weights_stage(core, comp, comp_bias, edge, edge_bias, turn):
    nc, w, ps = core.nc, core.pack(5), core.ps
    with stage_scope(nc) as ctx:
        sem = lambda n: nc.alloc_semaphore(f"cellw_{n}")
        product_done, product_read = sem("product_done"), sem("product_read")
        scaled = sem("scaled")
        block = ctx.enter_context(nc.Block())

        @block.tensor
        def _(pe):
            wait_pack(pe, core, 5)
            for c in range(CELLS):
                for i, name in enumerate(("Wq", "Wk", "Wv")):
                    j = 3 * c + i
                    past(pe, product_read, j - 1)
                    pe.matmul(ps[:, j % 2, 0:P], w("WeT", j * P, P), w(name, c * P, P), start=True, stop=True)
                    pe.matmul(ps[:, j % 2, P:P + 1], w(name, c * P, P), w("be", j, 1), start=True,
                              stop=True).then_inc(product_done, 1)

        @block.vector
        def _(dve):
            wait_pack(dve, core, 5)
            for j in range(3 * CELLS):
                dve.wait_ge(product_done, j + 1)
                dve.tensor_scalar(comp[:, j, :], ps[:, j % 2, 0:P], w("ew", j, 1), None, ALU.mult)
                dve.tensor_scalar(comp_bias[:, j:j + 1], ps[:, j % 2, P:P + 1], w("ew", j, 1), None,
                                  ALU.mult).then_inc(product_read, 1)
            for c in range(CELLS):
                dve.tensor_scalar(edge[:, c, :], w("We", c * P, P), w("ew", 3 * c, 1), None, ALU.mult)
                dve.tensor_scalar(turn[:, c, :], w("Wo", c * P, P), w("act", c, 1), None, ALU.mult)
                dve.tensor_scalar(edge_bias[:, c:c + 1], w("be", 3 * c, 1), w("ew", 3 * c, 1), None,
                                  ALU.mult).then_inc(scaled, 1)
            dve.wait_ge(scaled, CELLS)


def cell_attention(core, comp, comp_bias, edge, edge_bias, turn):
    w, const, ps = core.pack(5), core.const, core.ps

    def cfg(nc, ctx, s, name, qm, kt, ot):
        own = ctx.enter_context(nc.sbuf_tensor(f"{name}_nodes", [P, 2, CELLS, 2 * P], F32))

        def node(pair, slot):
            if pair < 2:
                return own[:, pair, slot, :]
            at = ((pair - 2) * CELLS + slot) * (2 * P)
            return core.b[:, at:at + 2 * P]

        def inputs(c):
            nsrc = min(c + 1, MAX_PREV)
            snode = c - nsrc
            return c, snode + 1, snode + nsrc // 2 + 1

        def start(eng):
            pass

        def pool(pool, st):
            if st.m < PAIRS:
                past(pool, s["qk_done"], st.n - (2 * PAIRS - 1))
                pool.tensor_copy(node(st.m, 0), core.a[:, tok(st.u * (2 * P * PAIRS) + st.m * (2 * P), 2 * P)]).then_inc(
                    s["source_ready"], 1)

        def pe_qk(pe, st, bank):
            c, ab = st.m // PAIRS, st.m % PAIRS
            iq, ik, _ = inputs(c)
            if c == 0:
                pe.wait_ge(s["source_ready"], st.u * PAIRS + (ab + 1))
            pe.matmul(ps[:, bank, 0:2 * P], comp[:, 3 * c, :], node(ab, iq), start=True, stop=True)
            return pe.matmul(ps[:, bank, 2 * P:4 * P], comp[:, 3 * c + 1, :], node(ab, ik), start=True,
                             stop=True)

        def pe_v(pe, st, bank):
            c, ab = st.m // PAIRS, st.m % PAIRS
            for bb in range(2):
                last = pe.matmul(ps[:, bank, bb * P:(bb + 1) * P], node(ab, inputs(c)[2])[:, bb * P:(bb + 1) * P],
                                 comp[:, 3 * c + 2, :], start=True, stop=True)
            return last

        def pe_out(pe, st, bank):
            c, ab = st.m // PAIRS, st.m % PAIRS
            pe.matmul(ps[:, bank, 2 * P:4 * P], turn[:, c, :], ot[:, :], start=True, stop=False)
            return pe.matmul(ps[:, bank, 2 * P:4 * P], edge[:, c, :], node(ab, c), start=False, stop=True)

        def act_k(act, st, bank):
            c = st.m // PAIRS
            act.wait_ge(s["q_ready"], st.n + 1)
            act.activation(kt[:, st.m % 2, :], ps[:, bank, 2 * P:4 * P], ACT.Identity,
                           bias=comp_bias[:, 3 * c + 1:3 * c + 2]).then_inc(s["k_ready"], 1)

        def dve_q(dve, st, bank, head_mask):
            c = st.m // PAIRS
            dve.wait_ge(s["qk_done"], st.n + 1)
            for r in range(2):
                last = dve.tensor_scalar(qm[:, st.m % 2, r, :], ps[:, bank, 0:2 * P], comp_bias[:, 3 * c:3 * c + 1],
                                         head_mask[:, r:r + 1], ALU.add, ALU.mult)
            last.then_inc(s["q_ready"], 1)

        def dve_out(dve, st, bank):
            c, ab = st.m // PAIRS, st.m % PAIRS
            out = node(ab, c + 1) if c < CELLS - 1 else core.a[:, tok(st.u * (2 * P * PAIRS) + ab * (2 * P), 2 * P)]
            return dve.tensor_scalar(out, ps[:, bank, 2 * P:4 * P], edge_bias[:, c:c + 1], None, ALU.add)

        return dict(start=start, pool=pool, pe_qk=pe_qk, pe_v=pe_v, pe_out=pe_out, act_k=act_k, dve_q=dve_q,
                    dve_out=dve_out, bv=lambda m: comp_bias[:, 3 * (m // PAIRS) + 2:3 * (m // PAIRS) + 3])

    return cfg


def layer2_cells(core, next_load=None):
    nc = core.nc
    with ExitStack() as ctx:
        sb = lambda n, shape: ctx.enter_context(nc.sbuf_tensor("cellw_" + n, shape, F32))
        tiles = (sb("comp", [P, 3 * CELLS, P]), sb("comp_bias", [P, 3 * CELLS]), sb("edge", [P, CELLS, P]),
                 sb("edge_bias", [P, CELLS]), sb("turn", [P, CELLS, P]))
        cell_weights_stage(core, *tiles)
        attention_stage(core, "cells", NB // 2 * CELLS, PAIRS * CELLS, 8, cell_attention(core, *tiles), next_load=next_load)
    w = core.pack(5)
    norm_stage(core, "norm2", 5, core.a, core.x, P, core.const("center"), core.const("mean"), core.const("eps6"),
               gamma=w("ln_g"), beta=w("ln_b"), add_to=core.x)


def modulated_stage(core):
    nc, w, ps, const = core.nc, core.pack(6), core.ps, core.const
    with stage_scope(nc) as ctx:
        sb = lambda n, shape: ctx.enter_context(nc.sbuf_tensor(f"mod_{n}", shape, F32))
        sem = lambda n: nc.alloc_semaphore(f"mod_{n}")
        ys, ys2, w2 = sb("ys", [P, NB]), sb("ys_square", [P, NB]), sb("weight_square", [P, P])
        dev, d = sb("deviation", [P, NB]), sb("demodulation", [P, NB])
        xs = sb("scaled", [P, 2, 4, P])
        s = {n: sem(n) for n in ["own", "squares", "d_done", "dev_ready", "ys_ready", "xs_ready", "y_done", "y_read"]}
        block = ctx.enter_context(nc.Block())
        nb = CHUNK // P

        def loop(eng, one):
            one(0, 0)
            one(1, 1)
            with eng.Fori(1, NCHUNK // 2) as i:
                one(i * 2, 0)
                one(i * 2 + 1, 1)

        @block.gpsimd
        def _(pool):
            pool.wait_ge(s["ys_ready"], 1)

            def one(c, p):
                past(pool, s["y_done"], c - 1)
                pool.tensor_tensor(xs[:, p, :, :], core.x[:, tok(c * CHUNK, CHUNK)].rearrange("p (b t) -> p b t", b=nb),
                                   ys[:, bass.ds(c * nb, nb)].unsqueeze(2).broadcast_to([P, nb, P]),
                                   ALU.mult).then_inc(s["xs_ready"], 1)

            loop(pool, one)

        @block.tensor
        def _(pe):
            wait_pack(pe, core, 6)
            pe.wait_ge(s["squares"], 2)
            pe.matmul(ps[:, 2, 0:NB], w2[:, :], ys2[:, :], start=True, stop=True).then_inc(s["d_done"], 1)

            def one(c, p):
                pe.wait_ge(s["xs_ready"], c + 1)
                past(pe, s["y_read"], c - 1)
                pe.matmul(ps[:, p, :], w("weight"), xs[:, p, :, :].rearrange("p b t -> p (b t)"), start=True,
                          stop=True).then_inc(s["y_done"], 1)

            loop(pe, one)

        @block.scalar
        def _(act):
            act.wait_ge(s["d_done"], 1)
            act.activation(dev[:, :], ps[:, 2, 0:NB], ACT.Sqrt, bias=const("eps8")).then_inc(s["dev_ready"], 1)

        @block.vector
        def _(dve):
            wait_pack(dve, core, 6)
            dve.tensor_scalar(ys[:, :], const("cond"), float(P) ** -0.5, None, ALU.mult).then_inc(s["ys_ready"], 1)
            dve.tensor_tensor(w2[:, :], w("weight"), w("weight"), ALU.mult).then_inc(s["squares"], 1)
            dve.wait_ge(s["ys_ready"], 1)
            dve.tensor_tensor(ys2[:, :], ys[:, :], ys[:, :], ALU.mult).then_inc(s["squares"], 1)
            dve.wait_ge(s["dev_ready"], 1)
            dve.reciprocal(d[:, :], dev[:, :]).then_inc(s["own"], 1)
            dve.wait_ge(s["own"], 1)

            def one(c, p):
                dve.wait_ge(s["y_done"], c + 1)
                dve.tensor_tensor(core.a[:, tok(c * CHUNK, CHUNK)].rearrange("p (b t) -> p b t", b=nb),
                                  ps[:, p, :].rearrange("p (b t) -> p b t", b=nb),
                                  d[:, bass.ds(c * nb, nb)].unsqueeze(2).broadcast_to([P, nb, P]),
                                  ALU.mult).then_inc(s["y_read"], 1)

            loop(dve, one)


def layer0_ffn(core):
    w = core.pack(1)
    norm_stage(core, "norm0", 1, core.a, core.b, P, core.const("center"), core.const("mean"), core.const("eps5"))
    extra, gate_fn = layer0_gates(core)
    router_stage(core, "route0", 1, core.a, 8, lambda b: w("WgT"), gate_fn, core.gate(8), extra=extra)
    setup, hidden = layer0_experts(core)
    expert_stage(core, "experts0", 1, 8, core.gate(8), hidden, lambda e, f, lo, n: w("W2", (e // 4) * P, P, rows=n, first=lo),
                 1, lambda e: (e // 4, 32 * (e % 4), 32), b2=w("b2", rows=8), finish=add_to_x(core), setup=setup,
                 n_hidden=2)


def layer1_ffn(core):
    w = core.pack(3)
    extra, gate_fn, act_fn = layer1_gates(core)
    router_stage(core, "route1", 3, core.a, 16, lambda b: w("Wr"), gate_fn, core.gate(16), extra=extra, act_fn=act_fn)
    setup, hidden = layer1_experts(core)
    expert_stage(core, "experts1", 3, 16, core.gate(16), hidden, lambda e, f, lo, n: w("W2", e * P, P), 1,
                 lambda e: (e, 0, P), b2=w("b2", rows=16), finish=add_to_x(core), setup=setup, n_hidden=16)


def layer3_cond2(core):
    w = core.pack(7)
    extra, gate_fn, act_fn, pe_first = layer3_gates(core)
    router_stage(core, "route3", 7, core.x, 8, lambda b: w("rW"), gate_fn, core.gate(8), extra=extra, act_fn=act_fn,
                 pe_first=pe_first)
    setup, hidden, shared, finish = layer3_experts(core)
    expert_stage(core, "experts3", 7, 8, core.gate(8), hidden, lambda e, f, lo, n: w("W2e", e * P, P), 1,
                 lambda e: (e, 0, P), shared=shared, finish=finish, setup=setup, n_hidden=8)


def layer3_ffn(core):
    w = core.pack(7)
    extra, gate_fn, act_fn, pe_first = cosine_gates(core)
    router_stage(core, "route4", 7, core.a, 8, lambda b: b["comp"][:, :], gate_fn, core.gate(8), extra=extra,
                 act_fn=act_fn, pe_first=pe_first)
    expert_stage(core, "experts4", 7, 8, core.gate(8), wide_experts(core),
                 lambda e, f, lo, n: w("W2", (e * 4 + f) * P, P), 4, lambda e: (4 * e, 0, P), b2=w("b2", rows=8),
                 finish=add_to_x(core), n_hidden=32)


def program(nc, dram, out):
    with ExitStack() as ctx:
        core = Core(nc, ctx)
        stages = [
            (0, lambda: low_rank_stage(core, dram)),
            (0, lambda: attention_stage(core, "attn0", NB, 4, 16, plain_attention(core, 0, True))),
            (1, lambda: leaky_stage(core, lambda sp: load_pack(sp, core, dram, 2))),
            (1, lambda: layer0_ffn(core)),
            (2, lambda: lstm_stage(core, "lstm1", 2, lambda sp: load_pack(sp, core, dram, 3))),
            (2, lambda: linear_attention_stage(core)),
            (3, lambda: lstm_stage(core, "lstm2", 3, lambda sp: load_pack(sp, core, dram, 4))),
            (3, lambda: layer1_ffn(core)),
            (4, lambda: lstm_stage(core, "lstm3", 4, lambda sp: load_pack(sp, core, dram, 5))),
            (4, lambda: (latent_stage(core), attention_stage(core, "attn2", NB, 4, 16, latent_attention(core)))),
            (5, lambda: gru_stage(core, lambda sp: load_pack(sp, core, dram, 6))),
            (5, lambda: layer2_cells(core)),
            (6, lambda: modulated_stage(core)),
            (6, lambda: attention_stage(core, "attn3", NB, 4, 16, plain_attention(core, 6, False),
                                        next_load=lambda sp: load_pack(sp, core, dram, 7))),
            (7, lambda: layer3_cond2(core)),
            (7, lambda: layer3_ffn(core)),
        ]
        for _, run in stages:
            run()
        with ExitStack() as end:
            stored = end.enter_context(nc.semaphore("stored"))
            block = end.enter_context(nc.Block())

            @block.sync
            def _(sp):
                sp.dma_start(out, core.x[:, :]).then_inc(stored, 16)
                sp.wait_ge(stored, 16)


def host_layout(i):
    f = np.float32
    part = np.arange(P)
    c = {}
    c["ident"] = np.eye(P, dtype=f)
    c["center"] = np.eye(P, dtype=f) - f(1.0 / P)
    c["mean"] = np.full((P, P), 1.0 / P, f)
    c["head8"] = ((part[:, None] % 32) // 8 == np.arange(4)[None, :]).astype(f) * f(8 ** -0.5)
    c["head16"] = ((part[:, None] % 32) // 16 == np.arange(2)[None, :]).astype(f) * f(16 ** -0.5)
    c["causal_add"] = np.where(part[:, None] >= part[None, :], f(0), f(MASKED))
    c["causal_mul"] = (part[:, None] <= part[None, :]).astype(f)
    c["gate_pick"] = np.repeat(np.eye(4, dtype=f), NB, axis=1)
    inv = (1.0 / 10000.0 ** (np.arange(4, dtype=f) / 4)).astype(f)
    angle = (part[None, :].astype(f) * inv[(part % 8) % 4][:, None]).astype(f)
    c["cos"] = np.cos(angle).astype(f)
    c["sin"] = (np.sin(angle) * np.where(part % 8 < 4, -1.0, 1.0)[:, None]).astype(f)
    c["center32"] = np.eye(32, dtype=f) - f(1.0 / 32)
    c["mean32"] = np.full((32, P), 1.0 / 32, f)
    c["half_block"] = np.where(part[:, None] // 64 == part[None, :] // 64, f(-0.5), f(0))
    c["cond"] = i["cond_1024"].T
    c["eps5"] = np.full((P, 1), 1e-5, f)
    c["eps6"] = np.full((P, 1), 1e-6, f)
    c["eps8"] = np.full((P, 1), 1e-8, f)
    c["ln_m"] = np.full((P, 1), -math.log(8.0), f)
    c["tie8"] = np.tile(np.arange(8, 0, -1).astype(f), (P, 1))
    c["tie16"] = np.tile(np.arange(16, 0, -1).astype(f), (P, 1))

    def col(a):
        return np.asarray(a).reshape(-1, P).T

    def wide(a):
        return np.asarray(a).transpose(1, 0, 2).reshape(a.shape[1], -1)

    pos = np.clip(part[:, None] + 127 - part[None, :], 0, 126)
    rel = i["L0_attn_rel_table"][pos].transpose(0, 2, 1).reshape(P, 16 * P)
    p0 = dict(W=i["L0_cond_W"].T, fc_bias=col(i["L0_cond_fc_bias"]), Wq=i["L0_attn_Wq"], Wk=i["L0_attn_Wk"],
              Wv=i["L0_attn_Wv"], Wo=i["L0_attn_Wo"], bq=col(i["L0_attn_bq"]), bk=col(i["L0_attn_bk"]),
              bv=col(i["L0_attn_bv"]), bo=col(i["L0_attn_bo"]), rel=rel)
    p1 = dict(WhT=i["L0_cond2_W"][:, :P].T, WzT=i["L0_cond2_W"][:, P:].T, b=col(i["L0_cond2_b"]),
              alpha=col(i["L0_cond2_alpha"]), WgT=i["L0_ffn_Wg"].T, ln_scale=col(i["L0_ffn_ln_scale"]),
              ln_bias=col(i["L0_ffn_ln_bias"]), W1=wide(i["L0_ffn_W1"]), b1=col(i["L0_ffn_b1"]),
              W2=wide(i["L0_ffn_W2"].reshape(2, P, P)), b2=i["L0_ffn_b2"])
    omegaT = i["L1_attn_omega"].T
    pair = np.zeros((P, P), f)
    pair[:64, :64] = omegaT
    pair[64:, 64:] = omegaT
    p2 = dict(Wx=i["L1_cond_Wx"], Wh=i["L1_cond_Wh"], b=i["L1_cond_b"].reshape(4, P), omegaT=pair,
              wqT=i["L1_attn_wq"].T, wkT=i["L1_attn_wk"].T, wvT=i["L1_attn_wv"].T,
              woT=wide(i["L1_attn_wo"].T.reshape(8, P, P)), bo=col(i["L1_attn_bo"]))
    p3 = dict(Wx=i["L1_cond2_Wx"], Wh=i["L1_cond2_Wh"], b=i["L1_cond2_b"].reshape(4, P), Wr=i["L1_ffn_Wr"],
              br=np.tile(i["L1_ffn_br"], (P, 1)), W1T=wide(i["L1_ffn_W1"].transpose(0, 2, 1)),
              b1=col(i["L1_ffn_b1"]), g1=col(i["L1_ffn_g1"]), be1=col(i["L1_ffn_be1"]),
              W2=wide(i["L1_ffn_W2"]), b2=i["L1_ffn_b2"])
    swap = (part // 8) * 8 + (part + 4) % 8
    p4 = dict(Wx=i["L2_cond_Wx"], Wh=i["L2_cond_Wh"], b=i["L2_cond_b"].reshape(4, P), Wq=i["L2_attn_W_q"],
              Wqs=i["L2_attn_W_q"][:, swap], WdT=i["L2_attn_W_dkv"].T, Wuk=i["L2_attn_W_uk"],
              Wuks=i["L2_attn_W_uk"][:, swap], Wuv=i["L2_attn_W_uv"], Wo=i["L2_attn_W_o"],
              gamma=i["L2_attn_ln_gamma"].reshape(32, 1), beta=i["L2_attn_ln_beta"].reshape(32, 1))
    cells, lind = [], 0
    for c_ in range(6):
        n = min(c_ + 1, 5)
        cells += [lind + n - 1, lind, lind + n // 2]
        lind += n
    We, be = i["L2_ffn_We"], i["L2_ffn_be"]
    p5 = dict(Wz=i["L2_cond2_W_z"], Uz=i["L2_cond2_U_z"], Cz=i["L2_cond2_C_z"], bz=col(i["L2_cond2_b_z"]),
              Wr=i["L2_cond2_W_r"], Ur=i["L2_cond2_U_r"], Cr=i["L2_cond2_C_r"], br=col(i["L2_cond2_b_r"]),
              W=i["L2_cond2_W"], U=i["L2_cond2_U"], C=i["L2_cond2_C"], b=col(i["L2_cond2_b"]),
              ew=np.tile(i["L2_ffn_ew"].reshape(1, 18), (P, 1)), act=np.tile(i["L2_ffn_act_w"].reshape(1, 6), (P, 1)),
              We=wide(We[cells[0::3]]), WeT=wide(We[cells].transpose(0, 2, 1)), be=col(be[cells]),
              Wq=wide(i["L2_ffn_Wq"]), Wk=wide(i["L2_ffn_Wk"]), Wv=wide(i["L2_ffn_Wv"]), Wo=wide(i["L2_ffn_Wo"]),
              ln_g=col(i["L2_ffn_ln_g"]), ln_b=col(i["L2_ffn_ln_b"]))
    p6 = dict(weight=i["L3_cond_weight"], Wq=i["L3_attn_Wq"].T, Wk=i["L3_attn_Wk"].T, Wv=i["L3_attn_Wv"].T,
              Wo=i["L3_attn_Wo"].T)
    rW = i["L3_cond2_router_W"]
    p7 = dict(rW=rW[:P], rT=rW[P:], rbias=np.tile(i["L3_cond2_router_bias"], (P, 1)), w1=i["L3_cond2_w1"],
              w3=i["L3_cond2_w3"], w2=wide(i["L3_cond2_w2"].reshape(2, P, P)), W1e=wide(i["L3_cond2_W1e"]),
              W2e=wide(i["L3_cond2_W2e"]), Wp=i["L3_ffn_Wp"], WpT=i["L3_ffn_Wp"].T, sim=i["L3_ffn_sim_matrix"],
              temp=np.tile(i["L3_ffn_temperature"].reshape(1, 1), (P, 1)), W1=wide(i["L3_ffn_W1"]),
              b1=col(i["L3_ffn_b1"]), W2=wide(i["L3_ffn_W2"].reshape(32, P, P)), b2=i["L3_ffn_b2"])
    arrays = {"x": i["x"].reshape(NTOK, P).T, "factors": i["fside_Bx1x1024x16_0"].reshape(NTOK, 16).T}
    for name, parts in dict(const=c, p0=p0, p1=p1, p2=p2, p3=p3, p4=p4, p5=p5, p6=p6, p7=p7).items():
        assert list(parts) == list(PACKS[name]), name
        cols = []
        for key, a in parts.items():
            a = np.asarray(a)
            assert a.shape[1] == PACKS[name][key] and a.shape[0] <= P, (name, key, a.shape)
            cols.append(a if a.shape[0] == P else np.concatenate([a, np.zeros((P - a.shape[0], a.shape[1]), a.dtype)]))
        arrays[name] = np.concatenate(cols, axis=1)
    return {k: np.ascontiguousarray(v) for k, v in arrays.items()}


def kernel(**inputs):
    import concourse.bacc as bacc
    from concourse.bass_utils import run_bass_kernel_spmd

    arrays = host_layout({k: np.asarray(v) for k, v in inputs.items()})
    nc = bacc.Bacc("TRN2", target_bir_lowering=False, num_devices=1)
    dram = {k: nc.dram_tensor(f"in_{k}", v.shape, F32, kind="ExternalInput").ap() for k, v in arrays.items()}
    out = nc.dram_tensor("out_x", (P, NTOK), F32, kind="ExternalOutput").ap()
    program(nc, dram, out)
    got = run_bass_kernel_spmd(nc, [{f"in_{k}": v for k, v in arrays.items()}], core_ids=[0])
    return np.ascontiguousarray(got.results[0]["out_x"].T).reshape(NB, P, P)
```

```python
import math
from contextlib import ExitStack, contextmanager

import numpy as np
import concourse.bass as bass
from concourse import mybir

F32 = mybir.dt.float32
ALU = mybir.AluOpType
ACT = mybir.ActivationFunctionType
AX_X = mybir.AxisListType.X

P = 128
NB = 32
NTOK = NB * P
BANK = 512
CHUNK = 512
NCHUNK = NTOK // CHUNK
MASKED = -1.0e30

PACKS = {
    "const": dict(ident=P, center=P, mean=P, head8=4, head16=2, causal_add=P, causal_mul=P, gate_pick=P,
                  cos=P, sin=P, center32=32, mean32=P, half_block=P, cond=NB, spread8=2 * P, eps5=1, eps6=1, eps8=1,
                  ln_m=1, tie8=8, tie16=16),
    "p0": dict(W=P, fc_bias=1, Wq=P, Wk=P, Wv=P, Wo=P, bq=1, bk=1, bv=1, bo=1, rel=16 * P),
    "p1": dict(WhT=P, WzT=P, b=1, alpha=1, WgT=8, ln_scale=8, ln_bias=8, W1=256, b1=2, W2=2 * P, b2=P),
    "p2": dict(Wx=512, Wh=512, b=P, omegaT=P, wqT=1024, wkT=1024, wvT=1024, woT=1024, bo=1),
    "p3": dict(Wx=512, Wh=512, b=P, Wr=16, br=16, W1T=2048, b1=16, g1=16, be1=16, W2=2048, b2=P),
    "p4": dict(Wx=512, Wh=512, b=P, Wq=P, Wqs=P, WdT=P, Wuk=P, Wuks=P, Wuv=P, Wo=P, gamma=1, beta=1),
    "p5": dict(Wz=P, Uz=P, Cz=P, bz=1, Wr=P, Ur=P, Cr=P, br=1, W=P, U=P, C=P, b=1, ew=18, act=6,
               We=6 * P, WeT=18 * P, be=18, Wq=6 * P, Wk=6 * P, Wv=6 * P, Wo=6 * P, ln_g=1, ln_b=1),
    "p6": dict(weight=P, Wq=P, Wk=P, Wv=P, Wo=P),
    "p7": dict(rW=8, rT=8, rbias=8, w1=256, w3=256, w2=2 * P, W1e=8 * P, W2e=8 * P, Wp=P, WpT=P, sim=P,
               temp=1, W1=32 * P, b1=32, W2=32 * P, b2=P),
}
WIDTH = {k: sum(v.values()) for k, v in PACKS.items()}
REGION = [max(WIDTH[f"p{k}"] for k in range(r, 8, 2)) for r in range(2)]
LOADS = ["const"] + [f"p{k}" for k in range(8)]


class Step:

    def __init__(self, i, k, unroll):
        self.i, self.k, self.unroll = i, k, unroll
        self.n, self.m, self.u = i * unroll + k, k % unroll, i + k // unroll

    def back(self):
        return Step(self.i, self.k - 1, self.unroll)


class View:

    def __init__(self, tile, pack):
        self.tile, self.at, here = tile, {}, 0
        for name, n in PACKS[pack].items():
            self.at[name] = (here, n)
            here += n

    def __call__(self, name, lo=0, n=None, rows=P, first=0):
        here, width = self.at[name]
        n = width - lo if n is None else n
        return self.tile[first:first + rows, here + lo:here + lo + n]


class Core:

    def __init__(self, nc, ctx):
        self.nc = nc
        self.x = ctx.enter_context(nc.sbuf_tensor("x_res", [P, NTOK], F32))
        self.a = ctx.enter_context(nc.sbuf_tensor("act_a", [P, NTOK], F32))
        self.b = ctx.enter_context(nc.sbuf_tensor("act_b", [P, NTOK], F32))
        self.region = [ctx.enter_context(nc.sbuf_tensor(f"weights{r}", [P, REGION[r]], F32)) for r in range(2)]
        self.gates = ctx.enter_context(nc.sbuf_tensor("gates", [P, NB * 16], F32))
        self.ctile = ctx.enter_context(nc.sbuf_tensor("constants", [P, WIDTH["const"]], F32))
        self.ps = ctx.enter_context(nc.psum_tensor("banks", [P, 8, BANK], F32))
        self.loaded = {k: ctx.enter_context(nc.semaphore(f"loaded_{k}")) for k in LOADS + ["x", "f"]}
        self.const = View(self.ctile, "const")

    def gate(self, ne):
        return self.gates[:, 0:NB * ne].rearrange("p (t e) -> p t e", e=ne)

    def pack(self, k):
        return View(self.region[k % 2], f"p{k}")


@contextmanager
def stage_scope(nc):
    before = nc.snapshot_sems()
    with ExitStack() as ctx:
        yield ctx
    nc.clear_and_free_semaphores(nc.allocated_since(before))
    nc.all_engine_barrier()


def load_pack(sp, core, dram, k):
    w = WIDTH[f"p{k}"]
    half = w // 2
    sp.dma_start(core.region[k % 2][:, 0:half], dram[f"p{k}"][:, 0:half]).then_inc(core.loaded[f"p{k}"], 16)
    sp.dma_start(core.region[k % 2][:, half:w], dram[f"p{k}"][:, half:w]).then_inc(core.loaded[f"p{k}"], 16)


def wait_pack(eng, core, k):
    eng.wait_ge(core.loaded[f"p{k}"], 32)


def past(eng, sem, value):
    if not isinstance(value, int) or value > 0:
        eng.wait_ge(sem, value)


def tok(t, n):
    return bass.ds(t, n)


def low_rank_stage(core, dram):
    nc, w, ps = core.nc, core.pack(0), core.ps
    with stage_scope(nc) as ctx:
        sb = lambda name, shape: ctx.enter_context(nc.sbuf_tensor("lr_" + name, shape, F32))
        sem = lambda name: nc.alloc_semaphore("lr_" + name)
        factor = sb("factor", [16, 2, P])
        weight = sb("weight", [P, 2, P])
        shift = sb("shift", [P, NB])
        shift_ready, factor_ready, gram_done, weight_ready, y_done, gelu_done = map(
            sem, ["shift_ready", "factor_ready", "gram_done", "weight_ready", "y_done", "gelu_done"])
        block = ctx.enter_context(nc.Block())

        @block.sync
        def _(sp):
            sp.dma_start(core.b[0:16, :], dram["factors"]).then_inc(core.loaded["f"], 16)
            load_pack(sp, core, dram, 0)
            sp.dma_start(core.ctile[:, :], dram["const"]).then_inc(core.loaded["const"], 16)
            sp.dma_start(core.x[:, :], dram["x"]).then_inc(core.loaded["x"], 16)
            load_pack(sp, core, dram, 1)

        @block.gpsimd
        def _(pool):
            pool.wait_ge(core.loaded["f"], 16)

            def copy(b, p, first):
                if not first:
                    pool.wait_ge(gram_done, b - 1)
                pool.tensor_copy(factor[:, p, :], core.b[0:16, tok(b * P, P)]).then_inc(factor_ready, 1)

            copy(0, 0, True)
            copy(1, 1, True)
            with pool.Fori(1, NB // 2) as i:
                copy(i * 2, 0, False)
                copy(i * 2 + 1, 1, False)

        @block.tensor
        def _(pe):
            pe.wait_ge(core.loaded["x"], 16)

            def pair(i, first):
                for p in range(2):
                    pe.wait_ge(factor_ready, i * 2 + p + 1)
                    if not first:
                        pe.wait_ge(weight_ready, i * 2 + p - 1)
                    pe.matmul(ps[:, p, 0:P], factor[:, p, :], factor[:, p, :], start=True, stop=True).then_inc(
                        gram_done, 1)
                for p in range(2):
                    pe.wait_ge(weight_ready, i * 2 + p + 1)
                    if not first:
                        pe.wait_ge(gelu_done, i * 2 + p - 1)
                    pe.matmul(ps[:, 2 + p, 0:P], weight[:, p, :], core.x[:, tok((i * 2 + p) * P, P)],
                              start=True, stop=True).then_inc(y_done, 1)

            pair(0, True)
            with pe.Fori(1, NB // 2) as i:
                pair(i, False)

        @block.vector
        def _(dve):
            dve.wait_ge(core.loaded["const"], 16)
            wait_pack(dve, core, 0)
            dve.tensor_scalar(shift[:, :], core.const("cond"), w("fc_bias"), None, ALU.add).then_inc(shift_ready, 1)

            def one(b, p, first):
                dve.wait_ge(gram_done, b + 1)
                if not first:
                    dve.wait_ge(y_done, b - 1)
                dve.scalar_tensor_tensor(out=weight[:, p, :], in0=ps[:, p, 0:P], scalar=1.0 / (P * 16),
                                         in1=w("W"), op0=ALU.mult, op1=ALU.add).then_inc(weight_ready, 1)

            one(0, 0, True)
            one(1, 1, True)
            with dve.Fori(1, NB // 2) as i:
                one(i * 2, 0, False)
                one(i * 2 + 1, 1, False)

        @block.scalar
        def _(act):
            act.wait_ge(shift_ready, 1)
            with act.Fori(0, NB // 2) as i:
                for p in range(2):
                    b = i * 2 + p
                    act.wait_ge(y_done, b + 1)
                    act.activation(core.a[:, tok(b * P, P)], ps[:, 2 + p, 0:P], ACT.Gelu,
                                   bias=shift[:, tok(b, 1)]).then_inc(gelu_done, 1)


def attention_stage(core, name, steps, unroll, heads, cfg, next_load=None):
    nc, ps, const = core.nc, core.ps, core.const
    dh = P // heads
    per = 32 // dh
    batches = 4 // per
    nt = batches * P
    nh = batches * heads
    head_mask = const("head8" if dh == 8 else "head16")
    QKV, CTX = 6, 7
    with stage_scope(nc) as ctx:
        sb = lambda n, shape: ctx.enter_context(nc.sbuf_tensor(f"{name}_{n}", shape, F32))
        sem = lambda n: nc.alloc_semaphore(f"{name}_{n}")
        qm = sb("q_masked", [P, 2, per, nt])
        kt = sb("key", [P, 2, nt])
        span = heads * (dh + 1)
        vt = sb("value", [P, 2, batches, heads * (span + dh + 1)])
        e = sb("probs", [P, 2, 4, BANK])
        et = sb("probs_turned", [P, 4, BANK])
        mx = sb("row_max", [P, 2, 4])
        rs = sb("row_scale", [P, nh])
        o = sb("context", [P, nt])
        ot = sb("context_turned", [P, nt])
        s = {n: sem(n) for n in ["zero_ready", "ones_ready", "qk_done", "q_ready", "k_ready", "v_done", "v_ready",
                                 "scores_done", "max_ready", "scores_read", "exp_done", "turn_done", "turned_ready",
                                 "pv_done", "scale_ready", "context_ready", "ct_done", "ct_ready", "out_done",
                                 "out_read", "source_ready", "own"]}
        bufs = cfg(nc, ctx, s, name, qm, kt, ot)

        def own_columns(lo, hi):
            return vt[:, :, :, :].rearrange("q p b (h c) -> q p b h c", h=heads)[:, :, :, :, lo:hi]

        block = ctx.enter_context(nc.Block())
        loops = steps // unroll - 1
        assert (loops + 1) * unroll == steps and unroll >= 4

        def tiles(g):
            for t in range(4):
                bb, r = t // per, t % per
                yield t, bb, r, g * per + r

        def run(eng, body):
            for k in range(unroll):
                body(*(Step(0, k - d, unroll) if k >= d else None for d in range(4)))
            with eng.Fori(0, loops) as i:
                for k in range(unroll, 2 * unroll):
                    body(*(Step(i, k - d, unroll) for d in range(4)))
            for k in range(steps, steps + 3):
                body(*(Step(0, k - d, unroll) if k - d < steps else None for d in range(4)))

        @block.sync
        def _(sp):
            if next_load is not None:
                next_load(sp)

        @block.gpsimd
        def _(pool):
            pool.memset(vt[:, :, :, :], 0.0).then_inc(s["zero_ready"], 1)
            pool.wait_ge(s["zero_ready"], 1)
            for p in range(2):
                for bb in range(batches):
                    last = pool.memset(own_columns(dh, dh + 1)[:, p, bb], 1.0)
            last.then_inc(s["ones_ready"], 1)

            def body(a, m, c, t):
                if a is not None:
                    bufs["pool"](pool, a)

            run(pool, body)

        @block.tensor
        def _(pe):
            bufs["start"](pe)

            def project(st):
                past(pe, s["out_read"], st.n - 2)
                past(pe, s["v_ready"], st.n)
                bufs["pe_qk"](pe, st, QKV).then_inc(s["qk_done"], 1)

            def value(st):
                pe.wait_ge(s["q_ready"], st.n + 1)
                pe.wait_ge(s["k_ready"], st.n + 1)
                bufs["pe_v"](pe, st, QKV).then_inc(s["v_done"], 1)

            def scores(st, g):
                n, p = st.n, st.m % 2
                past(pe, s["scores_read"], n * 4 + (g - 3))
                bias = bufs.get("bias")
                if bias is not None:
                    bias(pe, ps[:, g, :].rearrange("p (t j) -> p t j", t=4), g)
                for t, bb, r, h in tiles(g):
                    last = pe.matmul(ps[:, g, t * P:(t + 1) * P], qm[32 * g:32 * g + 32, p, r, bb * P:(bb + 1) * P],
                                     kt[32 * g:32 * g + 32, p, bb * P:(bb + 1) * P],
                                     start=bias is None, stop=True, skip_group_check=bias is not None)
                last.then_inc(s["scores_done"], 1)

            def turn(st, g):
                n, p = st.n, st.m % 2
                pe.wait_ge(s["exp_done"], n * 4 + (g + 1))
                past(pe, s["turned_ready"], n * 4 + (g - 1))
                for t in range(4):
                    last = pe.transpose(ps[:, 4 + g % 2, t * P:(t + 1) * P], e[:, p, g, t * P:(t + 1) * P],
                                        const("ident"))
                last.then_inc(s["turn_done"], 1)

            def context(st, g):
                n, p = st.n, st.m % 2
                pe.wait_ge(s["turned_ready"], n * 4 + (g + 1))
                if g == 0:
                    pe.wait_ge(s["v_ready"], n + 1)
                    past(pe, s["context_ready"], n)
                for t, bb, r, h in tiles(g):
                    last = pe.matmul(ps[:, CTX, bb * span:(bb + 1) * span], et[:, g, t * P:(t + 1) * P],
                                     vt[:, p, bb, h * span:(h + 1) * span], start=(g == 0 and t == 0),
                                     stop=(g == 3), skip_group_check=True)
                last.then_inc(s["pv_done"], 1)

            def turn_context(st, newest):
                pe.wait_ge(s["context_ready"], st.n + 1)
                if newest is not None:
                    pe.wait_ge(s["v_ready"], newest.n + 1)
                for bb in range(batches):
                    last = pe.transpose(ps[:, QKV, bb * P:(bb + 1) * P], o[:, bb * P:(bb + 1) * P], const("ident"))
                last.then_inc(s["ct_done"], 1)

            def output(st):
                pe.wait_ge(s["ct_ready"], st.n + 1)
                bufs["pe_out"](pe, st, QKV).then_inc(s["out_done"], 1)

            def body(a, m, c, t):
                for g in range(4):
                    if c is not None:
                        turn(c, g)
                    if g == 3 and a is not None:
                        project(a)
                    if m is not None:
                        scores(m, g)
                    if g == 1 and t is not None:
                        turn_context(t, m)
                    if g >= 1 and c is not None:
                        context(c, g - 1)
                    if g == 2 and t is not None:
                        output(t)
                if c is not None:
                    context(c, 3)
                if a is not None:
                    value(a)

            run(pe, body)

        @block.scalar
        def _(act):
            bufs["start"](act)
            act.wait_ge(s["ones_ready"], 1)

            def value(st):
                act.wait_ge(s["v_done"], st.n + 1)
                past(act, s["pv_done"], st.n * 4 - 4)
                act.activation(own_columns(0, dh)[:, st.m % 2], ps[:, QKV, 0:nt].rearrange(
                    "p (b h d) -> p b h d", b=batches, d=dh), ACT.Copy).then_inc(s["v_ready"], 1)

            def exps(st, g):
                act.wait_ge(s["scores_read"], st.n * 4 + (g + 1))
                act.activation(e[:, st.m % 2, g, :], e[:, st.m % 2, g, :], ACT.Exp).then_inc(s["exp_done"], 1)

            def turned(st, g):
                act.wait_ge(s["turn_done"], st.n * 4 + (g + 1))
                past(act, s["pv_done"], st.n * 4 + (g - 3))
                act.activation(et[:, g, :], ps[:, 4 + g % 2, :], ACT.Copy).then_inc(s["turned_ready"], 1)

            def context(st):
                act.wait_ge(s["ct_done"], st.n + 1)
                past(act, s["out_done"], st.n)
                act.activation(ot[:, :], ps[:, QKV, 0:nt], ACT.Identity, bias=bufs["bv"](st.m)).then_inc(
                    s["ct_ready"], 1)

            def body(a, m, c, t):
                for g in range(4):
                    if c is not None:
                        turned(c, g)
                    if g == 0 and m is not None:
                        value(m)
                    if g == 1 and t is not None:
                        context(t)
                    if g == 3 and a is not None and "act_k" in bufs:
                        bufs["act_k"](act, a, QKV)
                    if g >= 1 and m is not None:
                        exps(m, g - 1)
                if m is not None:
                    exps(m, 3)

            run(act, body)

        @block.vector
        def _(dve):
            bufs["start"](dve)

            def softmax_in(st, g):
                n = st.n
                dve.wait_ge(s["scores_done"], n * 4 + (g + 1))
                bank = ps[:, g, :].rearrange("p (t j) -> p t j", t=4)
                past(dve, s["scores_read"], n * 4 + (g - 1))
                dve.tensor_reduce(mx[:, g % 2, :], bank, AX_X, ALU.max).then_inc(s["max_ready"], 1)
                dve.wait_ge(s["max_ready"], n * 4 + (g + 1))
                past(dve, s["turn_done"], n * 4 + (g - 7))
                dve.tensor_tensor(e[:, st.m % 2, g, :].rearrange("p (t j) -> p t j", t=4), bank,
                                  mx[:, g % 2, :].unsqueeze(2).broadcast_to([P, 4, P]), ALU.subtract).then_inc(
                    s["scores_read"], 1)

            def normalise(st):
                n = st.n
                dve.wait_ge(s["pv_done"], n * 4 + 4)
                ctx_ps = ps[:, CTX, 0:nh * (dh + 1)].rearrange("p (h d) -> p h d", d=dh + 1)
                past(dve, s["context_ready"], n)
                dve.reciprocal(rs[:, :], ctx_ps[:, :, dh]).then_inc(s["scale_ready"], 1)
                dve.wait_ge(s["scale_ready"], n + 1)
                past(dve, s["ct_done"], n)
                dve.tensor_tensor(o[:, :].rearrange("p (h d) -> p h d", d=dh), ctx_ps[:, :, 0:dh],
                                  rs[:, :].unsqueeze(2).broadcast_to([P, nh, dh]), ALU.mult).then_inc(
                    s["context_ready"], 1)

            def body(a, m, c, t):
                for g in range(4):
                    if g == 3 and t is not None:
                        dve.wait_ge(s["out_done"], t.n + 1)
                        bufs["dve_out"](dve, t, QKV).then_inc(s["out_read"], 1)
                    if g == 3 and a is not None:
                        bufs["dve_q"](dve, a, QKV, head_mask)
                    if m is not None:
                        softmax_in(m, g)
                if c is not None:
                    normalise(c)

            run(dve, body)


def plain_attention(core, k, with_bias):
    w, const, ps = core.pack(k), core.const, core.ps

    def cfg(nc, ctx, s, name, qm, kt, ot):
        src = ctx.enter_context(nc.sbuf_tensor(f"{name}_src", [P, 2, P], F32))
        zero = None if with_bias else ctx.enter_context(nc.sbuf_tensor(f"{name}_zero", [P, 1], F32))

        def start(eng):
            wait_pack(eng, core, k)
            if zero is not None:
                if eng is nc.vector:
                    eng.memset(zero[:, :], 0.0).then_inc(s["own"], 1)
                eng.wait_ge(s["own"], 1)

        def pool(pool, st):
            n, m = st.n, st.m
            past(pool, s["v_done"], n - 1)
            pool.tensor_copy(src[:, m % 2, :], core.a[:, tok(n * P, P)]).then_inc(s["source_ready"], 1)

        def pe_qk(pe, st, bank):
            n, m = st.n, st.m
            pe.wait_ge(s["source_ready"], n + 1)
            pe.matmul(ps[:, bank, 0:P], w("Wq"), src[:, m % 2, :], start=True, stop=True)
            return pe.matmul(ps[:, bank, P:2 * P], w("Wk"), src[:, m % 2, :], start=True, stop=True)

        def pe_v(pe, st, bank):
            n, m = st.n, st.m
            return pe.matmul(ps[:, bank, 0:P], src[:, m % 2, :], w("Wv"), start=True, stop=True)

        def pe_out(pe, st, bank):
            n, m = st.n, st.m
            return pe.matmul(ps[:, bank, P:2 * P], w("Wo"), ot[:, :], start=True, stop=True)

        bq, bk, bv, bo = [w(x) if with_bias else zero[:, :] for x in ("bq", "bk", "bv", "bo")]

        def act_k(act, st, bank):
            n, m = st.n, st.m
            act.wait_ge(s["q_ready"], n + 1)
            act.activation(kt[:, m % 2, :], ps[:, bank, P:2 * P], ACT.Identity, bias=bk).then_inc(s["k_ready"], 1)

        def dve_q(dve, st, bank, head_mask):
            n, m = st.n, st.m
            dve.wait_ge(s["qk_done"], n + 1)
            dve.scalar_tensor_tensor(out=qm[:, m % 2, :, :], in0=ps[:, bank, 0:P].unsqueeze(1).broadcast_to([P, 4, P]),
                                     scalar=bq, in1=head_mask.unsqueeze(2).broadcast_to([P, 4, P]),
                                     op0=ALU.add, op1=ALU.mult).then_inc(s["q_ready"], 1)

        def dve_out(dve, st, bank):
            n, m = st.n, st.m
            xb = core.x[:, tok(n * P, P)]
            return dve.scalar_tensor_tensor(out=xb, in0=ps[:, bank, P:2 * P], scalar=bo, in1=xb,
                                            op0=ALU.add, op1=ALU.add)

        cfg_out = dict(start=start, pool=pool, pe_qk=pe_qk, pe_v=pe_v, pe_out=pe_out, act_k=act_k, dve_q=dve_q,
                       dve_out=dve_out, bv=lambda m: bv)
        if with_bias:
            def bias(pe, out, g):
                pe.matmul(out, const("ident"), w("rel", g * BANK, BANK).rearrange("p (t j) -> p t j", t=4), start=True,
                          stop=False, skip_group_check=True)

            cfg_out["bias"] = bias
        return cfg_out

    return cfg


AHEAD = 4
UNROLL_T = 8


def positions(tile, t, n=1):
    return tile[:, :].rearrange("p (b t) -> p t b", t=P)[:, bass.ds(t, n), :]


def time_loop(eng, step):
    for k in range(UNROLL_T):
        step(k, k)
    with eng.Fori(0, P // UNROLL_T - 2) as i:
        for k in range(UNROLL_T):
            step(i * UNROLL_T + (UNROLL_T + k), k)
    for k in range(UNROLL_T):
        step(P - UNROLL_T + k, k)


def in_group(bank, k, gates=1):
    return bank[:, 0:gates * AHEAD * NB].rearrange("p (g t b) -> p g t b", g=gates, t=AHEAD)[:, :, k % AHEAD, :]


def lstm_stage(core, name, k, next_load=None):
    nc, w, ps, const = core.nc, core.pack(k), core.ps, core.const
    PLACE = [(0, 0), (0, 1), (2, 0), (0, 2)]
    WIDE = AHEAD * NB
    with stage_scope(nc) as ctx:
        sb = lambda n, shape: ctx.enter_context(nc.sbuf_tensor(f"{name}_{n}", shape, F32))
        sem = lambda n: nc.alloc_semaphore(f"{name}_{n}")
        sig = sb("sig", [P, 2, NB])
        og = sb("output_gate", [P, 1, NB])
        cand = sb("cand", [P, NB])
        c = sb("c", [P, NB])
        ic = sb("ic", [P, NB])
        fc = sb("fc", [P, NB])
        tc = sb("tc", [P, 1, NB])
        z_done, o_done, sig_ready, cand_ready, o_ready, c_ready, tc_ready, h_ready, parts, c_set = map(
            sem, ["z_done", "o_done", "sig_ready", "cand_ready", "o_ready", "c_ready", "tc_ready", "h_ready", "parts",
                  "c_set"])
        block = ctx.enter_context(nc.Block())

        @block.sync
        def _(sp):
            if next_load is not None:
                next_load(sp)

        @block.tensor
        def _(pe):
            wait_pack(pe, core, k)

            def pre(base, parity, g):
                first, at = PLACE[g]
                out = ps[:, first + parity, at * WIDE:(at + 1) * WIDE].rearrange("p (t b) -> p t b", t=AHEAD)
                pe.matmul(out, w("b", rows=4), const("gate_pick", g * NB, NB, rows=4).unsqueeze(1).broadcast_to(
                    [4, AHEAD, NB]), start=(at == 0), stop=False, skip_group_check=True)
                pe.matmul(out, w("Wx", g * P, P), positions(core.x, base, AHEAD), start=False, stop=False,
                          skip_group_check=True)

            def step(t, k):
                past(pe, h_ready, t)
                state = const("cond").unsqueeze(1) if isinstance(t, int) and t == 0 else positions(core.a, t - 1)
                parity = k // AHEAD % 2
                for g in (0, 1, 3, 2):
                    first, at = PLACE[g]
                    lo = at * WIDE + k % AHEAD * NB
                    last = pe.matmul(ps[:, first + parity, lo:lo + NB].unsqueeze(1), w("Wh", g * P, P), state,
                                     start=False, stop=True, skip_group_check=True)
                    if g == 3:
                        last.then_inc(z_done, 1)
                last.then_inc(o_done, 1)
                if not isinstance(t, int) or t < P - AHEAD:
                    pre(t + (AHEAD - k % AHEAD), 1 - parity, k % AHEAD)

            for g in range(4):
                pre(0, 0, g)
            time_loop(pe, step)

        @block.scalar
        def _(act):
            def step(t, k):
                bank = k // AHEAD % 2
                act.wait_ge(z_done, t + 1)
                gates = in_group(ps[:, bank, :], k, 3)
                act.activation(sig[:, :, :], gates[:, 0:2, :], ACT.Sigmoid).then_inc(sig_ready, 1)
                act.activation(cand[:, :].unsqueeze(1), gates[:, 2:3, :], ACT.Tanh).then_inc(cand_ready, 1)
                act.wait_ge(o_done, t + 1)
                act.activation(og[:, :, :], in_group(ps[:, 2 + bank, :], k), ACT.Sigmoid).then_inc(o_ready, 1)
                act.wait_ge(c_ready, t + 1)
                act.activation(tc[:, 0, :], c[:, :], ACT.Tanh).then_inc(tc_ready, 1)

            time_loop(act, step)

        @block.vector
        def _(dve):
            dve.memset(c[:, :], 0.0).then_inc(c_set, 1)
            dve.wait_ge(c_set, 1)

            def step(t, k):
                dve.wait_ge(sig_ready, t + 1)
                past(dve, c_ready, t)
                dve.tensor_tensor(fc[:, :], c[:, :], sig[:, 1, :], ALU.mult).then_inc(parts, 1)
                dve.wait_ge(cand_ready, t + 1)
                dve.tensor_tensor(ic[:, :], cand[:, :], sig[:, 0, :], ALU.mult).then_inc(parts, 1)
                dve.wait_ge(parts, t * 2 + 2)
                dve.tensor_tensor(c[:, :], fc[:, :], ic[:, :], ALU.add).then_inc(c_ready, 1)
                dve.wait_ge(o_ready, t + 1)
                dve.wait_ge(tc_ready, t + 1)
                dve.tensor_tensor(positions(core.a, t), tc[:, :, :], og[:, :, :], ALU.mult).then_inc(h_ready, 1)

            time_loop(dve, step)


def leaky_stage(core, next_load=None):
    nc, w, ps, const = core.nc, core.pack(1), core.ps, core.const
    with stage_scope(nc) as ctx:
        sb = lambda n, shape: ctx.enter_context(nc.sbuf_tensor(f"leaky_{n}", shape, F32))
        sem = lambda n: nc.alloc_semaphore(f"leaky_{n}")
        gate = sb("gate", [P, 1, NB])
        gz = sb("gz", [P, 1, NB])
        pre_act = sb("pre_act", [P, 1, NB])
        leak = sb("leak", [P, 1])
        z_done, gate_ready, gz_ready, mixed, h_ready, leak_ready = map(
            sem, ["z_done", "gate_ready", "gz_ready", "mixed", "h_ready", "leak_ready"])
        block = ctx.enter_context(nc.Block())

        def state(t):
            return const("cond").unsqueeze(1) if isinstance(t, int) and t == 0 else positions(core.a, t - 1)

        @block.sync
        def _(sp):
            if next_load is not None:
                next_load(sp)

        @block.tensor
        def _(pe):
            wait_pack(pe, core, 1)

            def pre(base, parity):
                pe.matmul(ps[:, parity, 0:AHEAD * NB].rearrange("p (t b) -> p t b", t=AHEAD), w("WzT"),
                          positions(core.x, base, AHEAD), start=True, stop=False, skip_group_check=True)

            def step(t, k):
                parity, lo = k // AHEAD % 2, k % AHEAD * NB
                past(pe, h_ready, t)
                pe.matmul(ps[:, parity, lo:lo + NB].unsqueeze(1), w("WhT"), state(t), start=False, stop=True,
                          skip_group_check=True).then_inc(z_done, 1)
                if k % AHEAD == 0 and (not isinstance(t, int) or t < P - AHEAD):
                    pre(t + AHEAD, 1 - parity)

            pre(0, 0)
            time_loop(pe, step)

        @block.scalar
        def _(act):
            wait_pack(act, core, 1)

            def step(t, k):
                act.wait_ge(z_done, t + 1)
                act.activation(gate[:, :, :], in_group(ps[:, k // AHEAD % 2, :], k), ACT.Sigmoid,
                               bias=w("b")).then_inc(gate_ready, 1)
                act.wait_ge(mixed, t + 1)
                act.activation(positions(core.a, t), pre_act[:, :, :], ACT.Tanh).then_inc(h_ready, 1)

            time_loop(act, step)

        @block.vector
        def _(dve):
            wait_pack(dve, core, 1)
            dve.tensor_scalar(leak[:, :], w("alpha"), -1.0, 1.0, ALU.mult, ALU.add).then_inc(leak_ready, 1)
            dve.wait_ge(leak_ready, 1)

            def step(t, k):
                dve.wait_ge(gate_ready, t + 1)
                dve.tensor_tensor(gz[:, :, :], gate[:, :, :], positions(core.x, t), ALU.mult).then_inc(gz_ready, 1)
                dve.wait_ge(gz_ready, t + 1)
                past(dve, h_ready, t)
                dve.scalar_tensor_tensor(out=pre_act[:, :, :], in0=state(t), scalar=leak[:, :], in1=gz[:, :, :],
                                         op0=ALU.mult, op1=ALU.add).then_inc(mixed, 1)

            time_loop(dve, step)


def gru_stage(core, next_load=None):
    nc, w, ps, const = core.nc, core.pack(5), core.ps, core.const
    with stage_scope(nc) as ctx:
        sb = lambda n, shape: ctx.enter_context(nc.sbuf_tensor(f"gru_{n}", shape, F32))
        sem = lambda n: nc.alloc_semaphore(f"gru_{n}")
        start_state = sb("start_state", [P, 1, NB])
        r, z, rh, cand, zh, rest, zc = (sb(n, [P, 1, NB]) for n in ("r", "z", "rh", "cand", "zh", "rest", "zc"))
        (r_done, z_done, cand_done, r_ready, z_ready, rh_ready, cand_ready, zh_ready, rest_ready, zc_ready, h_ready,
         zeroed) = map(sem, ["r_done", "z_done", "cand_done", "r_ready", "z_ready", "rh_ready", "cand_ready",
                             "zh_ready", "rest_ready", "zc_ready", "h_ready", "zeroed"])
        block = ctx.enter_context(nc.Block())
        R, Z, CAND = 0, 2, 4

        def state(t):
            return start_state[:, :, :] if isinstance(t, int) and t == 0 else positions(core.a, t - 1)

        @block.sync
        def _(sp):
            if next_load is not None:
                next_load(sp)

        @block.tensor
        def _(pe):
            wait_pack(pe, core, 5)
            pe.wait_ge(zeroed, 1)

            def pre(base, parity, which):
                bank, x_w, c_w = ((R, "Wr", "Cr"), (Z, "Wz", "Cz"), (CAND, "W", "C"))[which]
                out = ps[:, bank + parity, 0:AHEAD * NB].rearrange("p (t b) -> p t b", t=AHEAD)
                pe.matmul(out, w(c_w), const("cond").unsqueeze(1).broadcast_to([P, AHEAD, NB]), start=True,
                          stop=False, skip_group_check=True)
                pe.matmul(out, w(x_w), positions(core.x, base, AHEAD), start=False, stop=False,
                          skip_group_check=True)

            def step(t, k):
                parity, lo = k // AHEAD % 2, k % AHEAD * NB

                def rec(bank, weight, moving):
                    return pe.matmul(ps[:, bank + parity, lo:lo + NB].unsqueeze(1), w(weight), moving, start=False,
                                     stop=True, skip_group_check=True)

                past(pe, h_ready, t)
                rec(R, "Ur", state(t)).then_inc(r_done, 1)
                rec(Z, "Uz", state(t)).then_inc(z_done, 1)
                pe.wait_ge(rh_ready, t + 1)
                rec(CAND, "U", rh[:, :, :]).then_inc(cand_done, 1)
                if k % AHEAD < 3 and (not isinstance(t, int) or t < P - AHEAD):
                    pre(t + (AHEAD - k % AHEAD), 1 - parity, k % AHEAD)

            for which in range(3):
                pre(0, 0, which)
            time_loop(pe, step)

        @block.scalar
        def _(act):
            wait_pack(act, core, 5)

            def step(t, k):
                bank = k // AHEAD % 2
                act.wait_ge(r_done, t + 1)
                act.activation(r[:, :, :], in_group(ps[:, R + bank, :], k), ACT.Sigmoid, bias=w("br")).then_inc(
                    r_ready, 1)
                act.wait_ge(z_done, t + 1)
                act.activation(z[:, :, :], in_group(ps[:, Z + bank, :], k), ACT.Sigmoid, bias=w("bz")).then_inc(
                    z_ready, 1)
                act.wait_ge(cand_done, t + 1)
                act.activation(cand[:, :, :], in_group(ps[:, CAND + bank, :], k), ACT.Tanh, bias=w("b")).then_inc(
                    cand_ready, 1)

            time_loop(act, step)

        @block.vector
        def _(dve):
            dve.memset(start_state[:, :, :], 0.0).then_inc(zeroed, 1)
            dve.wait_ge(zeroed, 1)

            def step(t, k):
                dve.wait_ge(r_ready, t + 1)
                past(dve, h_ready, t)
                dve.tensor_tensor(rh[:, :, :], r[:, :, :], state(t), ALU.mult).then_inc(rh_ready, 1)
                dve.wait_ge(z_ready, t + 1)
                dve.tensor_tensor(zh[:, :, :], z[:, :, :], state(t), ALU.mult).then_inc(zh_ready, 1)
                dve.wait_ge(zh_ready, t + 1)
                dve.tensor_tensor(rest[:, :, :], state(t), zh[:, :, :], ALU.subtract).then_inc(rest_ready, 1)
                dve.wait_ge(cand_ready, t + 1)
                dve.tensor_tensor(zc[:, :, :], cand[:, :, :], z[:, :, :], ALU.mult).then_inc(zc_ready, 1)
                dve.wait_ge(rest_ready, t + 1)
                dve.wait_ge(zc_ready, t + 1)
                dve.tensor_tensor(positions(core.a, t), zc[:, :, :], rest[:, :, :], ALU.add).then_inc(h_ready, 1)

            time_loop(dve, step)


def norm_stage(core, name, k, src, dst, m, lhs, mean, eps, gamma=None, beta=None, add_to=None, prepare=None):
    nc, ps, const = core.nc, core.ps, core.const
    with stage_scope(nc) as ctx:
        sb = lambda n, shape: ctx.enter_context(nc.sbuf_tensor(f"{name}_{n}", shape, F32))
        sem = lambda n: nc.alloc_semaphore(f"{name}_{n}")
        xc = sb("centred", [m, 2, CHUNK])
        sq = sb("square", [m, 2, CHUNK])
        sd = sb("deviation", [m, 2, CHUNK])
        inv = sb("inverse", [m, 2, CHUNK])
        s = {n: sem(n) for n in ["centred_done", "centred_ready", "square_ready", "var_done", "sd_ready", "inv_ready",
                                 "norm_ready", "scaled", "written", "prepared"]}
        block = ctx.enter_context(nc.Block())

        def pairs(eng, one):
            one(0, 0)
            one(1, 1)
            with eng.Fori(1, NCHUNK // 2) as i:
                one(i * 2, 0)
                one(i * 2 + 1, 1)

        @block.tensor
        def _(pe):
            wait_pack(pe, core, k)
            if prepare is not None:
                prepare["pe"](pe, s)

            def centre(c, p):
                past(pe, s["centred_ready"], c - 1)
                pe.matmul(ps[0:m, p, :], lhs, src[:, tok(c * CHUNK, CHUNK)], start=True, stop=True).then_inc(
                    s["centred_done"], 1)

            def variance(c, p):
                pe.wait_ge(s["square_ready"], c + 1)
                past(pe, s["sd_ready"], c - 1)
                pe.matmul(ps[:, 2 + p, :], mean, sq[:, p, :], start=True, stop=True).then_inc(s["var_done"], 1)

            def two(c):
                centre(c, 0)
                centre(c + 1, 1)
                variance(c, 0)
                variance(c + 1, 1)

            two(0)
            with pe.Fori(1, NCHUNK // 2) as i:
                two(i * 2)

        @block.scalar
        def _(act):
            if prepare is not None:
                prepare["act"](act, s)

            def two(c):
                for p in range(2):
                    act.wait_ge(s["centred_done"], c + p + 1)
                    past(act, s["norm_ready"], c + p - 1)
                    act.activation(xc[:, p, :], ps[0:m, p, :], ACT.Copy).then_inc(s["centred_ready"], 1)
                for p in range(2):
                    act.wait_ge(s["var_done"], c + p + 1)
                    past(act, s["inv_ready"], c + p - 1)
                    act.activation(sd[:, p, :], ps[0:m, 2 + p, :], ACT.Sqrt, bias=eps[0:m, :]).then_inc(
                        s["sd_ready"], 1)

            two(0)
            with act.Fori(1, NCHUNK // 2) as i:
                two(i * 2)

        @block.gpsimd
        def _(pool):
            def one(c, p):
                pool.wait_ge(s["centred_ready"], c + 1)
                past(pool, s["var_done"], c - 1)
                pool.tensor_tensor(sq[:, p, :], xc[:, p, :], xc[:, p, :], ALU.mult).then_inc(s["square_ready"], 1)

            pairs(pool, one)

        @block.vector
        def _(dve):
            def one(c, p):
                dve.wait_ge(s["sd_ready"], c + 1)
                past(dve, s["norm_ready"], c - 1)
                dve.reciprocal(inv[:, p, :], sd[:, p, :]).then_inc(s["inv_ready"], 1)
                dve.wait_ge(s["inv_ready"], c + 1)
                if gamma is None:
                    dve.tensor_tensor(dst[0:m, tok(c * CHUNK, CHUNK)], xc[:, p, :], inv[:, p, :],
                                      ALU.mult).then_inc(s["norm_ready"], 1)
                    return
                dve.scalar_tensor_tensor(out=xc[:, p, :], in0=xc[:, p, :], scalar=gamma, in1=inv[:, p, :],
                                         op0=ALU.mult, op1=ALU.mult).then_inc(s["scaled"], 1)
                dve.wait_ge(s["scaled"], c + 1)
                out = dst[0:m, tok(c * CHUNK, CHUNK)]
                if add_to is None:
                    dve.tensor_scalar(out, xc[:, p, :], beta, None, ALU.add).then_inc(s["norm_ready"], 1)
                else:
                    dve.scalar_tensor_tensor(out=out, in0=xc[:, p, :], scalar=beta,
                                             in1=add_to[0:m, tok(c * CHUNK, CHUNK)], op0=ALU.add,
                                             op1=ALU.add).then_inc(s["norm_ready"], 1)

            pairs(dve, one)


class Chain:

    def __init__(self, dve, sem):
        self.dve, self.sem, self.n = dve, sem, 0

    def __call__(self, ins):
        self.n += 1
        ins.then_inc(self.sem, 1)
        self.dve.wait_ge(self.sem, self.n)


def pick_first_best(dve, link, values, tie, ne, best, hot, n=NB):
    link(dve.tensor_reduce(best, values, AX_X, ALU.max))
    link(dve.tensor_tensor(hot, values, best.unsqueeze(2).broadcast_to([P, n, ne]), ALU.is_equal))
    link(dve.tensor_tensor(hot, hot, tie.unsqueeze(1).broadcast_to([P, n, ne]), ALU.mult))
    link(dve.tensor_reduce(best, hot, AX_X, ALU.max))
    link(dve.tensor_tensor(hot, hot, best.unsqueeze(2).broadcast_to([P, n, ne]), ALU.is_equal))


def router_stage(core, name, k, src, ne, router, gate_fn, gates, extra=None, act_fn=None, pe_first=None, next_load=None):
    nc, ps = core.nc, core.ps
    with stage_scope(nc) as ctx:
        sb = lambda n, shape: ctx.enter_context(nc.sbuf_tensor(f"{name}_{n}", shape, F32))
        sem = lambda n: nc.alloc_semaphore(f"{name}_{n}")
        logits_done, own, act_done, dve_ready = map(sem, ["logits_done", "own", "act_done", "dve_ready"])
        bufs = extra(sb, sem) if extra is not None else {}
        block = ctx.enter_context(nc.Block())

        @block.sync
        def _(sp):
            if next_load is not None:
                next_load(sp)

        @block.gpsimd
        def _(pool):
            if "pool" in bufs:
                bufs["pool"](pool)

        @block.tensor
        def _(pe):
            wait_pack(pe, core, k)
            rhs = router(bufs)
            if pe_first is not None:
                pe_first(pe, bufs)
            for t in range(NB):
                out = ps[:, 0, t * ne:(t + 1) * ne]
                more = "second" in bufs
                last = pe.matmul(out, src[:, t * P:(t + 1) * P], rhs, start=True, stop=not more)
                if more:
                    last = pe.matmul(out, core.b[:, t * P:(t + 1) * P], bufs["second"], start=False, stop=True)
            last.then_inc(logits_done, 1)

        @block.scalar
        def _(act):
            if act_fn is not None:
                act_fn(act, ps, logits_done, act_done, dve_ready, bufs)

        @block.vector
        def _(dve):
            wait_pack(dve, core, k)
            link = Chain(dve, own)
            logits = ps[:, 0, 0:NB * ne].rearrange("p (t e) -> p t e", e=ne)
            gate_fn(dve, link, logits, gates, logits_done, act_done, dve_ready, bufs, sb)


def expert_stage(core, name, k, ne, gates, hidden, out_rhs, depth, rows_of, b2=None, shared=None, finish=None,
                 next_load=None, setup=None, n_hidden=None):
    nc, ps, const = core.nc, core.ps, core.const
    nj = n_hidden
    slots = 2 * max(depth, 1) if depth > 1 else 3
    with stage_scope(nc) as ctx:
        sb = lambda n, shape: ctx.enter_context(nc.sbuf_tensor(f"{name}_{n}", shape, F32))
        sem = lambda n: nc.alloc_semaphore(f"{name}_{n}")
        hs = sb("hidden", [P, slots, CHUNK])
        acc = sb("acc", [P, 4, P])
        g = sb("gate", [P, 4, ne])
        gt = sb("gate_turned", [ne, 4, P])
        s = {n: sem(n) for n in ["g_ready", "gt_done", "gt_ready", "init_done", "h_done", "h_ready", "y_done",
                                 "y_added", "sum_turned", "stored", "used"]}
        bufs = setup(sb, sem, s) if setup is not None else {}
        block = ctx.enter_context(nc.Block())

        def chunks(eng, one):
            one(0)
            with eng.Fori(1, NCHUNK) as c:
                one(c)

        first_tile = lambda e: rows_of(e)[0]

        @block.sync
        def _(sp):
            if next_load is not None:
                next_load(sp)

        @block.gpsimd
        def _(pool):
            def one(c):
                past(pool, s["y_added"], c * ne)
                pool.tensor_copy(g[:, :, :], gates[:, bass.ds(c * 4, 4), :]).then_inc(s["g_ready"], 1)
                if "pool" in hidden:
                    hidden["pool"](pool, c, bufs)

            chunks(pool, one)

        @block.tensor
        def _(pe):
            wait_pack(pe, core, k)

            def hidden_tile(c, j):
                if "pe" not in hidden:
                    return
                past(pe, s["h_ready"], c * nj + (j - 1))
                hidden["pe"](pe, c, j, j % 2, bufs).then_inc(s["h_done"], 1)

            def one(c):
                if "pe_first" in hidden:
                    hidden["pe_first"](pe, c, bufs)
                if b2 is not None:
                    pe.wait_ge(s["g_ready"], c + 1)
                    past(pe, s["stored"], c)
                    for t in range(4):
                        last = pe.transpose(ps[0:ne, 4, t * P:(t + 1) * P], g[:, t, :], const("ident"))
                    last.then_inc(s["gt_done"], 1)
                    pe.wait_ge(s["gt_ready"], c + 1)
                    past(pe, s["used"], c)
                    for t in range(4):
                        last = pe.matmul(ps[:, 5, t * P:(t + 1) * P], gt[:, t, :], b2, start=True, stop=True)
                    last.then_inc(s["init_done"], 1)
                else:
                    past(pe, s["used"], c)
                    shared["pe"](pe, c, bufs).then_inc(s["init_done"], 1)
                sent = 0
                for e in range(ne):
                    tile, lo, n = rows_of(e)
                    ahead = min(nj, tile + 2 * depth) if depth > 1 else min(nj, tile + 2)
                    while sent < ahead:
                        hidden_tile(c, sent)
                        sent += 1
                    past(pe, s["y_added"], c * ne + (e - 1))
                    pe.wait_ge(s["h_ready"], c * nj + (tile + depth))
                    for t in range(4):
                        for f in range(depth):
                            last = pe.matmul(ps[:, 2 + e % 2, t * P:(t + 1) * P],
                                             hs[lo:lo + n, (tile + f) % slots, t * P:(t + 1) * P],
                                             out_rhs(e, f, lo, n), start=(f == 0), stop=(f == depth - 1))
                    last.then_inc(s["y_done"], 1)
                pe.wait_ge(s["y_added"], c * ne + ne)
                past(pe, s["stored"], c)
                for t in range(4):
                    last = pe.transpose(ps[:, 4, t * P:(t + 1) * P], acc[:, t, :], const("ident"))
                last.then_inc(s["sum_turned"], 1)

            chunks(pe, one)

        @block.scalar
        def _(act):
            wait_pack(act, core, k)
            users = [max([e for e in range(ne) if first_tile(e) <= j < first_tile(e) + depth]) for j in range(nj)]

            def one(c):
                if "act_first" in hidden:
                    hidden["act_first"](act, c, bufs)
                if b2 is not None:
                    act.wait_ge(s["gt_done"], c + 1)
                    past(act, s["init_done"], c)
                    act.activation(gt[:, :, :], ps[0:ne, 4, :].rearrange("p (t j) -> p t j", t=4),
                                   ACT.Copy).then_inc(s["gt_ready"], 1)
                for j in range(nj):
                    if "pe" in hidden:
                        act.wait_ge(s["h_done"], c * nj + (j + 1))
                    if j >= slots:
                        act.wait_ge(s["y_done"], c * ne + (users[j - slots] + 1))
                    else:
                        past(act, s["y_done"], c * ne)
                    hidden["act"](act, c, j, j % 2, hs[:, j % slots, :], bufs).then_inc(s["h_ready"], 1)

            chunks(act, one)

        @block.vector
        def _(dve):
            wait_pack(dve, core, k)

            def one(c):
                if "dve_first" in hidden:
                    hidden["dve_first"](dve, c, bufs)
                dve.wait_ge(s["init_done"], c + 1)
                past(dve, s["sum_turned"], c)
                dve.tensor_copy(acc[:, :, :], ps[:, 5, :].rearrange("p (t j) -> p t j", t=4)).then_inc(s["used"], 1)
                dve.wait_ge(s["g_ready"], c + 1)
                for e in range(ne):
                    dve.wait_ge(s["y_done"], c * ne + (e + 1))
                    dve.wait_ge(s["used"], c + 1)
                    past(dve, s["y_added"], c * ne + e)
                    for t in range(4):
                        last = dve.scalar_tensor_tensor(out=acc[:, t, :], in0=ps[:, 2 + e % 2, t * P:(t + 1) * P],
                                                        scalar=g[:, t, e:e + 1], in1=acc[:, t, :], op0=ALU.mult,
                                                        op1=ALU.add)
                    last.then_inc(s["y_added"], 1)
                dve.wait_ge(s["sum_turned"], c + 1)
                finish(dve, c, ps[:, 4, :]).then_inc(s["stored"], 1)

            chunks(dve, one)


def layer0_gates(core):
    def extra(sb, sem):
        return dict(lg=sb("scores", [P, NB, 8]), best=sb("best", [P, NB]))

    def gate_fn(dve, link, logits, gates, logits_done, act_done, dve_ready, bufs, sb):
        dve.wait_ge(logits_done, 1)
        link(dve.tensor_copy(bufs["lg"][:, :, :], logits))
        pick_first_best(dve, link, bufs["lg"][:, :, :], core.const("tie8"), 8, bufs["best"][:, :], gates)

    return extra, gate_fn


def layer0_expert_stage(core):
    nc, w, ps, const = core.nc, core.pack(1), core.ps, core.const
    NE, TILES, PER = 8, 2, 4
    GATE, OUT = 2, 4
    gates = core.gate(NE)
    with stage_scope(nc) as ctx:
        sb = lambda n, shape: ctx.enter_context(nc.sbuf_tensor(f"experts0_{n}", shape, F32))
        sem = lambda n: nc.alloc_semaphore("experts0_" + n)
        w1, b1 = sb("w1_scaled", [P, 256]), sb("b1_full", [P, 2])
        hidden = sb("hidden", [P, 2, TILES, CHUNK])
        scaled = sb("scaled", [P, 2, TILES, CHUNK])
        s = {n: sem(n) for n in ["folded", "shifted", "gates_turned", "gates_kept", "h_done", "g_done", "h_ready",
                                 "scaled_ready", "out_done", "stored"]}
        block = ctx.enter_context(nc.Block())

        def run(eng, body):
            body((0, 0), None)
            body((1, 1), (0, 0))
            with eng.Fori(1, NCHUNK // 2) as i:
                body((i * 2, 0), (i * 2 - 1, 1))
                body((i * 2 + 1, 1), (i * 2, 0))
            body(None, (NCHUNK - 1, 1))

        def turned(c):
            return core.a[0:NE, tok(c * CHUNK, CHUNK)]

        @block.tensor
        def _(pe):
            wait_pack(pe, core, 1)
            for e in range(NE):
                lo = 32 * (e % PER)
                last = pe.matmul(ps[lo:lo + 32, 7, e // PER:e // PER + 1], w("W1", e * 32, 32), w("ln_bias", e, 1),
                                 start=True, stop=True)
            last.then_inc(s["shifted"], 1)
            for c in range(NCHUNK):
                past(pe, s["gates_kept"], c - 1)
                for t in range(4):
                    last = pe.transpose(ps[0:NE, 4 + c % 2, t * P:(t + 1) * P], gates[:, c * 4 + t, :],
                                        const("ident"))
                last.then_inc(s["gates_turned"], 1)
            pe.wait_ge(s["folded"], NE + 1)
            pe.wait_ge(s["gates_kept"], NCHUNK)

            def body(a, b):
                if a is not None:
                    c, p = a
                    for j in range(TILES):
                        past(pe, s["h_ready"], c * 2 + (j - 1))
                        past(pe, s["scaled_ready"], c * 2 + (j - 1))
                        pe.matmul(ps[:, j, :], w1[:, j * P:(j + 1) * P], core.b[:, tok(c * CHUNK, CHUNK)], start=True,
                                  stop=True).then_inc(s["h_done"], 1)
                        pe.matmul(ps[:, GATE + j, :], const("spread8", j * P, P, rows=NE), turned(c), start=True,
                                  stop=True).then_inc(s["g_done"], 1)
                if b is not None:
                    c, p = b
                    past(pe, s["stored"], c - 1)
                    pe.wait_ge(s["scaled_ready"], c * 2 + 2)
                    for j in range(TILES):
                        pe.matmul(ps[:, OUT + p, :], w("W2", j * P, P), scaled[:, p, j, :], start=(j == 0), stop=False)
                    last = pe.matmul(ps[:, OUT + p, :], w("b2", rows=NE), turned(c), start=False, stop=True)
                    last.then_inc(s["out_done"], 1)

            run(pe, body)

        @block.scalar
        def _(act):
            for c in range(NCHUNK):
                act.wait_ge(s["gates_turned"], c + 1)
                act.activation(core.a[0:NE, c * CHUNK:(c + 1) * CHUNK], ps[0:NE, 4 + c % 2, :], ACT.Copy).then_inc(
                    s["gates_kept"], 1)
            act.wait_ge(s["folded"], NE + 1)

            def body(a, b):
                if a is not None:
                    c, p = a
                    for j in range(TILES):
                        act.wait_ge(s["h_done"], c * 2 + (j + 1))
                        past(act, s["scaled_ready"], c * 2 + (j - 3))
                        act.activation(hidden[:, p, j, :], ps[:, j, :], ACT.Gelu, bias=b1[:, j:j + 1]).then_inc(
                            s["h_ready"], 1)

            run(act, body)

        @block.vector
        def _(dve):
            wait_pack(dve, core, 1)
            for e in range(NE):
                dve.tensor_scalar(w1[:, e * 32:(e + 1) * 32], w("W1", e * 32, 32), w("ln_scale", e, 1), None,
                                  ALU.mult).then_inc(s["folded"], 1)
            dve.wait_ge(s["shifted"], 1)
            dve.tensor_tensor(b1[:, :], ps[:, 7, 0:2], w("b1"), ALU.add).then_inc(s["folded"], 1)

            def body(a, b):
                if a is not None:
                    c, p = a
                    for j in range(TILES):
                        dve.wait_ge(s["g_done"], c * 2 + (j + 1))
                        dve.wait_ge(s["h_ready"], c * 2 + (j + 1))
                        past(dve, s["out_done"], c - 1)
                        dve.tensor_tensor(scaled[:, p, j, :], hidden[:, p, j, :], ps[:, GATE + j, :],
                                          ALU.mult).then_inc(s["scaled_ready"], 1)
                if b is not None:
                    c, p = b
                    dve.wait_ge(s["out_done"], c + 1)
                    xs = core.x[:, tok(c * CHUNK, CHUNK)]
                    dve.tensor_tensor(xs, ps[:, OUT + p, :], xs, ALU.add).then_inc(s["stored"], 1)

            run(dve, body)


def add_to_x(core):
    def finish(dve, c, bank):
        xs = core.x[:, tok(c * CHUNK, CHUNK)]
        return dve.tensor_tensor(xs, bank, xs, ALU.add)

    return finish


def two_best(dve, link, core, values, work, tie, ne, best, hot, hot2):
    pick_first_best(dve, link, values, tie, ne, best, hot)
    link(dve.scalar_tensor_tensor(out=work, in0=hot, scalar=-1.0e30, in1=values, op0=ALU.mult, op1=ALU.add))
    pick_first_best(dve, link, work, tie, ne, best, hot2)
    link(dve.tensor_tensor(hot, hot, hot2, ALU.add))


def layer1_gates(core):
    w = core.pack(3)

    def extra(sb, sem):
        return dict(lg=sb("scores", [P, NB, 16]), best=sb("best", [P, NB]), work=sb("work", [P, NB, 16]),
                    hot=sb("hot", [P, NB, 16]), hot2=sb("hot2", [P, NB, 16]))

    def act_fn(act, ps, logits_done, act_done, dve_ready, bufs):
        act.wait_ge(dve_ready, 1)
        act.activation(bufs["lg"][:, :, :], bufs["lg"][:, :, :], ACT.Exp).then_inc(act_done, 1)

    def gate_fn(dve, link, logits, gates, logits_done, act_done, dve_ready, bufs, sb):
        lg, best, work, hot, hot2 = (bufs[n] for n in ("lg", "best", "work", "hot", "hot2"))
        wide = lambda: best[:, :].unsqueeze(2).broadcast_to([P, NB, 16])
        dve.wait_ge(logits_done, 1)
        link(dve.tensor_tensor(lg[:, :, :], logits, w("br").unsqueeze(1).broadcast_to([P, NB, 16]), ALU.add))
        link(dve.tensor_reduce(best[:, :], lg[:, :, :], AX_X, ALU.max))
        dve.tensor_tensor(lg[:, :, :], lg[:, :, :], wide(), ALU.subtract).then_inc(dve_ready, 1)
        dve.wait_ge(act_done, 1)
        link(dve.tensor_reduce(best[:, :], lg[:, :, :], AX_X, ALU.add))
        link(dve.reciprocal(best[:, :], best[:, :]))
        link(dve.tensor_tensor(lg[:, :, :], lg[:, :, :], wide(), ALU.mult))
        two_best(dve, link, core, lg[:, :, :], work[:, :, :], core.const("tie16"), 16, best[:, :], hot[:, :, :],
                 hot2[:, :, :])
        link(dve.tensor_tensor(gates, lg[:, :, :], hot[:, :, :], ALU.mult))
        link(dve.tensor_reduce(best[:, :], gates, AX_X, ALU.add))
        link(dve.tensor_scalar(best[:, :], best[:, :], 1.0e-9, None, ALU.max))
        link(dve.reciprocal(best[:, :], best[:, :]))
        link(dve.tensor_tensor(gates, gates, wide(), ALU.mult))

    return extra, gate_fn, act_fn


def layer1_expert_stage(core):
    nc, w, ps, const = core.nc, core.pack(3), core.ps, core.const
    NE, NQ = 16, 4
    TURN, OUT = 4, 6
    gates = core.gate(NE)
    with stage_scope(nc) as ctx:
        sb = lambda n, shape, t=F32: ctx.enter_context(nc.sbuf_tensor(f"experts1_{n}", shape, t))
        sem = lambda n: nc.alloc_semaphore("experts1_" + n)
        w1 = sb("w1_centred", [P, NE * P])
        b1_parts = sb("b1_parts", [P, 3, NE])
        b1_left = sb("b1_left", [P, 2, NE])
        b1_half = sb("b1_half", [P, 3, NE], mybir.dt.bfloat16)
        b1_rows = sb("b1_rows", [3, NE * P], mybir.dt.bfloat16)
        ones = sb("ones", [3, P], mybir.dt.bfloat16)
        src = sb("src", [P, 2, P])
        g = sb("gate", [P, 2, NE])
        sq = sb("square", [P, 2, CHUNK])
        var, sd, inv = (sb(n, [P, NE]) for n in ("variance", "deviation", "inverse"))
        u = sb("units", [P, NQ, CHUNK])
        ht = sb("hidden_turned", [P, NQ, CHUNK])
        acc = sb("acc", [P, 4, P])
        s = {n: sem(n) for n in ["fold_done", "folded", "split", "rows_done", "rows_ready", "gates_turned",
                                 "gates_kept", "source_ready", "gate_ready", "h_done", "square_ready", "summed",
                                 "sd_ready", "inv_ready", "unit_ready", "turn_done", "gelu_ready", "y_done", "y_added",
                                 "sum_done", "stored"]}
        block = ctx.enter_context(nc.Block())

        def run(eng, body):
            for k in range(2):
                body(*(Step(0, k - d, 2) if k >= d else None for d in range(3)))
            with eng.Fori(0, NB // 2 - 1) as i:
                for k in range(2, 4):
                    body(*(Step(i, k - d, 2) for d in range(3)))
            for k in range(NB, NB + 2):
                body(*(Step(0, k - d, 2) if k - d < NB else None for d in range(3)))

        @block.gpsimd
        def _(pool):
            def body(a, b, c):
                if a is None:
                    return
                past(pool, s["h_done"], a.n * 4 - 4)
                pool.tensor_copy(src[:, a.m, :], core.a[:, tok(a.n * P, P)]).then_inc(s["source_ready"], 1)
                past(pool, s["y_added"], a.n * 4 - 4)
                pool.tensor_copy(g[:, a.m, :].unsqueeze(1), gates[:, bass.ds(a.n, 1), :]).then_inc(s["gate_ready"], 1)

            run(pool, body)

        @block.tensor
        def _(pe):
            wait_pack(pe, core, 3)
            for e in range(NE):
                last = pe.matmul(ps[:, e // 4, (e % 4) * P:(e % 4 + 1) * P], w("W1T", e * P, P), const("center"),
                                 start=True, stop=True)
                if e % 4 == 3:
                    last.then_inc(s["fold_done"], 1)
            pe.matmul(ps[:, TURN, 0:NE], const("center"), w("b1"), start=True, stop=True).then_inc(s["fold_done"], 1)
            for q in range(NB // 4):
                past(pe, s["gates_kept"], q - 1)
                for t in range(4):
                    last = pe.transpose(ps[0:NE, OUT + q % 2, t * P:(t + 1) * P], gates[:, q * 4 + t, :],
                                        const("ident"))
                last.then_inc(s["gates_turned"], 1)
            pe.wait_ge(s["split"], 6)
            pe.wait_ge(s["folded"], NQ + 1)
            for e in range(NE):
                last = pe.matmul(ps[0:3, e // 4, (e % 4) * P:(e % 4 + 1) * P], b1_parts[:, :, e], const("ident"),
                                 start=True, stop=True)
            last.then_inc(s["rows_done"], 1)
            pe.wait_ge(s["rows_ready"], 2)
            pe.wait_ge(s["gates_kept"], NB // 4)

            def hidden(a, q):
                if q == 0:
                    pe.wait_ge(s["source_ready"], a.n + 1)
                past(pe, s["unit_ready"], a.n * 4 + (q - 3))
                pe.matmul(ps[:, q, :], ones[:, :], b1_rows[:, q * CHUNK:(q + 1) * CHUNK], start=True, stop=False,
                          skip_group_check=True)
                pe.matmul(ps[:, q, :], src[:, a.m, :], w1[:, q * CHUNK:(q + 1) * CHUNK], start=False, stop=True,
                          skip_group_check=True).then_inc(s["h_done"], 1)

            def turn(b, q):
                pe.wait_ge(s["unit_ready"], b.n * 4 + (q + 1))
                past(pe, s["gelu_ready"], b.n * 4 + (q - 1))
                for j in range(4):
                    last = pe.transpose(ps[:, TURN + q % 2, j * P:(j + 1) * P], u[:, q, j * P:(j + 1) * P],
                                        const("ident"))
                last.then_inc(s["turn_done"], 1)

            def output(b, q):
                pe.wait_ge(s["gelu_ready"], b.n * 4 + (q + 1))
                if q == 0:
                    past(pe, s["stored"], b.n)
                past(pe, s["y_added"], b.n * 4 + (q - 1))
                for j in range(4):
                    last = pe.matmul(ps[:, OUT + q % 2, j * P:(j + 1) * P], ht[:, q, j * P:(j + 1) * P],
                                     w("W2", (4 * q + j) * P, P), start=True, stop=True)
                last.then_inc(s["y_done"], 1)

            def total(c):
                pe.wait_ge(s["y_added"], c.n * 4 + 4)
                out = ps[:, OUT, 0:P]
                pe.matmul(out, w("b2", rows=NE), core.b[0:NE, tok(c.n * P, P)], start=True, stop=False)
                for j in range(4):
                    last = pe.matmul(out, acc[:, j, :], const("ident"), start=False, stop=(j == 3))
                last.then_inc(s["sum_done"], 1)

            def body(a, b, c):
                for q in range(4):
                    if b is not None:
                        turn(b, q)
                    if a is not None:
                        hidden(a, q)
                    if c is not None and q == 0:
                        output(c, 3)
                    if c is not None and q == 1:
                        total(c)
                if b is not None:
                    for q in range(3):
                        output(b, q)

            run(pe, body)

        @block.scalar
        def _(act):
            wait_pack(act, core, 3)
            for q in range(NB // 4):
                act.wait_ge(s["gates_turned"], q + 1)
                act.activation(core.b[0:NE, q * CHUNK:(q + 1) * CHUNK], ps[0:NE, OUT + q % 2, :], ACT.Copy).then_inc(
                    s["gates_kept"], 1)

            def gelus(b, q):
                act.wait_ge(s["turn_done"], b.n * 4 + (q + 1))
                past(act, s["y_done"], b.n * 4 + (q - 3))
                for j in range(4):
                    e = 4 * q + j
                    last = act.activation(ht[:, q, j * P:(j + 1) * P], ps[:, TURN + q % 2, j * P:(j + 1) * P],
                                          ACT.Gelu, bias=w("be1", e, 1), scale=w("g1", e, 1))
                last.then_inc(s["gelu_ready"], 1)

            def square(a, q):
                act.wait_ge(s["h_done"], a.n * 4 + (q + 1))
                past(act, s["summed"], a.n * 4 + (q - 1))
                act.activation(sq[:, q % 2, :], ps[:, q, :], ACT.Square).then_inc(s["square_ready"], 1)

            def deviation(a):
                act.wait_ge(s["summed"], a.n * 4 + 4)
                act.activation(sd[:, :], var[:, :], ACT.Sqrt, bias=const("eps5"), scale=1.0 / P).then_inc(
                    s["sd_ready"], 1)

            def body(a, b, c):
                for q in range(4):
                    if b is not None and q < 3:
                        gelus(b, q)
                    if a is not None:
                        square(a, q)
                if a is not None:
                    deviation(a)
                if b is not None:
                    gelus(b, 3)

            run(act, body)

        @block.vector
        def _(dve):
            wait_pack(dve, core, 3)
            dve.memset(ones[:, :], 1.0).then_inc(s["rows_ready"], 1)
            dve.wait_ge(s["fold_done"], NQ + 1)
            dve.tensor_copy(b1_left[:, 0, :], ps[:, TURN, 0:NE]).then_inc(s["folded"], 1)
            for q in range(NQ):
                dve.tensor_copy(w1[:, q * CHUNK:(q + 1) * CHUNK], ps[:, q, :]).then_inc(s["folded"], 1)
            link = Chain(dve, s["split"])
            dve.wait_ge(s["folded"], 1)
            left = [b1_left[:, 0, :], b1_left[:, 1, :], b1_left[:, 0, :]]
            for part in range(3):
                link(dve.tensor_copy(b1_half[:, part, :], left[part]))
                if part < 2:
                    link(dve.tensor_tensor(left[part + 1], left[part], b1_half[:, part, :], ALU.subtract))
            link(dve.tensor_copy(b1_parts[:, :, :], b1_half[:, :, :]))
            dve.wait_ge(s["rows_done"], 1)
            for q in range(NQ):
                last = dve.tensor_copy(b1_rows[:, q * CHUNK:(q + 1) * CHUNK], ps[0:3, q, :])
            last.then_inc(s["rows_ready"], 1)

            def sums(a, q):
                dve.wait_ge(s["square_ready"], a.n * 4 + (q + 1))
                dve.tensor_reduce(var[:, q * 4:(q + 1) * 4], sq[:, q % 2, :].rearrange("p (e j) -> p e j", e=4), AX_X,
                                  ALU.add).then_inc(s["summed"], 1)

            def inverse(a):
                dve.wait_ge(s["sd_ready"], a.n + 1)
                dve.reciprocal(inv[:, :], sd[:, :]).then_inc(s["inv_ready"], 1)
                dve.wait_ge(s["inv_ready"], a.n + 1)

            def units(a, q):
                dve.tensor_tensor(u[:, q, :].rearrange("p (e j) -> p e j", e=4),
                                  ps[:, q, :].rearrange("p (e j) -> p e j", e=4),
                                  inv[:, q * 4:(q + 1) * 4].unsqueeze(2).broadcast_to([P, 4, P]), ALU.mult).then_inc(
                    s["unit_ready"], 1)

            def add(b, q):
                dve.wait_ge(s["y_done"], b.n * 4 + (q + 1))
                if q == 0:
                    dve.wait_ge(s["gate_ready"], b.n + 1)
                    past(dve, s["sum_done"], b.n)
                past(dve, s["y_added"], b.n * 4 + q)
                for j in range(4):
                    y, gate = ps[:, OUT + q % 2, j * P:(j + 1) * P], g[:, b.m, 4 * q + j:4 * q + j + 1]
                    if q == 0:
                        last = dve.tensor_scalar(acc[:, j, :], y, gate, None, ALU.mult)
                    else:
                        last = dve.scalar_tensor_tensor(out=acc[:, j, :], in0=y, scalar=gate, in1=acc[:, j, :],
                                                        op0=ALU.mult, op1=ALU.add)
                last.then_inc(s["y_added"], 1)

            def store(c):
                dve.wait_ge(s["sum_done"], c.n + 1)
                xs = core.x[:, tok(c.n * P, P)]
                dve.tensor_tensor(xs, ps[:, OUT, 0:P], xs, ALU.add).then_inc(s["stored"], 1)

            def body(a, b, c):
                if c is not None:
                    add(c, 3)
                if a is not None:
                    sums(a, 0)
                if c is not None:
                    store(c)
                if a is not None:
                    for q in range(1, 4):
                        sums(a, q)
                if b is not None:
                    add(b, 0)
                    add(b, 1)
                if a is not None:
                    inverse(a)
                    units(a, 0)
                    units(a, 1)
                if b is not None:
                    add(b, 2)
                if a is not None:
                    units(a, 2)
                    units(a, 3)

            run(dve, body)


def layer3_gates(core):
    w = core.pack(7)

    def extra(sb, sem):
        b = dict(lg=sb("scores", [P, NB, 8]), best=sb("best", [P, NB]), work=sb("work", [P, NB, 8]),
                 hot=sb("hot", [P, NB, 8]), hot2=sb("hot2", [P, NB, 8]), low=sb("low", [P, NB]),
                 cond_ready=sem("cond_ready"), second=w("rT"))

        def pool(pool):
            pool.tensor_copy(core.b[:, :].rearrange("p (b t) -> p b t", t=P),
                             core.const("cond").unsqueeze(2).broadcast_to([P, NB, P])).then_inc(b["cond_ready"], 1)

        b["pool"] = pool
        return b

    def pe_first(pe, b):
        pe.wait_ge(b["cond_ready"], 1)

    def act_fn(act, ps, logits_done, act_done, dve_ready, b):
        act.wait_ge(logits_done, 1)
        act.activation(b["lg"][:, :, :], ps[:, 0, 0:NB * 8].rearrange("p (t e) -> p t e", e=8),
                       ACT.Sigmoid).then_inc(act_done, 1)

    def gate_fn(dve, link, logits, gates, logits_done, act_done, dve_ready, b, sb):
        lg, best, work, hot, hot2, low = (b[n] for n in ("lg", "best", "work", "hot", "hot2", "low"))
        bc = lambda t: t[:, :].unsqueeze(2).broadcast_to([P, NB, 8])
        dve.wait_ge(act_done, 1)
        link(dve.tensor_tensor(work[:, :, :], lg[:, :, :], w("rbias").unsqueeze(1).broadcast_to([P, NB, 8]), ALU.add))
        two_best(dve, link, core, work[:, :, :], work[:, :, :], core.const("tie8"), 8, best[:, :], hot[:, :, :],
                 hot2[:, :, :])
        link(dve.tensor_tensor(gates, lg[:, :, :], hot[:, :, :], ALU.mult))
        link(dve.tensor_reduce(best[:, :], gates, AX_X, ALU.add))
        link(dve.tensor_scalar(low[:, :], best[:, :], 1.0e-9, 0.5, ALU.is_le, ALU.mult))
        link(dve.tensor_tensor(hot[:, :, :], hot[:, :, :], bc(low), ALU.mult))
        link(dve.tensor_scalar(low[:, :], best[:, :], 1.0e-9, None, ALU.is_gt))
        link(dve.tensor_scalar(best[:, :], best[:, :], 1.0e-9, None, ALU.add))
        link(dve.reciprocal(best[:, :], best[:, :]))
        link(dve.tensor_tensor(best[:, :], best[:, :], low[:, :], ALU.mult))
        link(dve.tensor_tensor(gates, gates, bc(best), ALU.mult))
        link(dve.tensor_tensor(gates, gates, hot[:, :, :], ALU.add))

    return extra, gate_fn, act_fn, pe_first


def layer3_experts(core):
    w, ps = core.pack(7), core.ps

    def setup(sb, sem, s):
        b = dict(gate=sb("shared_gate", [P, 2, CHUNK]), up=sb("shared", [P, 2, CHUNK]))
        for n in ["gate_done", "up_done", "gate_ready", "up_ready"]:
            b[n] = sem(n)
        b["s"] = s
        return b

    def chunk(c):
        return core.x[:, tok(c * CHUNK, CHUNK)]

    def pe_first(pe, c, b):
        for f in range(2):
            past(pe, b["gate_ready"], c * 2 + f)
            pe.matmul(ps[:, 6, :], w("w1", f * P, P), chunk(c), start=True, stop=True).then_inc(b["gate_done"], 1)
            past(pe, b["up_ready"], c * 2 + f)
            pe.matmul(ps[:, 7, :], w("w3", f * P, P), chunk(c), start=True, stop=True).then_inc(b["up_done"], 1)

    def act_first(act, c, b):
        for f in range(2):
            act.wait_ge(b["gate_done"], c * 2 + (f + 1))
            past(act, b["up_ready"], c * 2 + (f - 1))
            act.activation(b["gate"][:, f, :], ps[:, 6, :], ACT.Silu).then_inc(b["gate_ready"], 1)

    def dve_first(dve, c, b):
        for f in range(2):
            dve.wait_ge(b["up_done"], c * 2 + (f + 1))
            dve.wait_ge(b["gate_ready"], c * 2 + (f + 1))
            past(dve, b["s"]["init_done"], c)
            dve.tensor_tensor(b["up"][:, f, :], ps[:, 7, :], b["gate"][:, f, :], ALU.mult).then_inc(b["up_ready"], 1)

    def shared_pe(pe, c, b):
        pe.wait_ge(b["up_ready"], c * 2 + 2)
        for t in range(4):
            for f in range(2):
                last = pe.matmul(ps[:, 5, t * P:(t + 1) * P], b["up"][:, f, t * P:(t + 1) * P], w("w2", f * P, P),
                                 start=(f == 0), stop=(f == 1))
        return last

    def pe(pe, c, j, bank, b):
        return pe.matmul(ps[:, bank, :], w("W1e", j * P, P), chunk(c), start=True, stop=True)

    def act(act, c, j, bank, out, b):
        return act.activation(out, ps[:, bank, :], ACT.Gelu)

    def finish(dve, c, bank):
        return dve.tensor_scalar(core.a[:, tok(c * CHUNK, CHUNK)], bank, 1.0 / 3.0, None, ALU.mult)

    hidden = dict(pe=pe, act=act, pe_first=pe_first, act_first=act_first, dve_first=dve_first)
    return setup, hidden, dict(pe=shared_pe), finish


def cosine_gates(core):
    w, ps, const = core.pack(7), core.ps, core.const

    def extra(sb, sem):
        b = dict(lg=sb("scores", [P, NB, 8]), best=sb("best", [P, NB]), work=sb("work", [P, NB, 8]),
                 hot=sb("hot", [P, NB, 8]), hot2=sb("hot2", [P, NB, 8]), norm=sb("norm", [P, NB]),
                 sq=sb("square", [P, 2, CHUNK]), sn=sb("sim_unit", [8, P]), snt=sb("sim_turned", [P, 8]),
                 ss=sb("sim_sum", [8, 1]), ssq=sb("sim_square", [8, P]), comp=sb("composite", [P, 8]),
                 itemp=sb("inverse_temp", [P, 1]))
        for n in ["sim_sq", "sim_scaled", "sim_turned", "comp_done", "snt_ready", "comp_ready", "proj_done",
                  "proj_read", "sq_summed", "norm_ready"]:
            b[n] = sem(n)
        return b

    def pe_first(pe, b):
        pe.wait_ge(b["sim_scaled"], 1)
        pe.transpose(ps[:, 6, 0:8], b["sn"][:, :], const("ident", 0, 8, rows=8)).then_inc(b["sim_turned"], 1)
        pe.wait_ge(b["snt_ready"], 1)
        pe.matmul(ps[:, 7, 0:8], w("Wp"), b["snt"][:, :], start=True, stop=True).then_inc(b["comp_done"], 1)
        pe.wait_ge(b["comp_ready"], 1)
        for q in range(NB // 4):
            past(pe, b["proj_read"], q - 1)
            for t in range(4):
                tile = core.a[:, (q * 4 + t) * P:(q * 4 + t + 1) * P]
                last = pe.matmul(ps[:, 1 + q % 2, t * P:(t + 1) * P], tile, w("WpT"), start=True, stop=True)
            last.then_inc(b["proj_done"], 1)

    def act_fn(act, ps_, logits_done, act_done, dve_ready, b):
        act.wait_ge(core.loaded["p7"], 32)
        act.activation(b["ssq"][:, :], w("sim", rows=8), ACT.Square).then_inc(b["sim_sq"], 1)
        act.wait_ge(dve_ready, 1)
        act.activation(b["ss"][:, :], b["ss"][:, :], ACT.Sqrt).then_inc(act_done, 1)
        for q in range(NB // 4):
            act.wait_ge(b["proj_done"], q + 1)
            past(act, b["sq_summed"], q - 1)
            act.activation(b["sq"][:, q % 2, :], ps[:, 1 + q % 2, :], ACT.Square).then_inc(b["proj_read"], 1)
        act.wait_ge(b["sq_summed"], NB // 4)
        act.activation(b["norm"][:, :], b["norm"][:, :], ACT.Sqrt).then_inc(b["norm_ready"], 1)
        act.wait_ge(dve_ready, 2)
        act.activation(b["work"][:, :, :], b["work"][:, :, :], ACT.Exp).then_inc(act_done, 1)

    def gate_fn(dve, link, logits, gates, logits_done, act_done, dve_ready, b, sb):
        lg, best, work, hot, hot2 = (b[n] for n in ("lg", "best", "work", "hot", "hot2"))
        bc = lambda t: t[:, :].unsqueeze(2).broadcast_to([P, NB, 8])
        dve.wait_ge(b["sim_sq"], 1)
        dve.tensor_reduce(b["ss"][:, :], b["ssq"][:, :], AX_X, ALU.add).then_inc(dve_ready, 1)
        link(dve.reciprocal(b["itemp"][:, :], w("temp")))
        dve.wait_ge(act_done, 1)
        link(dve.tensor_scalar(b["ss"][:, :], b["ss"][:, :], 1.0e-12, None, ALU.max))
        link(dve.reciprocal(b["ss"][:, :], b["ss"][:, :]))
        dve.tensor_scalar(b["sn"][:, :], w("sim", rows=8), b["ss"][:, :], None, ALU.mult).then_inc(b["sim_scaled"], 1)
        dve.wait_ge(b["sim_turned"], 1)
        dve.tensor_copy(b["snt"][:, :], ps[:, 6, 0:8]).then_inc(b["snt_ready"], 1)
        dve.wait_ge(b["comp_done"], 1)
        dve.tensor_copy(b["comp"][:, :], ps[:, 7, 0:8]).then_inc(b["comp_ready"], 1)
        for q in range(NB // 4):
            dve.wait_ge(b["proj_read"], q + 1)
            dve.tensor_reduce(b["norm"][:, q * 4:(q + 1) * 4], b["sq"][:, q % 2, :].rearrange("p (t j) -> p t j", t=4),
                              AX_X, ALU.add).then_inc(b["sq_summed"], 1)
        dve.wait_ge(b["norm_ready"], 1)
        link(dve.tensor_scalar(b["norm"][:, :], b["norm"][:, :], 1.0e-12, None, ALU.max))
        link(dve.reciprocal(b["norm"][:, :], b["norm"][:, :]))
        dve.wait_ge(logits_done, 1)
        link(dve.tensor_tensor(lg[:, :, :], logits, bc(b["norm"]), ALU.mult))
        link(dve.tensor_scalar(lg[:, :, :], lg[:, :, :], b["itemp"][:, :], None, ALU.mult))
        two_best(dve, link, core, lg[:, :, :], work[:, :, :], core.const("tie8"), 8, best[:, :], hot[:, :, :],
                 hot2[:, :, :])
        link(dve.tensor_reduce(best[:, :], lg[:, :, :], AX_X, ALU.max))
        dve.tensor_tensor(work[:, :, :], lg[:, :, :], bc(best), ALU.subtract).then_inc(dve_ready, 1)
        dve.wait_ge(act_done, 2)
        link(dve.tensor_tensor(gates, work[:, :, :], hot[:, :, :], ALU.mult))
        link(dve.tensor_reduce(best[:, :], gates, AX_X, ALU.add))
        link(dve.reciprocal(best[:, :], best[:, :]))
        link(dve.tensor_tensor(gates, gates, bc(best), ALU.mult))

    return extra, gate_fn, act_fn, pe_first


def wide_experts(core):
    w, ps = core.pack(7), core.ps

    def pe(pe, c, j, bank, b):
        return pe.matmul(ps[:, bank, :], w("W1", j * P, P), core.a[:, tok(c * CHUNK, CHUNK)], start=True, stop=True)

    def act(act, c, j, bank, out, b):
        return act.activation(out, ps[:, bank, :], ACT.Gelu, bias=w("b1", j, 1))

    return dict(pe=pe, act=act)


def linear_attention_stage(core, next_load=None):
    nc, w, ps, const = core.nc, core.pack(2), core.ps, core.const
    NJ, DH = 8, 64
    PHI, VAL, SCORE, SUMS, OUT = 2, 3, 4, 6, 7
    DEPTH = 6
    SPAN = 2 * (DH + 1)
    steps = NB * NJ
    with stage_scope(nc) as ctx:
        sb = lambda n, shape: ctx.enter_context(nc.sbuf_tensor(f"lin_{n}", shape, F32))
        sem = lambda n: nc.alloc_semaphore(f"lin_{n}")
        src = sb("src", [P, 2, P])
        qk = sb("qk", [P, 2, 2 * P])
        sq = sb("square", [P, 2, 2 * P])
        phi = sb("features", [P, 2, 2, P])
        vt = sb("value", [P, 4, 2, SPAN])
        sm = sb("masked", [P, 2, 2, P])
        den = sb("denominator", [P, 2])
        inv = sb("inverse", [P, 2])
        o = sb("context", [P, 2, P])
        ot = sb("context_turned", [P, NJ, P])
        s = {n: sem(n) for n in ["source_ready", "ones_ready", "qk_done", "qk_ready", "sq_ready", "phi_done", "phi_ready",
                                 "v_done", "v_ready", "s_done", "s_masked", "sum_done", "den_ready", "inv_ready",
                                 "context_ready", "ct_done", "ct_ready", "out_done", "out_read"]}
        block = ctx.enter_context(nc.Block())

        def run(eng, body):
            unroll = 2 * NJ
            for k in range(unroll):
                body([Step(0, k - d, NJ) if k >= d else None for d in range(DEPTH)])
            with eng.Fori(0, NB // 2 - 1) as i:
                for k in range(unroll, 2 * unroll):
                    body([Step(i * 2, k - d, NJ) for d in range(DEPTH)])
            for k in range(steps, steps + DEPTH - 1):
                body([Step(0, k - d, NJ) if k - d < steps else None for d in range(DEPTH)])

        def slot(st):
            return st.k // NJ % 2

        @block.sync
        def _(sp):
            if next_load is not None:
                next_load(sp)

        @block.gpsimd
        def _(pool):
            def body(p):
                st = p[0]
                if st is not None and st.m == 0:
                    past(pool, s["v_done"], st.n - NJ)
                    pool.tensor_copy(src[:, slot(st), :], core.a[:, tok(st.u * P, P)]).then_inc(s["source_ready"], 1)

            run(pool, body)

        @block.tensor
        def _(pe):
            wait_pack(pe, core, 2)

            def project(st):
                if st.m == 0:
                    pe.wait_ge(s["source_ready"], st.u + 1)
                x, bank = src[:, slot(st), :], st.m % 2
                past(pe, s["sq_ready"], st.n - 1)
                pe.matmul(ps[:, bank, 0:P], w("wqT", st.m * P, P), x, start=True, stop=True)
                pe.matmul(ps[:, bank, P:2 * P], w("wkT", st.m * P, P), x, start=True, stop=True).then_inc(
                    s["qk_done"], 1)

            def value(st):
                past(pe, s["v_ready"], st.n)
                pe.matmul(ps[:, VAL, 0:P], src[:, slot(st), :], w("wvT", st.m * P, P), start=True, stop=True).then_inc(
                    s["v_done"], 1)

            def features(st):
                p = st.m % 2
                pe.wait_ge(s["qk_ready"], st.n + 1)
                past(pe, s["phi_ready"], st.n)
                pe.matmul(ps[:, PHI, 0:2 * P], w("omegaT"), qk[:, p, :], start=True, stop=False)
                pe.wait_ge(s["sq_ready"], st.n + 1)
                pe.matmul(ps[:, PHI, 0:2 * P], const("half_block"), sq[:, p, :], start=False, stop=True).then_inc(
                    s["phi_done"], 1)

            def scores(st):
                p = st.m % 2
                pe.wait_ge(s["phi_ready"], st.n + 1)
                past(pe, s["s_masked"], st.n)
                for hh in range(2):
                    last = pe.matmul(ps[:, SCORE + hh, 0:P], phi[DH * hh:DH * (hh + 1), p, 1, :],
                                     phi[DH * hh:DH * (hh + 1), p, 0, :], start=True, stop=True)
                last.then_inc(s["s_done"], 1)

            def sums(st):
                pe.wait_ge(s["s_masked"], st.n + 1)
                pe.wait_ge(s["v_ready"], st.n + 1)
                past(pe, s["context_ready"], st.n)
                for hh in range(2):
                    last = pe.matmul(ps[:, SUMS, 0:SPAN], sm[:, st.m % 2, hh, :], vt[:, st.m % 4, hh, :],
                                     start=(hh == 0), stop=(hh == 1))
                last.then_inc(s["sum_done"], 1)

            def turn(st):
                pe.wait_ge(s["context_ready"], st.n + 1)
                past(pe, s["ct_ready"], st.n)
                if st.m == 0:
                    past(pe, s["out_read"], st.u)
                pe.transpose(ps[:, OUT, 0:P], o[:, st.m % 2, :], const("ident")).then_inc(s["ct_done"], 1)

            def output(st):
                pe.wait_ge(s["ct_ready"], st.n + 1)
                for j in range(NJ):
                    last = pe.matmul(ps[:, OUT, P:2 * P], w("woT", j * P, P), ot[:, j, :], start=(j == 0),
                                     stop=(j == NJ - 1))
                last.then_inc(s["out_done"], 1)

            def body(p):
                for st, part in ((p[0], project), (p[1], features), (p[0], value), (p[2], scores)):
                    if st is not None:
                        part(st)
                if p[5] is not None and p[5].m == NJ - 1:
                    output(p[5])
                for st, part in ((p[3], sums), (p[4], turn)):
                    if st is not None:
                        part(st)

            run(pe, body)

        @block.scalar
        def _(act):
            def square(st):
                act.wait_ge(s["qk_ready"], st.n + 1)
                past(act, s["phi_done"], st.n - 1)
                act.activation(sq[:, st.m % 2, :], ps[:, st.m % 2, 0:2 * P], ACT.Square).then_inc(s["sq_ready"], 1)

            def features(st):
                act.wait_ge(s["phi_done"], st.n + 1)
                past(act, s["s_done"], st.n - 1)
                act.activation(phi[:, st.m % 2, :, :], ps[:, PHI, 0:2 * P].rearrange("p (t j) -> p t j", t=2), ACT.Exp,
                               bias=const("ln_m")).then_inc(s["phi_ready"], 1)

            def turned(st):
                act.wait_ge(s["ct_done"], st.n + 1)
                if st.m == 0:
                    past(act, s["out_done"], st.u)
                act.activation(ot[:, st.m, :], ps[:, OUT, 0:P], ACT.Copy).then_inc(s["ct_ready"], 1)

            def body(p):
                for st, part in ((p[0], square), (p[1], features), (p[4], turned)):
                    if st is not None:
                        part(st)

            run(act, body)

        @block.vector
        def _(dve):
            wait_pack(dve, core, 2)
            dve.memset(vt[:, :, :, :], 0.0).then_inc(s["ones_ready"], 1)
            dve.wait_ge(s["ones_ready"], 1)
            for hh in range(2):
                last = dve.memset(vt[:, :, hh, hh * (DH + 1) + DH:hh * (DH + 1) + DH + 1], 1.0)
            last.then_inc(s["ones_ready"], 1)
            dve.wait_ge(s["ones_ready"], 2)

            def query_key(st):
                dve.wait_ge(s["qk_done"], st.n + 1)
                past(dve, s["phi_done"], st.n - 1)
                dve.tensor_copy(qk[:, st.m % 2, :], ps[:, st.m % 2, 0:2 * P]).then_inc(s["qk_ready"], 1)

            def value(st):
                dve.wait_ge(s["v_done"], st.n + 1)
                past(dve, s["sum_done"], st.n - 3)
                own = vt[:, st.m % 4, :, :].rearrange("p h (g d) -> p (h g) d", g=2)[:, 0:4:3, 0:DH]
                dve.tensor_copy(own, ps[:, VAL, 0:P].rearrange("p (h d) -> p h d", h=2)).then_inc(s["v_ready"], 1)

            def mask(st):
                dve.wait_ge(s["s_done"], st.n + 1)
                past(dve, s["sum_done"], st.n - 1)
                dve.tensor_tensor(sm[:, st.m % 2, :, :], ps[:, SCORE:SCORE + 2, 0:P],
                                  const("causal_mul").unsqueeze(1).broadcast_to([P, 2, P]), ALU.mult).then_inc(
                    s["s_masked"], 1)

            def normalise(st):
                n = st.n
                dve.wait_ge(s["sum_done"], n + 1)
                total = ps[:, SUMS, 0:SPAN].rearrange("p (h d) -> p h d", h=2)
                past(dve, s["inv_ready"], n)
                dve.tensor_scalar(den[:, :], total[:, :, DH], 1.0e-6, None, ALU.add).then_inc(s["den_ready"], 1)
                dve.wait_ge(s["den_ready"], n + 1)
                past(dve, s["context_ready"], n)
                dve.reciprocal(inv[:, :], den[:, :]).then_inc(s["inv_ready"], 1)
                dve.wait_ge(s["inv_ready"], n + 1)
                past(dve, s["ct_done"], n - 1)
                dve.tensor_tensor(o[:, st.m % 2, :].rearrange("p (h d) -> p h d", h=2), total[:, :, 0:DH],
                                  inv[:, :].unsqueeze(2).broadcast_to([P, 2, DH]), ALU.mult).then_inc(
                    s["context_ready"], 1)

            def output(st):
                dve.wait_ge(s["out_done"], st.u + 1)
                xb = core.x[:, tok(st.u * P, P)]
                dve.scalar_tensor_tensor(out=xb, in0=ps[:, OUT, P:2 * P], scalar=w("bo"), in1=xb, op0=ALU.add,
                                         op1=ALU.add).then_inc(s["out_read"], 1)

            def body(p):
                for st, part in ((p[0], query_key), (p[0], value), (p[2], mask)):
                    if st is not None:
                        part(st)
                if p[5] is not None and p[5].m == NJ - 1:
                    output(p[5])
                if p[3] is not None:
                    normalise(p[3])

            run(dve, body)


def latent_stage(core):
    nc, w, ps, const = core.nc, core.pack(4), core.ps, core.const
    with ExitStack() as ctx:
        wd = ctx.enter_context(nc.sbuf_tensor("latent_weight", [P, 32], F32))

        def pe_prepare(pe, s):
            pe.matmul(ps[:, 6, 0:32], w("WdT", rows=32), const("center32", rows=32), start=True, stop=True).then_inc(
                s["prepared"], 1)
            pe.wait_ge(s["prepared"], 2)

        def act_prepare(act, s):
            act.wait_ge(s["prepared"], 1)
            act.activation(wd[:, :], ps[:, 6, 0:32], ACT.Copy).then_inc(s["prepared"], 1)

        norm_stage(core, "latent", 4, core.a, core.b, 32, wd[:, :], const("mean32", rows=32), const("eps5"),
                   gamma=w("gamma", rows=32), beta=w("beta", rows=32), prepare=dict(pe=pe_prepare, act=act_prepare))


def latent_attention(core):
    w, const, ps = core.pack(4), core.const, core.ps

    def cfg(nc, ctx, s, name, qm, kt, ot):
        sb = lambda n, shape: ctx.enter_context(nc.sbuf_tensor(f"{name}_{n}", shape, F32))
        src, lat = sb("src", [P, 2, P]), sb("latent", [32, 2, P])
        even, odd, q = sb("times_cos", [P, 2, P]), sb("times_sin", [P, 2, P]), sb("query", [P, P])
        zero = sb("zero", [P, 1])
        ident16, mask16 = [ctx.enter_context(nc.sbuf_tensor(f"{name}_{n}", [P, P], mybir.dt.bfloat16))
                           for n in ("ident16", "mask16")]
        rotated = nc.alloc_semaphore(f"{name}_rotated")

        def start(eng):
            wait_pack(eng, core, 4)
            if eng is nc.vector:
                eng.memset(zero[:, :], 0.0).then_inc(s["own"], 1)
                eng.tensor_copy(ident16[:, :], const("ident")).then_inc(s["own"], 1)
                eng.tensor_copy(mask16[:, :], const("causal_add")).then_inc(s["own"], 1)
            eng.wait_ge(s["own"], 3)

        def bias(pe, out, g):
            pe.matmul(out, ident16[:, :], mask16[:, :].unsqueeze(1).broadcast_to([P, 4, P]), start=True, stop=False,
                      skip_group_check=True)

        def pool(pool, st):
            n, m = st.n, st.m
            past(pool, s["v_done"], n - 1)
            pool.tensor_copy(src[:, m % 2, :], core.a[:, tok(n * P, P)]).then_inc(s["source_ready"], 1)
            pool.tensor_copy(lat[:, m % 2, :], core.b[0:32, tok(n * P, P)]).then_inc(s["source_ready"], 1)

        def pe_qk(pe, st, bank):
            n, p = st.n, st.m % 2
            pe.wait_ge(s["source_ready"], n * 2 + 2)
            pe.matmul(ps[:, bank, 0:P], w("Wq"), src[:, p, :], start=True, stop=True)
            pe.matmul(ps[:, bank, 2 * P:3 * P], w("Wqs"), src[:, p, :], start=True, stop=True)
            pe.matmul(ps[:, bank, P:2 * P], w("Wuk", rows=32), lat[:, p, :], start=True, stop=True)
            return pe.matmul(ps[:, bank, 3 * P:4 * P], w("Wuks", rows=32), lat[:, p, :], start=True, stop=True)

        def pe_v(pe, st, bank):
            return pe.matmul(ps[:, bank, 0:P], lat[:, st.m % 2, :], w("Wuv", rows=32), start=True, stop=True)

        def pe_out(pe, st, bank):
            return pe.matmul(ps[:, bank, P:2 * P], w("Wo"), ot[:, :], start=True, stop=True)

        def dve_q(dve, st, bank, head_mask):
            n, p = st.n, st.m % 2
            both = lambda lo: ps[:, bank, lo:lo + 2 * P].rearrange("p (t j) -> p t j", t=2)
            over = lambda c: const(c).unsqueeze(1).broadcast_to([P, 2, P])
            dve.wait_ge(s["qk_done"], n + 1)
            past(dve, s["q_ready"], n)
            past(dve, s["k_ready"], n)
            dve.tensor_tensor(even[:, :, :], both(0), over("cos"), ALU.mult).then_inc(rotated, 1)
            dve.tensor_tensor(odd[:, :, :], both(2 * P), over("sin"), ALU.mult).then_inc(rotated, 1)
            dve.wait_ge(rotated, n * 3 + 2)
            dve.tensor_tensor(q[:, :], even[:, 0, :], odd[:, 0, :], ALU.add).then_inc(rotated, 1)
            dve.tensor_tensor(kt[:, p, :], even[:, 1, :], odd[:, 1, :], ALU.add).then_inc(s["k_ready"], 1)
            dve.wait_ge(rotated, n * 3 + 3)
            dve.tensor_tensor(qm[:, p, :, :], q[:, :].unsqueeze(1).broadcast_to([P, 4, P]),
                              head_mask.unsqueeze(2).broadcast_to([P, 4, P]), ALU.mult).then_inc(s["q_ready"], 1)

        def dve_out(dve, st, bank):
            xb = core.x[:, tok(st.n * P, P)]
            return dve.tensor_tensor(xb, ps[:, bank, P:2 * P], xb, ALU.add)

        return dict(start=start, pool=pool, pe_qk=pe_qk, pe_v=pe_v, pe_out=pe_out, dve_q=dve_q, dve_out=dve_out,
                    bv=lambda m: zero[:, :], bias=bias)

    return cfg


CELLS, MAX_PREV, PAIRS = 6, 5, 4


def cell_weights_stage(core, comp, comp_bias, edge, edge_bias, turn):
    nc, w, ps = core.nc, core.pack(5), core.ps
    with stage_scope(nc) as ctx:
        sem = lambda n: nc.alloc_semaphore(f"cellw_{n}")
        product_done, product_read = sem("product_done"), sem("product_read")
        scaled = sem("scaled")
        block = ctx.enter_context(nc.Block())

        @block.tensor
        def _(pe):
            wait_pack(pe, core, 5)
            for c in range(CELLS):
                for i, name in enumerate(("Wq", "Wk", "Wv")):
                    j = 3 * c + i
                    past(pe, product_read, j - 1)
                    pe.matmul(ps[:, j % 2, 0:P], w("WeT", j * P, P), w(name, c * P, P), start=True, stop=True)
                    pe.matmul(ps[:, j % 2, P:P + 1], w(name, c * P, P), w("be", j, 1), start=True,
                              stop=True).then_inc(product_done, 1)

        @block.vector
        def _(dve):
            wait_pack(dve, core, 5)
            for j in range(3 * CELLS):
                dve.wait_ge(product_done, j + 1)
                dve.tensor_scalar(comp[:, j, :], ps[:, j % 2, 0:P], w("ew", j, 1), None, ALU.mult)
                dve.tensor_scalar(comp_bias[:, j:j + 1], ps[:, j % 2, P:P + 1], w("ew", j, 1), None,
                                  ALU.mult).then_inc(product_read, 1)
            for c in range(CELLS):
                dve.tensor_scalar(edge[:, c, :], w("We", c * P, P), w("ew", 3 * c, 1), None, ALU.mult)
                dve.tensor_scalar(turn[:, c, :], w("Wo", c * P, P), w("act", c, 1), None, ALU.mult)
                dve.tensor_scalar(edge_bias[:, c:c + 1], w("be", 3 * c, 1), w("ew", 3 * c, 1), None,
                                  ALU.mult).then_inc(scaled, 1)
            dve.wait_ge(scaled, CELLS)


def cell_attention(core, comp, comp_bias, edge, edge_bias, turn):
    w, const, ps = core.pack(5), core.const, core.ps

    def cfg(nc, ctx, s, name, qm, kt, ot):
        own = ctx.enter_context(nc.sbuf_tensor(f"{name}_nodes", [P, 2, CELLS, 2 * P], F32))

        def node(pair, slot):
            if pair < 2:
                return own[:, pair, slot, :]
            at = ((pair - 2) * CELLS + slot) * (2 * P)
            return core.b[:, at:at + 2 * P]

        def inputs(c):
            nsrc = min(c + 1, MAX_PREV)
            snode = c - nsrc
            return c, snode + 1, snode + nsrc // 2 + 1

        def start(eng):
            pass

        def pool(pool, st):
            if st.m < PAIRS:
                past(pool, s["qk_done"], st.n - (2 * PAIRS - 1))
                pool.tensor_copy(node(st.m, 0), core.a[:, tok(st.u * (2 * P * PAIRS) + st.m * (2 * P), 2 * P)]).then_inc(
                    s["source_ready"], 1)

        def pe_qk(pe, st, bank):
            c, ab = st.m // PAIRS, st.m % PAIRS
            iq, ik, _ = inputs(c)
            if c == 0:
                pe.wait_ge(s["source_ready"], st.u * PAIRS + (ab + 1))
            pe.matmul(ps[:, bank, 0:2 * P], comp[:, 3 * c, :], node(ab, iq), start=True, stop=True)
            return pe.matmul(ps[:, bank, 2 * P:4 * P], comp[:, 3 * c + 1, :], node(ab, ik), start=True,
                             stop=True)

        def pe_v(pe, st, bank):
            c, ab = st.m // PAIRS, st.m % PAIRS
            for bb in range(2):
                last = pe.matmul(ps[:, bank, bb * P:(bb + 1) * P], node(ab, inputs(c)[2])[:, bb * P:(bb + 1) * P],
                                 comp[:, 3 * c + 2, :], start=True, stop=True)
            return last

        def pe_out(pe, st, bank):
            c, ab = st.m // PAIRS, st.m % PAIRS
            pe.matmul(ps[:, bank, 2 * P:4 * P], turn[:, c, :], ot[:, :], start=True, stop=False)
            return pe.matmul(ps[:, bank, 2 * P:4 * P], edge[:, c, :], node(ab, c), start=False, stop=True)

        def act_k(act, st, bank):
            c = st.m // PAIRS
            act.wait_ge(s["q_ready"], st.n + 1)
            act.activation(kt[:, st.m % 2, :], ps[:, bank, 2 * P:4 * P], ACT.Identity,
                           bias=comp_bias[:, 3 * c + 1:3 * c + 2]).then_inc(s["k_ready"], 1)

        def dve_q(dve, st, bank, head_mask):
            c = st.m // PAIRS
            dve.wait_ge(s["qk_done"], st.n + 1)
            for r in range(2):
                last = dve.tensor_scalar(qm[:, st.m % 2, r, :], ps[:, bank, 0:2 * P], comp_bias[:, 3 * c:3 * c + 1],
                                         head_mask[:, r:r + 1], ALU.add, ALU.mult)
            last.then_inc(s["q_ready"], 1)

        def dve_out(dve, st, bank):
            c, ab = st.m // PAIRS, st.m % PAIRS
            out = node(ab, c + 1) if c < CELLS - 1 else core.a[:, tok(st.u * (2 * P * PAIRS) + ab * (2 * P), 2 * P)]
            return dve.tensor_scalar(out, ps[:, bank, 2 * P:4 * P], edge_bias[:, c:c + 1], None, ALU.add)

        return dict(start=start, pool=pool, pe_qk=pe_qk, pe_v=pe_v, pe_out=pe_out, act_k=act_k, dve_q=dve_q,
                    dve_out=dve_out, bv=lambda m: comp_bias[:, 3 * (m // PAIRS) + 2:3 * (m // PAIRS) + 3])

    return cfg


def layer2_cells(core, next_load=None):
    nc = core.nc
    with ExitStack() as ctx:
        sb = lambda n, shape: ctx.enter_context(nc.sbuf_tensor("cellw_" + n, shape, F32))
        tiles = (sb("comp", [P, 3 * CELLS, P]), sb("comp_bias", [P, 3 * CELLS]), sb("edge", [P, CELLS, P]),
                 sb("edge_bias", [P, CELLS]), sb("turn", [P, CELLS, P]))
        cell_weights_stage(core, *tiles)
        attention_stage(core, "cells", NB // 2 * CELLS, PAIRS * CELLS, 8, cell_attention(core, *tiles), next_load=next_load)
    w = core.pack(5)
    norm_stage(core, "norm2", 5, core.a, core.x, P, core.const("center"), core.const("mean"), core.const("eps6"),
               gamma=w("ln_g"), beta=w("ln_b"), add_to=core.x)


def modulated_stage(core):
    nc, w, ps, const = core.nc, core.pack(6), core.ps, core.const
    with stage_scope(nc) as ctx:
        sb = lambda n, shape: ctx.enter_context(nc.sbuf_tensor(f"mod_{n}", shape, F32))
        sem = lambda n: nc.alloc_semaphore(f"mod_{n}")
        ys, ys2, w2 = sb("ys", [P, NB]), sb("ys_square", [P, NB]), sb("weight_square", [P, P])
        dev, d = sb("deviation", [P, NB]), sb("demodulation", [P, NB])
        xs = sb("scaled", [P, 2, 4, P])
        s = {n: sem(n) for n in ["own", "squares", "d_done", "dev_ready", "ys_ready", "xs_ready", "y_done", "y_read"]}
        block = ctx.enter_context(nc.Block())
        nb = CHUNK // P

        def loop(eng, one):
            one(0, 0)
            one(1, 1)
            with eng.Fori(1, NCHUNK // 2) as i:
                one(i * 2, 0)
                one(i * 2 + 1, 1)

        @block.gpsimd
        def _(pool):
            pool.wait_ge(s["ys_ready"], 1)

            def one(c, p):
                past(pool, s["y_done"], c - 1)
                pool.tensor_tensor(xs[:, p, :, :], core.x[:, tok(c * CHUNK, CHUNK)].rearrange("p (b t) -> p b t", b=nb),
                                   ys[:, bass.ds(c * nb, nb)].unsqueeze(2).broadcast_to([P, nb, P]),
                                   ALU.mult).then_inc(s["xs_ready"], 1)

            loop(pool, one)

        @block.tensor
        def _(pe):
            wait_pack(pe, core, 6)
            pe.wait_ge(s["squares"], 2)
            pe.matmul(ps[:, 2, 0:NB], w2[:, :], ys2[:, :], start=True, stop=True).then_inc(s["d_done"], 1)

            def one(c, p):
                pe.wait_ge(s["xs_ready"], c + 1)
                past(pe, s["y_read"], c - 1)
                pe.matmul(ps[:, p, :], w("weight"), xs[:, p, :, :].rearrange("p b t -> p (b t)"), start=True,
                          stop=True).then_inc(s["y_done"], 1)

            loop(pe, one)

        @block.scalar
        def _(act):
            act.wait_ge(s["d_done"], 1)
            act.activation(dev[:, :], ps[:, 2, 0:NB], ACT.Sqrt, bias=const("eps8")).then_inc(s["dev_ready"], 1)

        @block.vector
        def _(dve):
            wait_pack(dve, core, 6)
            dve.tensor_scalar(ys[:, :], const("cond"), float(P) ** -0.5, None, ALU.mult).then_inc(s["ys_ready"], 1)
            dve.tensor_tensor(w2[:, :], w("weight"), w("weight"), ALU.mult).then_inc(s["squares"], 1)
            dve.wait_ge(s["ys_ready"], 1)
            dve.tensor_tensor(ys2[:, :], ys[:, :], ys[:, :], ALU.mult).then_inc(s["squares"], 1)
            dve.wait_ge(s["dev_ready"], 1)
            dve.reciprocal(d[:, :], dev[:, :]).then_inc(s["own"], 1)
            dve.wait_ge(s["own"], 1)

            def one(c, p):
                dve.wait_ge(s["y_done"], c + 1)
                dve.tensor_tensor(core.a[:, tok(c * CHUNK, CHUNK)].rearrange("p (b t) -> p b t", b=nb),
                                  ps[:, p, :].rearrange("p (b t) -> p b t", b=nb),
                                  d[:, bass.ds(c * nb, nb)].unsqueeze(2).broadcast_to([P, nb, P]),
                                  ALU.mult).then_inc(s["y_read"], 1)

            loop(dve, one)


def layer0_ffn(core):
    w = core.pack(1)
    norm_stage(core, "norm0", 1, core.a, core.b, P, core.const("center"), core.const("mean"), core.const("eps5"))
    extra, gate_fn = layer0_gates(core)
    router_stage(core, "route0", 1, core.a, 8, lambda b: w("WgT"), gate_fn, core.gate(8), extra=extra)
    layer0_expert_stage(core)


def layer1_ffn(core):
    w = core.pack(3)
    extra, gate_fn, act_fn = layer1_gates(core)
    router_stage(core, "route1", 3, core.a, 16, lambda b: w("Wr"), gate_fn, core.gate(16), extra=extra, act_fn=act_fn)
    layer1_expert_stage(core)


def layer3_cond2(core):
    w = core.pack(7)
    extra, gate_fn, act_fn, pe_first = layer3_gates(core)
    router_stage(core, "route3", 7, core.x, 8, lambda b: w("rW"), gate_fn, core.gate(8), extra=extra, act_fn=act_fn,
                 pe_first=pe_first)
    setup, hidden, shared, finish = layer3_experts(core)
    expert_stage(core, "experts3", 7, 8, core.gate(8), hidden, lambda e, f, lo, n: w("W2e", e * P, P), 1,
                 lambda e: (e, 0, P), shared=shared, finish=finish, setup=setup, n_hidden=8)


def layer3_ffn(core):
    w = core.pack(7)
    extra, gate_fn, act_fn, pe_first = cosine_gates(core)
    router_stage(core, "route4", 7, core.a, 8, lambda b: b["comp"][:, :], gate_fn, core.gate(8), extra=extra,
                 act_fn=act_fn, pe_first=pe_first)
    expert_stage(core, "experts4", 7, 8, core.gate(8), wide_experts(core),
                 lambda e, f, lo, n: w("W2", (e * 4 + f) * P, P), 4, lambda e: (4 * e, 0, P), b2=w("b2", rows=8),
                 finish=add_to_x(core), n_hidden=32)


def program(nc, dram, out):
    with ExitStack() as ctx:
        core = Core(nc, ctx)
        stages = [
            (0, lambda: low_rank_stage(core, dram)),
            (0, lambda: attention_stage(core, "attn0", NB, 4, 16, plain_attention(core, 0, True))),
            (1, lambda: leaky_stage(core, lambda sp: load_pack(sp, core, dram, 2))),
            (1, lambda: layer0_ffn(core)),
            (2, lambda: lstm_stage(core, "lstm1", 2, lambda sp: load_pack(sp, core, dram, 3))),
            (2, lambda: linear_attention_stage(core)),
            (3, lambda: lstm_stage(core, "lstm2", 3, lambda sp: load_pack(sp, core, dram, 4))),
            (3, lambda: layer1_ffn(core)),
            (4, lambda: lstm_stage(core, "lstm3", 4, lambda sp: load_pack(sp, core, dram, 5))),
            (4, lambda: (latent_stage(core), attention_stage(core, "attn2", NB, 4, 16, latent_attention(core)))),
            (5, lambda: gru_stage(core, lambda sp: load_pack(sp, core, dram, 6))),
            (5, lambda: layer2_cells(core)),
            (6, lambda: modulated_stage(core)),
            (6, lambda: attention_stage(core, "attn3", NB, 4, 16, plain_attention(core, 6, False),
                                        next_load=lambda sp: load_pack(sp, core, dram, 7))),
            (7, lambda: layer3_cond2(core)),
            (7, lambda: layer3_ffn(core)),
        ]
        for _, run in stages:
            run()
        with ExitStack() as end:
            stored = end.enter_context(nc.semaphore("stored"))
            block = end.enter_context(nc.Block())

            @block.sync
            def _(sp):
                sp.dma_start(out, core.x[:, :]).then_inc(stored, 16)
                sp.wait_ge(stored, 16)


def host_layout(i):
    f = np.float32
    part = np.arange(P)
    c = {}
    c["ident"] = np.eye(P, dtype=f)
    c["center"] = np.eye(P, dtype=f) - f(1.0 / P)
    c["mean"] = np.full((P, P), 1.0 / P, f)
    c["head8"] = ((part[:, None] % 32) // 8 == np.arange(4)[None, :]).astype(f) * f(8 ** -0.5)
    c["head16"] = ((part[:, None] % 32) // 16 == np.arange(2)[None, :]).astype(f) * f(16 ** -0.5)
    c["causal_add"] = np.where(part[:, None] >= part[None, :], f(0), f(MASKED))
    c["causal_mul"] = (part[:, None] <= part[None, :]).astype(f)
    c["gate_pick"] = np.repeat(np.eye(4, dtype=f), NB, axis=1)
    inv = (1.0 / 10000.0 ** (np.arange(4, dtype=f) / 4)).astype(f)
    angle = (part[None, :].astype(f) * inv[(part % 8) % 4][:, None]).astype(f)
    c["cos"] = np.cos(angle).astype(f)
    c["sin"] = (np.sin(angle) * np.where(part % 8 < 4, -1.0, 1.0)[:, None]).astype(f)
    c["center32"] = np.eye(32, dtype=f) - f(1.0 / 32)
    c["mean32"] = np.full((32, P), 1.0 / 32, f)
    c["half_block"] = np.where(part[:, None] // 64 == part[None, :] // 64, f(-0.5), f(0))
    c["cond"] = i["cond_1024"].T
    c["spread8"] = (4 * (np.arange(2 * P) // P) + np.arange(2 * P) % P // 32 == np.arange(8)[:, None]).astype(f)
    c["eps5"] = np.full((P, 1), 1e-5, f)
    c["eps6"] = np.full((P, 1), 1e-6, f)
    c["eps8"] = np.full((P, 1), 1e-8, f)
    c["ln_m"] = np.full((P, 1), -math.log(8.0), f)
    c["tie8"] = np.tile(np.arange(8, 0, -1).astype(f), (P, 1))
    c["tie16"] = np.tile(np.arange(16, 0, -1).astype(f), (P, 1))

    def col(a):
        return np.asarray(a).reshape(-1, P).T

    def wide(a):
        return np.asarray(a).transpose(1, 0, 2).reshape(a.shape[1], -1)

    pos = np.clip(part[:, None] + 127 - part[None, :], 0, 126)
    rel = i["L0_attn_rel_table"][pos].transpose(0, 2, 1).reshape(P, 16 * P)
    p0 = dict(W=i["L0_cond_W"].T, fc_bias=col(i["L0_cond_fc_bias"]), Wq=i["L0_attn_Wq"], Wk=i["L0_attn_Wk"],
              Wv=i["L0_attn_Wv"], Wo=i["L0_attn_Wo"], bq=col(i["L0_attn_bq"]), bk=col(i["L0_attn_bk"]),
              bv=col(i["L0_attn_bv"]), bo=col(i["L0_attn_bo"]), rel=rel)
    p1 = dict(WhT=i["L0_cond2_W"][:, :P].T, WzT=i["L0_cond2_W"][:, P:].T, b=col(i["L0_cond2_b"]),
              alpha=col(i["L0_cond2_alpha"]), WgT=i["L0_ffn_Wg"].T, ln_scale=col(i["L0_ffn_ln_scale"]),
              ln_bias=col(i["L0_ffn_ln_bias"]), W1=wide(i["L0_ffn_W1"]), b1=col(i["L0_ffn_b1"]),
              W2=wide(i["L0_ffn_W2"].reshape(2, P, P)), b2=i["L0_ffn_b2"])
    omegaT = i["L1_attn_omega"].T
    pair = np.zeros((P, P), f)
    pair[:64, :64] = omegaT
    pair[64:, 64:] = omegaT
    p2 = dict(Wx=i["L1_cond_Wx"], Wh=i["L1_cond_Wh"], b=i["L1_cond_b"].reshape(4, P), omegaT=pair,
              wqT=i["L1_attn_wq"].T, wkT=i["L1_attn_wk"].T, wvT=i["L1_attn_wv"].T,
              woT=wide(i["L1_attn_wo"].T.reshape(8, P, P)), bo=col(i["L1_attn_bo"]))
    p3 = dict(Wx=i["L1_cond2_Wx"], Wh=i["L1_cond2_Wh"], b=i["L1_cond2_b"].reshape(4, P), Wr=i["L1_ffn_Wr"],
              br=np.tile(i["L1_ffn_br"], (P, 1)), W1T=wide(i["L1_ffn_W1"].transpose(0, 2, 1)),
              b1=col(i["L1_ffn_b1"]), g1=col(i["L1_ffn_g1"]), be1=col(i["L1_ffn_be1"]),
              W2=wide(i["L1_ffn_W2"]), b2=i["L1_ffn_b2"])
    swap = (part // 8) * 8 + (part + 4) % 8
    p4 = dict(Wx=i["L2_cond_Wx"], Wh=i["L2_cond_Wh"], b=i["L2_cond_b"].reshape(4, P), Wq=i["L2_attn_W_q"],
              Wqs=i["L2_attn_W_q"][:, swap], WdT=i["L2_attn_W_dkv"].T, Wuk=i["L2_attn_W_uk"],
              Wuks=i["L2_attn_W_uk"][:, swap], Wuv=i["L2_attn_W_uv"], Wo=i["L2_attn_W_o"],
              gamma=i["L2_attn_ln_gamma"].reshape(32, 1), beta=i["L2_attn_ln_beta"].reshape(32, 1))
    cells, lind = [], 0
    for c_ in range(6):
        n = min(c_ + 1, 5)
        cells += [lind + n - 1, lind, lind + n // 2]
        lind += n
    We, be = i["L2_ffn_We"], i["L2_ffn_be"]
    p5 = dict(Wz=i["L2_cond2_W_z"], Uz=i["L2_cond2_U_z"], Cz=i["L2_cond2_C_z"], bz=col(i["L2_cond2_b_z"]),
              Wr=i["L2_cond2_W_r"], Ur=i["L2_cond2_U_r"], Cr=i["L2_cond2_C_r"], br=col(i["L2_cond2_b_r"]),
              W=i["L2_cond2_W"], U=i["L2_cond2_U"], C=i["L2_cond2_C"], b=col(i["L2_cond2_b"]),
              ew=np.tile(i["L2_ffn_ew"].reshape(1, 18), (P, 1)), act=np.tile(i["L2_ffn_act_w"].reshape(1, 6), (P, 1)),
              We=wide(We[cells[0::3]]), WeT=wide(We[cells].transpose(0, 2, 1)), be=col(be[cells]),
              Wq=wide(i["L2_ffn_Wq"]), Wk=wide(i["L2_ffn_Wk"]), Wv=wide(i["L2_ffn_Wv"]), Wo=wide(i["L2_ffn_Wo"]),
              ln_g=col(i["L2_ffn_ln_g"]), ln_b=col(i["L2_ffn_ln_b"]))
    p6 = dict(weight=i["L3_cond_weight"], Wq=i["L3_attn_Wq"].T, Wk=i["L3_attn_Wk"].T, Wv=i["L3_attn_Wv"].T,
              Wo=i["L3_attn_Wo"].T)
    rW = i["L3_cond2_router_W"]
    p7 = dict(rW=rW[:P], rT=rW[P:], rbias=np.tile(i["L3_cond2_router_bias"], (P, 1)), w1=i["L3_cond2_w1"],
              w3=i["L3_cond2_w3"], w2=wide(i["L3_cond2_w2"].reshape(2, P, P)), W1e=wide(i["L3_cond2_W1e"]),
              W2e=wide(i["L3_cond2_W2e"]), Wp=i["L3_ffn_Wp"], WpT=i["L3_ffn_Wp"].T, sim=i["L3_ffn_sim_matrix"],
              temp=np.tile(i["L3_ffn_temperature"].reshape(1, 1), (P, 1)), W1=wide(i["L3_ffn_W1"]),
              b1=col(i["L3_ffn_b1"]), W2=wide(i["L3_ffn_W2"].reshape(32, P, P)), b2=i["L3_ffn_b2"])
    arrays = {"x": i["x"].reshape(NTOK, P).T, "factors": i["fside_Bx1x1024x16_0"].reshape(NTOK, 16).T}
    for name, parts in dict(const=c, p0=p0, p1=p1, p2=p2, p3=p3, p4=p4, p5=p5, p6=p6, p7=p7).items():
        assert list(parts) == list(PACKS[name]), name
        cols = []
        for key, a in parts.items():
            a = np.asarray(a)
            assert a.shape[1] == PACKS[name][key] and a.shape[0] <= P, (name, key, a.shape)
            cols.append(a if a.shape[0] == P else np.concatenate([a, np.zeros((P - a.shape[0], a.shape[1]), a.dtype)]))
        arrays[name] = np.concatenate(cols, axis=1)
    return {k: np.ascontiguousarray(v) for k, v in arrays.items()}


def kernel(**inputs):
    import concourse.bacc as bacc
    from concourse.bass_utils import run_bass_kernel_spmd

    arrays = host_layout({k: np.asarray(v) for k, v in inputs.items()})
    nc = bacc.Bacc("TRN2", target_bir_lowering=False, num_devices=1)
    dram = {k: nc.dram_tensor(f"in_{k}", v.shape, F32, kind="ExternalInput").ap() for k, v in arrays.items()}
    out = nc.dram_tensor("out_x", (P, NTOK), F32, kind="ExternalOutput").ap()
    program(nc, dram, out)
    got = run_bass_kernel_spmd(nc, [{f"in_{k}": v for k, v in arrays.items()}], core_ids=[0])
    return np.ascontiguousarray(got.results[0]["out_x"].T).reshape(NB, P, P)
```
